# Optimizing a Trainium2 kernel written in Bass

```python
import numpy as np
import jax
import jax.numpy as jnp

def _softmax(x, axis=-1):
    return jax.nn.softmax(x, axis=axis)

def _gelu(x):
    return jax.nn.gelu(x, approximate=True)

def _silu(x):
    return jax.nn.silu(x)

def _sigmoid(x):
    return jax.nn.sigmoid(x)

def _layernorm(x, axis=-1, eps=1e-05):
    m = jnp.mean(x, axis=axis, keepdims=True)
    v = jnp.var(x, axis=axis, keepdims=True)
    return (x - m) / jnp.sqrt(v + eps)

def _scatter_add(tgt, idx, src, axis=0):
    return tgt.at[idx].add(src)

def _segment_sum(src, seg, n):
    return jax.ops.segment_sum(src, seg, n)
kernel_name = 'mk_adaln_d1_jaxref_r4_6dcafe'

def setup_inputs(seed: int=0):
    np.random.seed(seed)
    _w = jnp.asarray

    def _L0_attn_setup():
        import jax, jax.numpy as jnp
        import numpy as np
        B, S, D_MODEL = (2, 512, 256)
        NUM_HEADS, ATTN_DIM = (16, 64)
        key = jax.random.key(seed)
        ks = jax.random.split(key, 9)
        scale = 1.0 / np.sqrt(D_MODEL)
        states = jax.random.normal(ks[0], (B, S, D_MODEL), dtype=jnp.float32)
        Wq = jax.random.normal(ks[1], (D_MODEL, NUM_HEADS * ATTN_DIM), dtype=jnp.float32) * scale
        bq = jnp.zeros((NUM_HEADS * ATTN_DIM,), dtype=jnp.float32)
        Wk = jax.random.normal(ks[2], (D_MODEL, NUM_HEADS * ATTN_DIM), dtype=jnp.float32) * scale
        bk = jnp.zeros((NUM_HEADS * ATTN_DIM,), dtype=jnp.float32)
        Wv = jax.random.normal(ks[3], (D_MODEL, NUM_HEADS * ATTN_DIM), dtype=jnp.float32) * scale
        bv = jnp.zeros((NUM_HEADS * ATTN_DIM,), dtype=jnp.float32)
        Wo = jax.random.normal(ks[4], (NUM_HEADS * ATTN_DIM, D_MODEL), dtype=jnp.float32) * scale
        bo = jnp.zeros((D_MODEL,), dtype=jnp.float32)
        return {'states': states, 'Wq': Wq, 'bq': bq, 'Wk': Wk, 'bk': bk, 'Wv': Wv, 'bv': bv, 'Wo': Wo, 'bo': bo}
    _L0_attn_in = _L0_attn_setup()

    def _L0_ffn_setup():
        import jax, jax.numpy as jnp
        import numpy as np
        DIM = 256
        DEPTH = 2
        HEADS = 8
        DIM_HEAD = 64
        WINDOW = 128
        INNER = HEADS * DIM_HEAD
        HID = int(DIM * 4 * 2 / 3)
        B, N = (2, 2048)
        QK_SCALE = 8.0

        def shift_token(t):
            t1, t2 = jnp.split(t, 2, axis=-1)
            t2 = jnp.pad(t2, ((0, 0), (1, 0), (0, 0)))[:, :-1]
            return jnp.concatenate([t1, t2], axis=-1)

        def l2norm(t):
            return t / jnp.clip(jnp.linalg.norm(t, axis=-1, keepdims=True), 1e-12)

        def rotate_half(x):
            x1, x2 = jnp.split(x, 2, axis=-1)
            return jnp.concatenate([-x2, x1], axis=-1)

        def rotary_xpos(q, k):
            n = q.shape[-2]
            half_idx = jnp.arange(0, DIM_HEAD, 2, dtype=jnp.float32)
            inv_freq = 1.0 / 10000.0 ** (half_idx / DIM_HEAD)
            t = jnp.arange(n, dtype=jnp.float32)
            freqs = t[:, None] * inv_freq[None, :]
            freqs = jnp.concatenate([freqs, freqs], axis=-1)
            base = (half_idx + 0.4 * DIM_HEAD) / (1.4 * DIM_HEAD)
            power = (t - n // 2) / float(WINDOW // 2)
            scale = base[None, :] ** power[:, None]
            scale = jnp.concatenate([scale, scale], axis=-1)
            cos, sin = (jnp.cos(freqs), jnp.sin(freqs))
            q = q * cos * scale + rotate_half(q) * sin * scale
            k = k * cos / scale + rotate_half(k) * sin / scale
            return (q, k)

        def local_attention(q, k, v):
            b, h, n, d = q.shape
            w = n // WINDOW
            bq = q.reshape(b, h, w, WINDOW, d) * QK_SCALE
            bk = k.reshape(b, h, w, WINDOW, d)
            bv = v.reshape(b, h, w, WINDOW, d)

            def look_around(t):
                p = jnp.pad(t, ((0, 0), (0, 0), (1, 0), (0, 0), (0, 0)))
                return jnp.concatenate([p[:, :, :w], p[:, :, 1:]], axis=3)
            bk, bv = (look_around(bk), look_around(bv))
            bt = jnp.arange(n).reshape(w, WINDOW)
            btp = jnp.pad(bt, ((1, 0), (0, 0)), constant_values=-1)
            btk = jnp.concatenate([btp[:w], btp[1:]], axis=1)
            sim = jnp.einsum('bhwid,bhwjd->bhwij', bq, bk)
            i = bt[:, :, None]
            j = btk[:, None, :]
            mask = (i < j) | (i > j + WINDOW) | (j == -1)
            sim = jnp.where(mask, -jnp.finfo(sim.dtype).max, sim)
            attn = jax.nn.softmax(sim, axis=-1)
            out = jnp.einsum('bhwij,bhwjd->bhwid', attn, bv)
            return out.reshape(b, h, n, d)

        def _layer(x, wqkv, qs, ksc, wo, lg, lb, w1, b1, w2, b2):
            b, n, _ = x.shape
            h = shift_token(x)
            qkv = h @ wqkv
            q, k, v = jnp.split(qkv, 3, axis=-1)
            to_heads = lambda t: t.reshape(b, n, HEADS, DIM_HEAD).transpose(0, 2, 1, 3)
            q, k, v = (to_heads(q), to_heads(k), to_heads(v))
            q = l2norm(q) * qs
            k = l2norm(k) * ksc
            q, k = rotary_xpos(q, k)
            o = local_attention(q, k, v)
            o = o.transpose(0, 2, 1, 3).reshape(b, n, INNER)
            x = x + o @ wo
            h = shift_token(x)
            mu = h.mean(-1, keepdims=True)
            var = h.var(-1, keepdims=True)
            h = (h - mu) / jnp.sqrt(var + 1e-05) * lg + lb
            h = h @ w1 + b1
            a, g = jnp.split(h, 2, axis=-1)
            h = a * jax.nn.gelu(g, approximate=False)
            x = x + h @ w2 + b2
            return x
        key = jax.random.key(seed)
        ks = jax.random.split(key, 6)
        return {'x': jax.random.normal(ks[0], (B, N, DIM), jnp.float32), 'wqkv': jax.random.normal(ks[1], (DEPTH, DIM, 3 * INNER), jnp.float32) * 0.02, 'q_scale': jnp.ones((DEPTH, DIM_HEAD), jnp.float32), 'k_scale': jnp.ones((DEPTH, DIM_HEAD), jnp.float32), 'wo': jax.random.normal(ks[2], (DEPTH, INNER, DIM), jnp.float32) * 0.02, 'ln_g': jnp.ones((DEPTH, DIM), jnp.float32), 'ln_b': jnp.zeros((DEPTH, DIM), jnp.float32), 'w1': jax.random.normal(ks[3], (DEPTH, DIM, 2 * HID), jnp.float32) * 0.02, 'b1': jnp.zeros((DEPTH, 2 * HID), jnp.float32), 'w2': jax.random.normal(ks[4], (DEPTH, HID, DIM), jnp.float32) * 0.02, 'b2': jnp.zeros((DEPTH, DIM), jnp.float32)}
    _L0_ffn_in = _L0_ffn_setup()
    _L0_c = _w((lambda *s: np.random.randn(*s).astype(np.float32) * 0.05)(4, 256))
    _L0_wmod = _w((lambda *s: np.random.randn(*s).astype(np.float32) * 0.05)(256, 6 * 256) * 256 ** (-0.5))
    _d = {'L0_attn_states': _L0_attn_in['states'], 'L0_attn_Wq': _L0_attn_in['Wq'], 'L0_attn_bq': _L0_attn_in['bq'], 'L0_attn_Wk': _L0_attn_in['Wk'], 'L0_attn_bk': _L0_attn_in['bk'], 'L0_attn_Wv': _L0_attn_in['Wv'], 'L0_attn_bv': _L0_attn_in['bv'], 'L0_attn_Wo': _L0_attn_in['Wo'], 'L0_attn_bo': _L0_attn_in['bo'], 'L0_ffn_wqkv': _L0_ffn_in['wqkv'], 'L0_ffn_q_scale': _L0_ffn_in['q_scale'], 'L0_ffn_k_scale': _L0_ffn_in['k_scale'], 'L0_ffn_wo': _L0_ffn_in['wo'], 'L0_ffn_ln_g': _L0_ffn_in['ln_g'], 'L0_ffn_ln_b': _L0_ffn_in['ln_b'], 'L0_ffn_w1': _L0_ffn_in['w1'], 'L0_ffn_b1': _L0_ffn_in['b1'], 'L0_ffn_w2': _L0_ffn_in['w2'], 'L0_ffn_b2': _L0_ffn_in['b2'], 'L0_c': _L0_c, 'L0_wmod': _L0_wmod}
    _x0 = _d['L0_attn_states']
    _d['L0_attn_states'] = jax.random.normal(jax.random.fold_in(jax.random.key(seed), 1), (4, 1024, 256), dtype=_x0.dtype)
    del _x0
    return _d

def reference(L0_attn_states, L0_attn_Wq, L0_attn_bq, L0_attn_Wk, L0_attn_bk, L0_attn_Wv, L0_attn_bv, L0_attn_Wo, L0_attn_bo, L0_ffn_wqkv, L0_ffn_q_scale, L0_ffn_k_scale, L0_ffn_wo, L0_ffn_ln_g, L0_ffn_ln_b, L0_ffn_w1, L0_ffn_b1, L0_ffn_w2, L0_ffn_b2, L0_c, L0_wmod):

    def _L0_attn_ref(states, Wq, bq, Wk, bk, Wv, bv, Wo, bo):
        import jax, jax.numpy as jnp
        import numpy as np
        B, S, D_MODEL = (2, 512, 256)
        NUM_HEADS, ATTN_DIM = (16, 64)
        b, s, _ = states.shape
        h, d = (NUM_HEADS, ATTN_DIM)

        def proj(W, bias):
            y = jnp.tanh(states @ W + bias)
            return y.reshape(b, s, h, d).transpose(0, 2, 1, 3)
        q, k, v = (proj(Wq, bq), proj(Wk, bk), proj(Wv, bv))
        alpha = jnp.einsum('bhqd,bhkd->bhqk', q, k) / jnp.sqrt(jnp.float32(d))
        causal = jnp.tril(jnp.ones((s, s), dtype=bool))
        alpha = jnp.where(causal, alpha, jnp.finfo(jnp.float32).min)
        alpha = jax.nn.softmax(alpha, axis=-1)
        ctx = jnp.einsum('bhqk,bhkd->bhqd', alpha, v)
        ctx = ctx.transpose(0, 2, 1, 3).reshape(b, s, h * d)
        return jnp.tanh(ctx @ Wo + bo)

    def _L0_ffn_ref(x, wqkv, q_scale, k_scale, wo, ln_g, ln_b, w1, b1, w2, b2):
        import jax, jax.numpy as jnp
        import numpy as np
        DIM = 256
        DEPTH = 2
        HEADS = 8
        DIM_HEAD = 64
        WINDOW = 128
        INNER = HEADS * DIM_HEAD
        HID = int(DIM * 4 * 2 / 3)
        B, N = (2, 2048)
        QK_SCALE = 8.0

        def shift_token(t):
            t1, t2 = jnp.split(t, 2, axis=-1)
            t2 = jnp.pad(t2, ((0, 0), (1, 0), (0, 0)))[:, :-1]
            return jnp.concatenate([t1, t2], axis=-1)

        def l2norm(t):
            return t / jnp.clip(jnp.linalg.norm(t, axis=-1, keepdims=True), 1e-12)

        def rotate_half(x):
            x1, x2 = jnp.split(x, 2, axis=-1)
            return jnp.concatenate([-x2, x1], axis=-1)

        def rotary_xpos(q, k):
            n = q.shape[-2]
            half_idx = jnp.arange(0, DIM_HEAD, 2, dtype=jnp.float32)
            inv_freq = 1.0 / 10000.0 ** (half_idx / DIM_HEAD)
            t = jnp.arange(n, dtype=jnp.float32)
            freqs = t[:, None] * inv_freq[None, :]
            freqs = jnp.concatenate([freqs, freqs], axis=-1)
            base = (half_idx + 0.4 * DIM_HEAD) / (1.4 * DIM_HEAD)
            power = (t - n // 2) / float(WINDOW // 2)
            scale = base[None, :] ** power[:, None]
            scale = jnp.concatenate([scale, scale], axis=-1)
            cos, sin = (jnp.cos(freqs), jnp.sin(freqs))
            q = q * cos * scale + rotate_half(q) * sin * scale
            k = k * cos / scale + rotate_half(k) * sin / scale
            return (q, k)

        def local_attention(q, k, v):
            b, h, n, d = q.shape
            w = n // WINDOW
            bq = q.reshape(b, h, w, WINDOW, d) * QK_SCALE
            bk = k.reshape(b, h, w, WINDOW, d)
            bv = v.reshape(b, h, w, WINDOW, d)

            def look_around(t):
                p = jnp.pad(t, ((0, 0), (0, 0), (1, 0), (0, 0), (0, 0)))
                return jnp.concatenate([p[:, :, :w], p[:, :, 1:]], axis=3)
            bk, bv = (look_around(bk), look_around(bv))
            bt = jnp.arange(n).reshape(w, WINDOW)
            btp = jnp.pad(bt, ((1, 0), (0, 0)), constant_values=-1)
            btk = jnp.concatenate([btp[:w], btp[1:]], axis=1)
            sim = jnp.einsum('bhwid,bhwjd->bhwij', bq, bk)
            i = bt[:, :, None]
            j = btk[:, None, :]
            mask = (i < j) | (i > j + WINDOW) | (j == -1)
            sim = jnp.where(mask, -jnp.finfo(sim.dtype).max, sim)
            attn = jax.nn.softmax(sim, axis=-1)
            out = jnp.einsum('bhwij,bhwjd->bhwid', attn, bv)
            return out.reshape(b, h, n, d)

        def _layer(x, wqkv, qs, ksc, wo, lg, lb, w1, b1, w2, b2):
            b, n, _ = x.shape
            h = shift_token(x)
            qkv = h @ wqkv
            q, k, v = jnp.split(qkv, 3, axis=-1)
            to_heads = lambda t: t.reshape(b, n, HEADS, DIM_HEAD).transpose(0, 2, 1, 3)
            q, k, v = (to_heads(q), to_heads(k), to_heads(v))
            q = l2norm(q) * qs
            k = l2norm(k) * ksc
            q, k = rotary_xpos(q, k)
            o = local_attention(q, k, v)
            o = o.transpose(0, 2, 1, 3).reshape(b, n, INNER)
            x = x + o @ wo
            h = shift_token(x)
            mu = h.mean(-1, keepdims=True)
            var = h.var(-1, keepdims=True)
            h = (h - mu) / jnp.sqrt(var + 1e-05) * lg + lb
            h = h @ w1 + b1
            a, g = jnp.split(h, 2, axis=-1)
            h = a * jax.nn.gelu(g, approximate=False)
            x = x + h @ w2 + b2
            return x
        for l in range(DEPTH):
            x = _layer(x, wqkv[l], q_scale[l], k_scale[l], wo[l], ln_g[l], ln_b[l], w1[l], b1[l], w2[l], b2[l])
        return x
    x = L0_attn_states
    mod = (_silu(L0_c) @ L0_wmod).reshape(L0_c.shape[0], 6, 1, -1)
    sa, ca, ga, sb, cb, gb = (mod[:, 0], mod[:, 1], mod[:, 2], mod[:, 3], mod[:, 4], mod[:, 5])
    ga = (2 * (ga >= 0) - 1) * jnp.maximum(jnp.abs(ga), 0.25)
    gb = (2 * (gb >= 0) - 1) * jnp.maximum(jnp.abs(gb), 0.25)
    h = _layernorm(x, axis=-1) * (1 + ca) + sa
    x = x + ga * _L0_attn_ref(h, L0_attn_Wq, L0_attn_bq, L0_attn_Wk, L0_attn_bk, L0_attn_Wv, L0_attn_bv, L0_attn_Wo, L0_attn_bo)
    h = _layernorm(x, axis=-1) * (1 + cb) + sb
    x = x + gb * _L0_ffn_ref(h, L0_ffn_wqkv, L0_ffn_q_scale, L0_ffn_k_scale, L0_ffn_wo, L0_ffn_ln_g, L0_ffn_ln_b, L0_ffn_w1, L0_ffn_b1, L0_ffn_w2, L0_ffn_b2)
    return x

_drawn_inputs = setup_inputs


def setup_inputs(seed=0):
    import zlib

    import numpy as np

    out = dict(_drawn_inputs(seed))
    spreads = {'L0_attn_bq': (0.0, 2.0),
     'L0_attn_bk': (0.0, 2.0),
     'L0_attn_bv': (0.0, 0.298),
     'L0_attn_bo': (0.0, 0.342),
     'L0_ffn_q_scale': (1.0, 0.6),
     'L0_ffn_k_scale': (1.0, 0.6),
     'L0_ffn_ln_g': (1.0, 0.6),
     'L0_ffn_ln_b': (0.0, 0.8),
     'L0_ffn_b1': (0.0, 0.8),
     'L0_ffn_b2': (0.0, 0.467)}
    factors = {'L0_attn_Wq': 5.093,
     'L0_attn_Wk': 5.047,
     'L0_ffn_wqkv': 6.713,
     'L0_ffn_wo': 6.561,
     'L0_ffn_w1': 4.707,
     'L0_ffn_w2': 4.692}
    for name, (base, spread) in spreads.items():
        noise = np.random.default_rng([zlib.crc32(name.encode()), seed]).standard_normal(out[name].shape)
        drawn = base * np.exp(spread * noise) if base else spread * noise
        out[name] = jnp.asarray(drawn.astype(out[name].dtype))
    for name, factor in factors.items():
        out[name] = (out[name] * factor).astype(out[name].dtype)
    return out
```

```python
import numpy as np
import concourse.bass as bass
from concourse import mybir
from contextlib import ExitStack

F32 = mybir.dt.float32
F32R = mybir.dt.float32r
F16 = mybir.dt.float16
ALU = mybir.AluOpType
ACT = mybir.ActivationFunctionType
AX = mybir.AxisListType
ds = bass.ds

P = 128
B, S, D = 4, 1024, 256
KT = D // P
NT = B * S // P
TB = S // P
H, DH = 16, 64
HP = H // 2
CH = 512
NC = S // CH
CT = CH // P
EPS = 1e-5
SCORE_SCALE = DH ** -0.5
SCORE_SHIFT = 3.0
VW = 2 * DH + 2
MASKED = -1.0e30
CREDIT = 4


def at(n):
    return n + CREDIT


def hold(eng, tick, *waits):
    for sem, value in waits:
        eng.wait_ge(sem, value)
    eng.sem_inc(tick, 1)


def f32(ap):
    return ap.bitcast(F32)


class Allocator:
    def __init__(self, nc, ctx):
        self.nc, self.ctx = nc, ctx

    def sb(self, name, shape, dt=F32):
        return self.ctx.enter_context(self.nc.sbuf_tensor(name, shape, dt))

    def ps(self, name, shape, dt=F32):
        return self.ctx.enter_context(self.nc.psum_tensor(name, shape, dt))

    def sems(self, prefix, names):
        return [self.ctx.enter_context(self.nc.semaphore(prefix + n)) for n in names.split()]


def three_products(pe, out, w_hi, w_lo, x_hi, x_lo, first, last):
    pe.matmul(out, w_hi, x_hi, start=first, stop=False, skip_group_check=True)
    pe.matmul(out, w_hi, x_lo, start=False, stop=False, skip_group_check=True)
    return pe.matmul(out, w_lo, x_hi, start=False, stop=last, skip_group_check=True)


def variance_steps(dve, chain, n, st, mean2, tmp, var, var_ready):
    dve.tensor_tensor(tmp[:, 0, :], st[:, :, 1], st[:, :, 4], ALU.subtract).then_inc(chain, 1)
    dve.tensor_tensor(tmp[:, 1, :], st[:, :, 2], st[:, :, 5], ALU.add).then_inc(chain, 1)
    dve.tensor_tensor(mean2, st[:, :, 1], st[:, :, 4], ALU.add).then_inc(chain, 1)
    dve.wait_ge(chain, n + 2)
    dve.tensor_tensor(tmp[:, 2, :], tmp[:, 0, :], tmp[:, 0, :], ALU.mult).then_inc(chain, 1)
    dve.tensor_scalar(tmp[:, 3, :], tmp[:, 1, :], 1.0 / D, EPS, ALU.mult, ALU.add).then_inc(chain, 1)
    dve.wait_ge(chain, n + 5)
    dve.scalar_tensor_tensor(var, tmp[:, 2, :], 0.25, tmp[:, 3, :], ALU.mult, ALU.add).then_inc(var_ready, 1)
    return n + 5


def phase_modulation_and_norm1(nc, io, scr, keep):
    with ExitStack() as ctx:
        a = Allocator(nc, ctx)
        x = a.sb("n1_x", [P, NT, D])
        ident, modT, modB = keep["ident"], keep["modT"], keep["modB"]
        cT = a.sb("n1_cT", [P, KT, B])
        silu = a.sb("n1_silu", [P, 4, KT, B])
        silu_rows = a.sb("n1_silu_rows", [P, KT, B, P])
        wmod = a.sb("n1_wmod", [P, KT, 6 * D])
        gate = a.sb("n1_gate", [P, 3, D])
        st = a.sb("n1_stats", [P, NT, 6])
        tmp = a.sb("n1_tmp", [P, 4, NT])
        col = a.sb("n1_columns", [P, 5, NT])
        xn = a.sb("n1_xn", [P, NC, CT, D])
        full = a.sb("n1_full", [P, NC, KT, CH])
        hi = a.sb("n1_hi", [P, NC, KT, CH], F32R)
        lo = a.sb("n1_lo", [P, NC, KT, CH], F32R)
        ps_mod = a.ps("n1_ps_mod", [P, 12, B])
        ps_row = a.ps("n1_ps_row", [P, 2, CH])
        ps_t = [a.ps(f"n1_ps_t{i}", [P, KT, CH]) for i in range(NC)]
        (ld_c, ld_w, ld_i, ld_x, exp_done, silu_done, silu_bc, mod_mm, mod_ev, row_mm, row_ev, bn, chain, var_ready,
         std_ready, norm_ready, xn_ready, t_done, full_done, hi_done, lo_done, tick) = a.sems(
            "n1_", "ld_c ld_w ld_i ld_x exp_done silu_done silu_bc mod_mm mod_ev row_mm row_ev bn chain var_ready "
            "std_ready norm_ready xn_ready t_done full_done hi_done lo_done tick")
        out_hi = a.sems("n1_", "out_hi0 out_hi1")
        out_lo = a.sems("n1_", "out_lo0 out_lo1")
        with nc.Block() as block:

            @block.sync
            def _(sp):
                for s in out_hi + out_lo:
                    sp.sem_inc(s, 16)
                sp.dma_start(cT[:], io["cT"].rearrange("(k p) b -> p k b", p=P)).then_inc(ld_c, 16)
                sp.dma_start(wmod[:], io["wmod"].rearrange("(k p) n -> p k n", p=P)).then_inc(ld_w, 16)
                for b in range(B):
                    sp.dma_start(x[:, b * TB:(b + 1) * TB, :],
                                 io["states"][b].rearrange("(t p) d -> p t d", p=P)).then_inc(ld_x, 16)
                sp.dma_start(ident[:], io["ident"]).then_inc(ld_i, 16)
                with sp.Fori(0, B) as b:
                    for c in range(NC):
                        cols = slice(c * CH, (c + 1) * CH)
                        sp.wait_ge(hi_done, at(b * NC + c + 1))
                        sp.dma_start(scr["hT_hi"][b, :, :, cols], f32(hi[:, c])).then_inc(out_hi[c], 16)
                        sp.wait_ge(lo_done, at(b * NC + c + 1))
                        sp.dma_start(scr["hT_lo"][b, :, :, cols], f32(lo[:, c])).then_inc(out_lo[c], 16)
                for s in out_hi + out_lo:
                    sp.wait_ge(s, 16 * (B + 1))

            @block.scalar
            def _(act):
                act.sem_inc(full_done, CREDIT)
                act.wait_ge(ld_c, 16)
                act.activation(silu[:, 0], cT[:], ACT.Exp, scale=-1.0).then_inc(exp_done, 1)
                act.wait_ge(var_ready, 1)
                act.activation(col[:, 2, :], col[:, 1, :], ACT.Sqrt).then_inc(std_ready, 1)
                act.wait_ge(mod_ev, 2)
                with act.Fori(0, B) as b:
                    for c in range(NC):
                        hold(act, tick, (t_done, b * NC + c + 1), (lo_done, at(b * NC + c - 1)))
                        for k in range(KT):
                            step = act.activation(full[:, c, k, :], ps_t[c][:, k, :], ACT.Identity,
                                                  scale=modT[:, KT + k, ds(b, 1)], bias=modT[:, k, ds(b, 1)])
                        step.then_inc(full_done, 1)

            @block.gpsimd
            def _(pool):
                pool.sem_inc(hi_done, CREDIT)
                with pool.Fori(0, B) as b:
                    for c in range(NC):
                        hold(pool, tick, (full_done, at(b * NC + c + 1)), (out_hi[c], 16 * b + 16))
                        pool.tensor_copy(hi[:, c], full[:, c]).then_inc(hi_done, 1)

            @block.vector
            def _(dve):
                dve.sem_inc(lo_done, CREDIT)
                dve.wait_ge(exp_done, 1)
                dve.tensor_scalar(silu[:, 1], silu[:, 0], 1.0, None, ALU.add).then_inc(silu_done, 1)
                dve.wait_ge(silu_done, 1)
                dve.reciprocal(silu[:, 2], silu[:, 1]).then_inc(silu_done, 1)
                dve.wait_ge(silu_done, 2)
                dve.tensor_tensor(silu[:, 3], silu[:, 2], cT[:], ALU.mult).then_inc(silu_done, 1)
                dve.wait_ge(silu_done, 3)
                for k in range(KT):
                    dve.tensor_copy(silu_rows[:, k], silu[:, 3, k].unsqueeze(2).broadcast_to([P, B, P])).then_inc(silu_bc, 1)
                with dve.Fori(0, B) as b:
                    dve.wait_ge(ld_x, 16 * B)
                    with dve.Fori(0, TB) as t:
                        dve.bn_stats(st[:, b * TB + t, :], x[:, b * TB + t, :]).then_inc(bn, 1)
                dve.wait_ge(bn, NT)
                variance_steps(dve, chain, 0, st, col[:, 0, :], tmp, col[:, 1, :], var_ready)
                dve.wait_ge(mod_mm, 1)
                dve.tensor_copy(modT[:, 0:2, :], ps_mod[:, 0:2, :]).then_inc(mod_ev, 1)
                dve.tensor_scalar(modT[:, 2:4, :], ps_mod[:, 2:4, :], 1.0, None, ALU.add).then_inc(mod_ev, 1)
                dve.tensor_scalar(gate[:, 0, 0:8], ps_mod[:, 4:6, :].rearrange("p a b -> p (a b)"), 0.0, 2.0,
                                  ALU.is_ge, ALU.mult).then_inc(mod_ev, 1)
                dve.tensor_scalar(gate[:, 2, 0:8], ps_mod[:, 4:6, :].rearrange("p a b -> p (a b)"), -1.0, 0.25,
                                  ALU.mult, ALU.max).then_inc(mod_ev, 1)
                dve.wait_ge(mod_ev, 4)
                dve.tensor_tensor(gate[:, 1, 0:8], ps_mod[:, 4:6, :].rearrange("p a b -> p (a b)"), gate[:, 2, 0:8],
                                  ALU.max).then_inc(mod_ev, 1)
                dve.wait_ge(mod_ev, 5)
                dve.scalar_tensor_tensor(modT[:, 4:6, :].rearrange("p a b -> p (a b)"), gate[:, 0, 0:8], -1.0,
                                         gate[:, 1, 0:8], ALU.add, ALU.mult).then_inc(mod_ev, 1)
                dve.wait_ge(std_ready, 1)
                dve.reciprocal(col[:, 3, :], col[:, 2, :]).then_inc(norm_ready, 1)
                dve.wait_ge(norm_ready, 1)
                dve.scalar_tensor_tensor(col[:, 4, :], col[:, 0, :], -0.5, col[:, 3, :], ALU.mult,
                                         ALU.mult).then_inc(norm_ready, 1)
                dve.wait_ge(norm_ready, 2)
                for b in range(B):
                    dve.wait_ge(row_mm, b + 1)
                    dve.tensor_copy(modB[:, b, 0:D], ps_row[:, 0, 0:D]).then_inc(row_ev, 1)
                    dve.tensor_scalar(modB[:, b, D:2 * D], ps_row[:, 0, D:2 * D], 1.0, None, ALU.add).then_inc(row_ev, 1)
                    if b:
                        dve.wait_ge(row_ev, 6 * b)
                    dve.tensor_scalar(gate[:, 0, 0:D], ps_row[:, 1, 0:D], 0.0, 2.0, ALU.is_ge, ALU.mult).then_inc(row_ev, 1)
                    dve.tensor_scalar(gate[:, 2, 0:D], ps_row[:, 1, 0:D], -1.0, 0.25, ALU.mult, ALU.max).then_inc(row_ev, 1)
                    dve.wait_ge(row_ev, 6 * b + 4)
                    dve.tensor_tensor(gate[:, 1, 0:D], ps_row[:, 1, 0:D], gate[:, 2, 0:D], ALU.max).then_inc(row_ev, 1)
                    dve.wait_ge(row_ev, 6 * b + 5)
                    dve.scalar_tensor_tensor(modB[:, b, 2 * D:3 * D], gate[:, 0, 0:D], -1.0, gate[:, 1, 0:D],
                                             ALU.add, ALU.mult).then_inc(row_ev, 1)
                with dve.Fori(0, B) as b:
                    for c in range(NC):
                        dve.wait_ge(full_done, at(b * NC + c - 1))
                        for t in range(CT):
                            n = b * TB + c * CT + t
                            step = dve.tensor_scalar(xn[:, c, t, :], x[:, n, :], col[:, 3, ds(n, 1)], col[:, 4, ds(n, 1)],
                                                     ALU.mult, ALU.add)
                        step.then_inc(xn_ready, 1)
                        dve.wait_ge(hi_done, at(b * NC + c + 1))
                        dve.wait_ge(out_lo[c], 16 * b + 16)
                        dve.tensor_tensor(lo[:, c], full[:, c], f32(hi[:, c]), ALU.subtract).then_inc(lo_done, 1)

            @block.tensor
            def _(pe):
                pe.wait_ge(silu_bc, KT)
                pe.wait_ge(ld_w, 16)
                for m in range(12):
                    for k in range(KT):
                        step = pe.matmul(ps_mod[:, m, :], wmod[:, k, m * P:(m + 1) * P], silu[:, 3, k, :],
                                         start=(k == 0), stop=(k == KT - 1))
                step.then_inc(mod_mm, 1)
                for b in range(B):
                    if b:
                        pe.wait_ge(row_ev, 6 * b)
                    for half in range(2):
                        lo_c = 3 * D + half * CH
                        hi_c = min(lo_c + CH, 6 * D)
                        for k in range(KT):
                            step = pe.matmul(ps_row[:, half, 0:hi_c - lo_c], silu_rows[:, k, b, :], wmod[:, k, lo_c:hi_c],
                                             start=(k == 0), stop=(k == KT - 1))
                    step.then_inc(row_mm, 1)
                pe.wait_ge(ld_i, 16)
                with pe.Fori(0, B) as b:
                    for c in range(NC):
                        pe.wait_ge(xn_ready, b * NC + c + 1)
                        pe.wait_ge(full_done, at(b * NC + c - 1))
                        for t in range(CT):
                            for k in range(KT):
                                step = pe.transpose(ps_t[c][:, k, t * P:(t + 1) * P], xn[:, c, t, k * P:(k + 1) * P], ident[:])
                        step.then_inc(t_done, 1)


UNITS = [(qc, kt) for qc in range(NC) for kt in range((qc + 1) * CT)]
NU = len(UNITS)
LAG = 2
V_, Q_, K_ = range(3)
PROJ = [(w, c) for w in (V_, Q_, K_) for c in range(NC)]
NPJ = len(PROJ)
PROJ_AT = {0: 0, 1: 1, 3: 2, 4: 3, 6: 4, 7: 5}
SPLIT_W_AT = 8
CTX_AT = 9


def phase_attention(nc, io, scr, keep):
    with ExitStack() as ctx:
        a = Allocator(nc, ctx)
        ident, modT = keep["ident"], keep["modT"]
        ident16 = a.sb("at_ident16", [P, P], F16)
        causal = a.sb("at_causal", [P, P], F16)
        bias = a.sb("at_bias", [P, 3, HP])
        bo = a.sb("at_bo", [P, KT])
        shift = a.sb("at_shift", [P, 1])
        hT = a.sb("at_hT", [P, 2, 2, KT, S], F32R)
        w_raw = a.sb("at_w_raw", [P, 3, KT, P])
        w_hi = a.sb("at_w_hi", [P, 3, KT, P], F32R)
        w_lo = a.sb("at_w_lo", [P, 3, KT, P], F32R)
        stage = a.sb("at_stage", [P, 2, CH])
        qk = [[[a.sb(f"at_{n}{i}{part}", [P, S], F16) for part in ("hi", "lo")] for n in "qk"] for i in range(2)]
        vT = [a.sb(f"at_vT_{part}", [P, S], F16) for part in ("hi", "lo")]
        v = [a.sb(f"at_v{i}", [P, TB, 2, VW], F16) for i in range(2)]
        probs = [a.sb(f"at_p{i}", [P, 2, CH]) for i in range(2)]
        p_hi = [a.sb(f"at_p_hi{i}", [P, 2, CH], F16) for i in range(2)]
        p_lo = [a.sb(f"at_p_lo{i}", [P, 2, CH], F16) for i in range(2)]
        rsum = a.sb("at_rsum", [P, 2, CT])
        ctx_tok = a.sb("at_ctx_tok", [P, CT, 2, DH])
        cT_hi = a.sb("at_cT_hi", [P, HP, S], F32R)
        cT_lo = a.sb("at_cT_lo", [P, HP, S], F32R)
        xio = a.sb("at_xio", [P, TB, D])
        wo_hi = a.sb("at_wo_hi", [P, HP, D], F32R)
        wo_lo = a.sb("at_wo_lo", [P, HP, D], F32R)
        y = a.sb("at_y", [P, KT, CH])
        ps_s = [a.ps(f"at_ps_s{i}", [P, 2, CH]) for i in range(2)]
        ps_o = a.ps("at_ps_o", [P, 2, CH])
        ps_m = [a.ps(f"at_ps_m{i}", [P, CH]) for i in range(2)]
        ps_m16 = [m[:].bitcast(F16).rearrange("p (t h d) -> p t h d", t=TB, h=2) for m in ps_m]
        (ld_const, ld_wo, ld_hT, ld_w, ld_x, st_x, const_done, wo_done, sc_done, pv_done, pj_mm, vt_mm, ct_mm, op_mm, yt_mm,
         exp_done, pj_full, vt_hi, ct_hi, y_done, p_hi_done, pj_hi, wh_done, p_lo_done, pj_lo, wl_done, r_done, cx_done,
         vt_lo, ct_lo, yg_done, x1_done, tick) = a.sems(
            "at_", "ld_const ld_wo ld_hT ld_w ld_x st_x const_done wo_done sc_done pv_done pj_mm vt_mm ct_mm op_mm yt_mm "
            "exp_done pj_full vt_hi ct_hi y_done p_hi_done pj_hi wh_done p_lo_done pj_lo wl_done r_done cx_done "
            "vt_lo ct_lo yg_done x1_done tick")
        w_dram = [io[n].rearrange("(k p) n -> p k n", p=P) for n in ("Wv", "Wq", "Wk")]
        NPAIR = B * HP

        def o_view():
            return ps_o[:, :, 0:CT * (DH + 1)].rearrange("p h (t c) -> p h t c", c=DH + 1)

        with nc.Block() as block:

            @block.sync
            def _(sp):
                sp.dma_start(ident16[:], io["ident16"]).then_inc(ld_const, 16)
                sp.dma_start(causal[:], io["causal16"]).then_inc(ld_const, 16)
                sp.dma_start(bias[:], io["b_vqk"]).then_inc(ld_const, 16)
                sp.dma_start(bo[:], io["bo_col"]).then_inc(ld_const, 16)

                def load_hT(b):
                    for part, name in enumerate(("hT_hi", "hT_lo")):
                        sp.dma_start(f32(hT[:, b % 2, part]), scr[name][b % B]).then_inc(ld_hT, 16)

                def load_w(n):
                    for i in range(3):
                        sp.dma_start(w_raw[:, i], w_dram[i][:, :, ds((n % HP) * P, P)]).then_inc(ld_w, 16)

                load_w(0)
                load_hT(0)
                sp.wait_ge(wh_done, at(1))
                sp.wait_ge(wl_done, at(1))
                load_w(1)
                sp.dma_start(xio[:], io["Wo"].rearrange("(h p) n -> p h n", p=P)).then_inc(ld_wo, 16)
                sp.wait_ge(wo_done, 2)
                with sp.Fori(0, B) as b:
                    hold(sp, tick, (pj_mm, at(NPJ * HP * b)))
                    load_hT(b + 1)
                    sp.dma_start(xio[:], io["states"][b].rearrange("(t p) d -> p t d", p=P)).then_inc(ld_x, 16)
                    with sp.Fori(0, HP) as j:
                        hold(sp, tick, (wh_done, at(b * HP + j + 2)), (wl_done, at(b * HP + j + 2)))
                        load_w(b * HP + j + 2)
                    hold(sp, tick, (x1_done, at(NC * (b + 1))))
                    sp.dma_start(scr["x1"][b].rearrange("(t p) d -> p t d", p=P), xio[:]).then_inc(st_x, 16)
                    hold(sp, tick, (st_x, 16 * b + 16))

            @block.gpsimd
            def _(pool):
                for s in (pj_lo, wh_done):
                    pool.sem_inc(s, CREDIT)
                pool.memset(shift[:], SCORE_SHIFT).then_inc(const_done, 1)
                for i in range(2):
                    pool.memset(v[i][:, :, :, DH:DH + 2], 1.0).then_inc(const_done, 1)

                def split_weights(n):
                    hold(pool, tick, (ld_w, 48 * n + 48))
                    pool.tensor_copy(w_hi[:], w_raw[:]).then_inc(wh_done, 1)

                def split_projection(base, i, dst):
                    w, c = PROJ[i]
                    cols = slice(c * CH, (c + 1) * CH)
                    hi, lo = vT if w == V_ else qk[dst][w - 1]
                    hold(pool, tick, (pj_hi, at(base + i + 1)))
                    pool.tensor_tensor(lo[:, cols], stage[:, i % 2, :], hi[:, cols], ALU.subtract).then_inc(pj_lo, 1)

                split_weights(0)
                for i in range(NPJ):
                    split_projection(0, i, 0)
                pool.wait_ge(pj_mm, at(NPJ))
                split_weights(1)
                hold(pool, tick, (ld_wo, 16))
                pool.tensor_copy(wo_hi[:], xio[:]).then_inc(wo_done, 1)
                with pool.Fori(0, B) as b, pool.Fori(0, HP // 2) as j:
                    for par in range(2):
                        it = b * HP + j * 2 + par
                        for i in range(NPJ):
                            split_projection(NPJ * (it + 1), i, 1 - par)
                        pool.wait_ge(pj_mm, at(NPJ * (it + 2)))
                        split_weights(it + 2)

            @block.vector
            def _(dve):
                for s in (p_hi_done, p_lo_done, wl_done, r_done, cx_done, vt_lo, ct_lo, yg_done, x1_done):
                    dve.sem_inc(s, CREDIT)

                def split_weights(n):
                    dve.wait_ge(wh_done, at(n + 1))
                    dve.tensor_tensor(w_lo[:], w_raw[:], f32(w_hi[:]), ALU.subtract).then_inc(wl_done, 1)

                def low_values(n, dst):
                    dve.wait_ge(vt_mm, 2 * n + 2)
                    dve.tensor_copy(v[dst][:, :, :, DH + 2:VW], ps_m16[0]).then_inc(vt_lo, 1)

                def normalise(n, count):
                    dve.wait_ge(pv_done, at(count))
                    dve.reciprocal(rsum[:], o_view()[:, :, :, DH]).then_inc(r_done, 1)
                    dve.wait_ge(r_done, at(n + 1))
                    dve.tensor_tensor(ctx_tok[:].rearrange("p t h d -> p h t d"), o_view()[:, :, :, 0:DH],
                                      rsum[:].unsqueeze(3).broadcast_to([P, 2, CT, DH]), ALU.mult).then_inc(cx_done, 1)

                def low_context(n, hp, c):
                    dve.wait_ge(ct_hi, at(n + 1))
                    cols = slice(c * CH, (c + 1) * CH)
                    dve.tensor_tensor(cT_lo[:, hp, cols], ps_m[c][:], f32(cT_hi[:, hp, cols]), ALU.subtract).then_inc(ct_lo, 1)

                split_weights(0)
                dve.wait_ge(pj_mm, at(NPJ))
                split_weights(1)
                dve.wait_ge(const_done, 3)
                low_values(0, 0)
                dve.wait_ge(wo_done, 1)
                dve.tensor_tensor(wo_lo[:], xio[:], f32(wo_hi[:]), ALU.subtract).then_inc(wo_done, 1)
                with dve.Fori(0, B) as b:
                    with dve.Fori(0, HP // 2) as j:
                        for par in range(2):
                            hp = j * 2 + par
                            it = b * HP + hp
                            for u, (qc, kt) in enumerate(UNITS):
                                off = max(0, kt * P - qc * CH)
                                dve.wait_ge(exp_done, at(it * NU + u + 1))
                                dve.wait_ge(pv_done, at(it * NU + u - 1))
                                dve.tensor_copy(p_hi[u % 2][:, :, off:], probs[u % 2][:, :, off:]).then_inc(p_hi_done, 1)
                                dve.wait_ge(p_hi_done, at(it * NU + u + 1))
                                dve.tensor_tensor(p_lo[u % 2][:, :, off:], probs[u % 2][:, :, off:],
                                                  p_hi[u % 2][:, :, off:], ALU.subtract).then_inc(p_lo_done, 1)
                                if u == CT - 1 + LAG:
                                    normalise(it * NC, it * NU + CT)
                                if u == SPLIT_W_AT:
                                    split_weights(it + 2)
                                if u == CTX_AT:
                                    low_context(it * NC, hp, 0)
                            normalise(it * NC + 1, it * NU + NU)
                            low_values(it + 1, 1 - par)
                            low_context(it * NC + 1, hp, 1)
                    for c in range(NC):
                        for m in range(KT):
                            dve.wait_ge(y_done, at(b * NC * KT + c * KT + m + 1))
                            dve.tensor_scalar(y[:, m, :], y[:, m, :], modT[:, 2 * KT + m, ds(b, 1)], None,
                                              ALU.mult).then_inc(yg_done, 1)
                        if c == 0:
                            dve.wait_ge(ld_x, 16 * b + 16)
                        dve.wait_ge(yt_mm, at(b * NC + c + 1))
                        tiles = slice(c * CT, (c + 1) * CT)
                        dve.tensor_tensor(xio[:, tiles, :], xio[:, tiles, :],
                                          ps_o[:].rearrange("p h (t d) -> p (h t) d", d=D), ALU.add).then_inc(x1_done, 1)

            @block.scalar
            def _(act):
                for s in (exp_done, pj_full, pj_hi, vt_hi, ct_hi, y_done):
                    act.sem_inc(s, CREDIT)

                def project(base, i, hp, dst):
                    w, c = PROJ[i]
                    hold(act, tick, (pj_mm, at(base + i + 1)), (pj_lo, at(base + i - 1)))
                    act.activation(stage[:, i % 2, :], ps_m[i % 2][:], ACT.Tanh, bias=bias[:, w, ds(hp, 1)]).then_inc(pj_full, 1)
                    hi = vT[0] if w == V_ else qk[dst][w - 1][0]
                    act.activation(hi[:, c * CH:(c + 1) * CH], ps_m[i % 2][:], ACT.Tanh,
                                   bias=bias[:, w, ds(hp, 1)]).then_inc(pj_hi, 1)

                def high_values(n, dst):
                    act.wait_ge(vt_mm, 2 * n + 1)
                    act.activation(v[dst][:, :, :, 0:DH], ps_m16[1], ACT.Copy).then_inc(vt_hi, 1)

                def high_context(n, hp, c):
                    hold(act, tick, (ct_mm, n + 1))
                    act.activation(cT_hi[:, hp, c * CH:(c + 1) * CH], ps_m[c][:], ACT.Copy).then_inc(ct_hi, 1)

                act.wait_ge(ld_const, 16 * 4)
                for i in range(NPJ):
                    project(0, i, 0, 0)
                act.wait_ge(const_done, 3)
                high_values(0, 0)
                with act.Fori(0, B) as b:
                    with act.Fori(0, HP // 2) as j:
                        for par in range(2):
                            hp = j * 2 + par
                            it = b * HP + hp
                            for u, (qc, kt) in enumerate(UNITS):
                                off = max(0, kt * P - qc * CH)
                                act.wait_ge(sc_done, it * NU + u + 1)
                                act.wait_ge(p_lo_done, at(it * NU + u - 1))
                                act.activation(probs[u % 2][:, :, off:], ps_s[u % 2][:, :, off:], ACT.Exp,
                                               bias=shift[:], scale=SCORE_SCALE).then_inc(exp_done, 1)
                                if u in PROJ_AT:
                                    project(NPJ * (it + 1), PROJ_AT[u], (hp + 1) % HP, 1 - par)
                                if u == CTX_AT:
                                    high_context(it * NC, hp, 0)
                            high_values(it + 1, 1 - par)
                            high_context(it * NC + 1, hp, 1)
                    for c in range(NC):
                        for m in range(KT):
                            act.wait_ge(op_mm, b * NC * KT + c * KT + m + 1)
                            if m == 0:
                                act.wait_ge(yt_mm, at(b * NC + c))
                            act.activation(y[:, m, :], ps_s[c][:, m, :], ACT.Tanh, bias=bo[:, m:m + 1]).then_inc(y_done, 1)

            @block.tensor
            def _(pe):
                for s in (pv_done, pj_mm, yt_mm):
                    pe.sem_inc(s, CREDIT)

                def project(i, buf):
                    w, c = PROJ[i]
                    cols = slice(c * CH, (c + 1) * CH)
                    for k in range(KT):
                        step = three_products(pe, ps_m[i % 2][:], w_hi[:, w, k, :], w_lo[:, w, k, :],
                                              hT[:, buf, 0, k, cols], hT[:, buf, 1, k, cols], k == 0, k == KT - 1)
                    step.then_inc(pj_mm, 1)

                def values(part, base):
                    pe.wait_ge(pj_lo if part else pj_hi, at(base + NC))
                    for t in range(TB):
                        step = pe.transpose(ps_m16[1 - part][:, t, :, :].rearrange("p h d -> p (h d)"),
                                            vT[part][:, t * P:(t + 1) * P], ident16[:])
                    step.then_inc(vt_mm, 1)

                def scores(par, u):
                    qc, kt = UNITS[u]
                    off = max(0, kt * P - qc * CH)
                    cols = slice(qc * CH + off, (qc + 1) * CH)
                    diagonal = kt * P >= qc * CH
                    (q_hi, q_lo), (k_hi, k_lo) = qk[par]
                    keys = slice(kt * P, (kt + 1) * P)
                    pairs = [(k_hi, q_hi), (k_hi, q_lo), (k_lo, q_hi)]
                    for n, (kx, qx) in enumerate(pairs):
                        for h in range(2):
                            rows = slice(h * DH, (h + 1) * DH)
                            step = pe.matmul(ps_s[u % 2][:, h, off:], kx[rows, keys], qx[rows, cols], start=(n == 0),
                                             stop=(n == 2 and not diagonal), skip_group_check=True)
                    if diagonal:
                        for h in range(2):
                            step = pe.matmul(ps_s[u % 2][:, h, off:off + P], ident16[:], causal[:], start=False, stop=True,
                                             skip_group_check=True)
                    step.then_inc(sc_done, 1)

                def value_products(par, u):
                    qc, kt = UNITS[u]
                    first = max(0, kt - qc * CT)
                    for h in range(2):
                        ones_hi, lo = v[par][:, kt, h, 0:DH + 1], v[par][:, kt, h, DH + 2:VW]
                        for t in range(first, CT):
                            ph, pl = (p[u % 2][:, h, t * P:(t + 1) * P] for p in (p_hi, p_lo))
                            out = ps_o[:, h, t * (DH + 1):(t + 1) * (DH + 1)]
                            pe.matmul(out, ph, ones_hi, start=(kt == 0 and t == 0), stop=False, skip_group_check=True)
                            pe.matmul(out[:, 0:DH], ph, lo, start=False, stop=False, skip_group_check=True)
                            step = pe.matmul(out, pl, ones_hi, start=False, stop=(kt == qc * CT + t), skip_group_check=True)
                    step.then_inc(pv_done, 1)

                def context(n, c):
                    pe.wait_ge(cx_done, at(n + 1))
                    for t in range(CT):
                        step = pe.transpose(ps_m[c][:, t * P:(t + 1) * P], ctx_tok[:, t].rearrange("p h d -> p (h d)"),
                                            ident[:])
                    step.then_inc(ct_mm, 1)

                pe.wait_ge(ld_hT, 32)
                pe.wait_ge(wl_done, at(1))
                for i in range(NPJ):
                    if i >= 2:
                        pe.wait_ge(pj_hi, at(i - 1))
                    project(i, 0)
                pe.wait_ge(ld_const, 16 * 4)
                pe.wait_ge(pj_hi, at(NPJ))
                values(0, 0)
                values(1, 0)
                with pe.Fori(0, B) as b:
                    with pe.Fori(0, HP // 2) as j:
                        for par in range(2):
                            it = b * HP + j * 2 + par
                            nxt = it + 1
                            buf = (nxt // HP) % 2
                            base = NPJ * nxt
                            for s in range(NU + LAG):
                                if s < NU:
                                    if s == 0:
                                        pe.wait_ge(pj_lo, at(base))
                                        pe.wait_ge(y_done, at(b * NC * KT))
                                    pe.wait_ge(exp_done, at(it * NU + s - 1))
                                    scores(par, s)
                                if s in PROJ_AT:
                                    i = PROJ_AT[s]
                                    if i == 0:
                                        pe.wait_ge(ld_hT, 32 * (nxt // HP) + 32)
                                        pe.wait_ge(wl_done, at(nxt + 1))
                                        pe.wait_ge(vt_lo, at(it + 1))
                                    elif i == 1:
                                        pe.wait_ge(vt_hi, at(it + 1))
                                        pe.wait_ge(ct_lo, at(NC * it))
                                    else:
                                        pe.wait_ge(pj_hi, at(base + i - 1))
                                    project(i, buf)
                                if s == CTX_AT:
                                    pe.wait_ge(pj_hi, at(base + 5))
                                    context(it * NC, 0)
                                if s >= LAG:
                                    u = s - LAG
                                    if u == 0:
                                        pe.wait_ge(vt_hi, at(it + 1))
                                        pe.wait_ge(vt_lo, at(it + 1))
                                        pe.wait_ge(cx_done, at(it * NC))
                                        pe.wait_ge(x1_done, at(b * NC))
                                    if u == CT:
                                        pe.wait_ge(cx_done, at(it * NC + 1))
                                    pe.wait_ge(p_lo_done, at(it * NU + u + 1))
                                    value_products(par, u)
                            pe.wait_ge(pj_hi, at(base + NPJ))
                            values(0, base)
                            pe.wait_ge(ct_lo, at(it * NC + 1))
                            values(1, base)
                            pe.wait_ge(vt_hi, at(it + 2))
                            context(it * NC + 1, 1)
                    pe.wait_ge(exp_done, at((b + 1) * HP * NU))
                    pe.wait_ge(wo_done, 2)
                    for c in range(NC):
                        pe.wait_ge(ct_lo, at((b + 1) * HP * NC - 1 + c))
                        for m in range(KT):
                            outs = slice(m * P, (m + 1) * P)
                            for hp in range(HP):
                                step = three_products(pe, ps_s[c][:, m, :], wo_hi[:, hp, outs], wo_lo[:, hp, outs],
                                                      cT_hi[:, hp, c * CH:(c + 1) * CH], cT_lo[:, hp, c * CH:(c + 1) * CH],
                                                      hp == 0, hp == HP - 1)
                            step.then_inc(op_mm, 1)
                    for c in range(NC):
                        pe.wait_ge(yg_done, at(b * NC * KT + (c + 1) * KT))
                        if c == 0:
                            pe.wait_ge(cx_done, at((b + 1) * HP * NC))
                        else:
                            pe.wait_ge(x1_done, at(b * NC + 1))
                        for t in range(CT):
                            for m in range(KT):
                                step = pe.transpose(ps_o[:, t // 2, (t % 2) * D + m * P:(t % 2) * D + (m + 1) * P],
                                                    y[:, m, t * P:(t + 1) * P], ident[:])
                        step.then_inc(yt_mm, 1)


def phase_norm2(nc, io, scr, keep):
    with ExitStack() as ctx:
        a = Allocator(nc, ctx)
        h, modB = keep["stream"], keep["modB"]
        st = a.sb("n2_stats", [P, NT, 6])
        tmp = a.sb("n2_tmp", [P, 4, NT])
        col = a.sb("n2_columns", [P, 5, NT])
        (ld_x, bn, chain, var_ready, std_ready, norm_ready, xn_done, scaled) = a.sems(
            "n2_", "ld_x bn chain var_ready std_ready norm_ready xn_done scaled")
        with nc.Block() as block:

            @block.sync
            def _(sp):
                for b in range(B):
                    sp.dma_start(h[:, b * TB:(b + 1) * TB, :],
                                 scr["x1"][b].rearrange("(t p) d -> p t d", p=P)).then_inc(ld_x, 16)

            @block.scalar
            def _(act):
                act.wait_ge(var_ready, 1)
                act.activation(col[:, 2, :], col[:, 1, :], ACT.Sqrt).then_inc(std_ready, 1)

            @block.vector
            def _(dve):
                dve.wait_ge(ld_x, 16 * B)
                with dve.Fori(0, NT) as t:
                    dve.bn_stats(st[:, t, :], h[:, t, :]).then_inc(bn, 1)
                dve.wait_ge(bn, NT)
                variance_steps(dve, chain, 0, st, col[:, 0, :], tmp, col[:, 1, :], var_ready)
                dve.wait_ge(std_ready, 1)
                dve.reciprocal(col[:, 3, :], col[:, 2, :]).then_inc(norm_ready, 1)
                dve.wait_ge(norm_ready, 1)
                dve.scalar_tensor_tensor(col[:, 4, :], col[:, 0, :], -0.5, col[:, 3, :], ALU.mult,
                                         ALU.mult).then_inc(norm_ready, 1)
                dve.wait_ge(norm_ready, 2)
                with dve.Fori(0, NT) as t:
                    dve.tensor_scalar(h[:, t, :], h[:, t, :], col[:, 3, ds(t, 1)], col[:, 4, ds(t, 1)],
                                      ALU.mult, ALU.add).then_inc(xn_done, 1)
                dve.wait_ge(xn_done, NT)
                for b in range(B):
                    part = h[:, b * TB:(b + 1) * TB, :]
                    rows = [modB[:, b, i * D:(i + 1) * D].unsqueeze(1).broadcast_to([P, TB, D]) for i in range(2)]
                    dve.tensor_tensor(part, part, rows[1], ALU.mult).then_inc(scaled, 1)
                    dve.wait_ge(scaled, 2 * b + 1)
                    dve.tensor_tensor(part, part, rows[0], ALU.add).then_inc(scaled, 1)


def phase_output(nc, io, scr, keep):
    with ExitStack() as ctx:
        a = Allocator(nc, ctx)
        h, modB = keep["stream"], keep["modB"]
        x1 = a.sb("out_x1", [P, NT, D])
        ld, gated, added, stored = a.sems("out_", "ld gated added stored")
        with nc.Block() as block:

            @block.sync
            def _(sp):
                for b in range(B):
                    sp.dma_start(x1[:, b * TB:(b + 1) * TB, :],
                                 scr["x1"][b].rearrange("(t p) d -> p t d", p=P)).then_inc(ld, 16)
                for b in range(B):
                    sp.wait_ge(added, b + 1)
                    sp.dma_start(io["out"][b].rearrange("(t p) d -> p t d", p=P),
                                 h[:, b * TB:(b + 1) * TB, :]).then_inc(stored, 16)
                sp.wait_ge(stored, 16 * B)

            @block.vector
            def _(dve):
                for b in range(B):
                    part = h[:, b * TB:(b + 1) * TB, :]
                    gb = modB[:, b, 2 * D:3 * D].unsqueeze(1).broadcast_to([P, TB, D])
                    dve.tensor_tensor(part, part, gb, ALU.mult).then_inc(gated, 1)
                    dve.wait_ge(gated, b + 1)
                    if b == 0:
                        dve.wait_ge(ld, 16 * B)
                    dve.tensor_tensor(part, part, x1[:, b * TB:(b + 1) * TB, :], ALU.add).then_inc(added, 1)


L = 2
LH = 8
LP = LH // 2
INNER = LH * DH
HID = D * 4 * 2 // 3
HT = -(-HID // P)
QK_SCALE = 8.0
NORM_FLOOR = 1e-12
NCH = NT // CT
PREPS = NT + 1


def phase_layers(nc, io, scr, keep):
    with ExitStack() as ctx:
        a = Allocator(nc, ctx)
        x, ident = keep["stream"], keep["ident"]
        raw = a.sb("ly_raw", [P, 6144])
        w_hi = a.sb("ly_w_hi", [P, 4608], F32R)
        w_lo = a.sb("ly_w_lo", [P, 4608], F32R)
        opnd = a.sb("ly_operands", [P, 9232], F32R)
        rope = a.sb("ly_rope", [P, 4, TB, DH])
        rows = a.sb("ly_rows", [P, 4, DH])
        lncol = a.sb("ly_ln", [P, 2, KT])
        b1 = a.sb("ly_b1", [P, 2 * HT])
        b2 = a.sb("ly_b2", [P, D])
        prev_mask = a.sb("ly_prev_mask", [P, TB // 2, P])
        mask = a.sb("ly_mask", [P, 2, 2, P])
        carry = a.sb("ly_carry", [P, 2, TB + 1], F32R)
        shifted = a.sb("ly_shifted", [P, NT, P])
        expo = a.sb("ly_expo", [P, 2 * LH])
        sq = a.sb("ly_sq", [P, 2, INNER])
        norm2 = a.sb("ly_norm2", [P, 2, 2 * LH])
        rq = a.sb("ly_rq", [P, 2, LH])
        kn = a.sb("ly_kn", [P, INNER])
        xs = a.sb("ly_xs", [P, 2, D])
        ra = a.sb("ly_rope_a", [P, 2, INNER])
        rt = a.sb("ly_rope_t", [P, 2, INNER])
        sm = a.sb("ly_masked", [P, 2, 2, 2 * P])
        pr = a.sb("ly_probs", [P, 2, 2, 2 * P])
        small = a.sb("ly_small", [P, 2, 4, 2])
        def cut(start, *shape):
            n = int(np.prod(shape))
            names = "abcd"[:len(shape)]
            v = opnd[:, start:start + n]
            if len(shape) > 1:
                v = v.rearrange(f"p ({' '.join(names)}) -> p {' '.join(names)}", **dict(zip(names, shape)))
            return v, start + n
        hT, o = cut(0, 2, 2, KT, P + 1)
        qT, o = cut(o + o % 2, 2, 2, LP, P)
        kT, o = cut(o, 2, LP, 2 * P)
        vv, o = cut(o, 2, 2, INNER)
        pT, o = cut(o, 2, 2, 2 * P)
        oT, o = cut(o, 2, LP, P)
        assert o <= 9232
        fT, o = cut(0, 2, KT, CH)
        uT, o = cut(o, 2, HT, CH)
        assert o <= 9232
        st = a.sb("ly_st", [P, CT, 12])
        mv = a.sb("ly_mv", [P, CT, 2])
        nrm = a.sb("ly_nrm", [P, 3, CT])
        xn = sq[:].rearrange("p a (b d) -> p (a b) d", d=D)
        ffull = a.sb("ly_ffull", [P, KT, CH])
        gl = pr[:].rearrange("p a b c -> p a (b c)")
        uf = rt
        bank = [a.ps(f"ly_ps{i}", [P, CH]) for i in range(8)]
        ps_qkv, ps_s, ps_pt, ps_misc, ps_pv = bank[0:3], bank[3:5], bank[5], bank[6], bank[7]
        wqkv = [w[:, 0:KT * 3 * INNER].rearrange("p (k n) -> p k n", k=KT) for w in (w_hi, w_lo)]
        wo = [w[:, KT * 3 * INNER:KT * 3 * INNER + LP * D].rearrange("p (k n) -> p k n", k=LP) for w in (w_hi, w_lo)]
        w1 = [w[:, 0:KT * 2 * HT * P].rearrange("p (k n) -> p k n", k=KT) for w in (w_hi, w_lo)]
        w2 = [w[:, KT * 2 * HT * P:KT * 2 * HT * P + HT * D].rearrange("p (k n) -> p k n", k=HT) for w in (w_hi, w_lo)]
        A_COLS, F_COLS = KT * 3 * INNER + LP * D, KT * 2 * HT * P + HT * D
        T_COLS = 4 * TB * DH
        qkv_cols = slice(0, KT * 3 * INNER)
        names = ("ld_const ld_attn ld_ffn shift_in const_done zeroed "
                 "w_hi_done w_lo_done rope_q "
                 "xT_mm qkv_mm sc_mm pt_mm pv_mm qkT_mm wo_mm "
                 "h_hi ex_done sq_done pt_hi o_hi qkT_hi v_hi "
                 "mx_done nb_done h_lo rc_done nm_done pt_lo red_done fl_done ra_done kn_done o_lo qkT_lo v_lo xa_done msk "
                 "ca_in ca_out pw_done add_done rq_done xs_done "
                 "bn ag vr nr xnd fT_mm ff_done f_hi f_lo gu_mm gl_done uf_done u_hi u_lo y_mm ya_done pw2 b2_done tick")
        s = dict(zip(names.split(), a.sems("ly_", names)))
        PE_SEMS = "xT_mm qkv_mm sc_mm pt_mm pv_mm qkT_mm wo_mm fT_mm gu_mm y_mm"
        ACT_SEMS = "h_hi ex_done sq_done pt_hi o_hi qkT_hi v_hi w_hi_done ff_done f_hi gl_done"
        DVE_SEMS = ("mx_done nb_done h_lo rc_done nm_done pt_lo red_done fl_done ra_done kn_done o_lo qkT_lo v_lo xa_done msk "
                    "w_lo_done rope_q bn ag vr nr xnd f_lo uf_done u_lo ya_done")
        POOL_SEMS = "xs_done ca_in ca_out pw_done add_done rq_done u_hi pw2 b2_done"

        def start(eng, which):
            for n in which.split():
                eng.sem_inc(s[n], CREDIT)

        def after(eng, name, n):
            eng.wait_ge(s[name], at(n))

        def tiles_of(l, j, par, b):
            t = b * TB + j * 2 + par
            return t, l * NT + t, l * PREPS + t + 1

        with nc.Block() as block:

            @block.sync
            def _(sp):
                sp.dma_start(prev_mask[:], io["prev_mask"]).then_inc(s["ld_const"], 16)
                sp.dma_start(mask[:], io["mask"]).then_inc(s["ld_const"], 16)
                with sp.Fori(0, L) as l:
                    hold(sp, s["tick"], (s["w_lo_done"], at(4 * l)))
                    hold(sp, s["tick"], (s["rope_q"], at(4 * l)))
                    sp.dma_start(raw[:, qkv_cols].rearrange("p (k n) -> p k n", k=KT),
                                 io["ffn_wqkv"][l].rearrange("(k p) n -> p k n", p=P)).then_inc(s["ld_attn"], 16)
                    sp.dma_start(raw[:, KT * 3 * INNER:A_COLS].rearrange("p (k n) -> p k n", k=LP),
                                 io["ffn_wo"][l].rearrange("(k p) n -> p k n", p=P)).then_inc(s["ld_attn"], 16)
                    sp.dma_start(raw[:, A_COLS:A_COLS + T_COLS], io["rope"]).then_inc(s["ld_attn"], 16)
                    sp.dma_start(rows[:], io["qk_rows"][l].partition_broadcast(P)).then_inc(s["ld_attn"], 16)
                    hold(sp, s["tick"], (s["ya_done"], at(NCH * l)))
                    hold(sp, s["tick"], (s["w_lo_done"], at(4 * l + 2)))
                    hold(sp, s["tick"], (s["rope_q"], at(4 * l + 4)))
                    sp.dma_start(raw[:, 0:KT * 2 * HT * P].rearrange("p (k n) -> p k n", k=KT),
                                 io["w1"][l].rearrange("(k p) a n -> p k (a n)", p=P)).then_inc(s["ld_ffn"], 16)
                    sp.dma_start(raw[:, KT * 2 * HT * P:F_COLS].rearrange("p (k n) -> p k n", k=HT),
                                 io["w2"][l].rearrange("(k p) n -> p k n", p=P)).then_inc(s["ld_ffn"], 16)
                    sp.dma_start(lncol[:], io["ln_col"][l]).then_inc(s["ld_ffn"], 16)
                    sp.dma_start(b1[:], io["b1_col"][l]).then_inc(s["ld_ffn"], 16)
                    sp.dma_start(b2[:], io["ffn_b2"][l].partition_broadcast(P)).then_inc(s["ld_ffn"], 16)
                    with sp.Fori(0, B) as b:
                        hold(sp, s["tick"], (s["xa_done"], at(l * NT + b * TB + TB)))
                        sp.dma_start(shifted[1:P, ds(b * TB, TB), :], x[0:P - 1, ds(b * TB, TB), P:D]).then_inc(s["shift_in"], 16)
                        sp.dma_start(shifted[0:1, ds(b * TB + 1, TB - 1), :],
                                     x[P - 1:P, ds(b * TB, TB - 1), P:D]).then_inc(s["shift_in"], 16)

            @block.gpsimd
            def _(pool):
                start(pool, POOL_SEMS)
                pool.memset(expo[:], -0.5).then_inc(s["const_done"], 1)
                pool.memset(shifted[:], 0.0).then_inc(s["zeroed"], 1)
                pool.memset(f32(opnd[:]), 0.0).then_inc(s["zeroed"], 1)
                pool.memset(f32(carry[:]), 0.0).then_inc(s["zeroed"], 1)
                pool.wait_ge(s["const_done"], 1)
                pool.wait_ge(s["zeroed"], 3)

                def carry_over(pi, par, w):
                    hold(pool, s["tick"], (s["qkv_mm"], at(3 * pi - 3)), (s["ca_out"], at(pi)))
                    pool.tensor_copy(hT[:, par, :, 1, 0], f32(carry[:, :, ds(w, 1)]).rearrange("p a b -> p (a b)")).then_inc(s["ca_in"], 1)
                    hold(pool, s["tick"], (s["h_lo"], at(pi + 1)))
                    pool.tensor_copy(carry[:, :, ds(w + 1, 1)].rearrange("p a b -> p (a b)"), f32(hT[:, par, :, 1, P])).then_inc(s["ca_out"], 1)

                def stage_tile(buf, tile):
                    pool.tensor_copy(xs[:, buf, :], x[:, tile, :]).then_inc(s["xs_done"], 1)

                def prepare(pi, par, w, tile_after):
                    hold(pool, s["tick"], (s["xT_mm"], at(pi)))
                    stage_tile(1 - par, tile_after)
                    carry_over(pi, par, w)
                    hold(pool, s["tick"], (s["fl_done"], at(pi + 1)))
                    pool.tensor_tensor(norm2[:, 1, :], norm2[:, 0, :], expo[:], ALU.pow).then_inc(s["pw_done"], 1)
                    hold(pool, s["tick"], (s["pw_done"], at(pi + 1)))
                    pool.tensor_scalar(rq[:, par, :], norm2[:, 1, 0:LH], QK_SCALE, None, ALU.mult).then_inc(s["rq_done"], 1)
                    for i in range(2):
                        hold(pool, s["tick"], (s["ra_done"], at(6 * pi + 3 * i + 3)))
                        pool.tensor_tensor(ra[:, i, :], ra[:, i, :], rt[:, i, :], ALU.add).then_inc(s["add_done"], 1)

                with pool.Fori(0, L) as l:
                    hold(pool, s["tick"], (s["ya_done"], at(NCH * l)))
                    stage_tile(0, 0)
                    prepare(l * PREPS, 0, 0, 1)
                    with pool.Fori(0, B) as b, pool.Fori(0, TB // 2) as j:
                        for par in range(2):
                            t, g, pi = tiles_of(l, j, par, b)
                            prepare(pi, 1 - par, (j * 2 + par + 1) % TB, (t + 2) % NT)
                    with pool.Fori(0, NCH) as c:
                        ci = l * NCH + c
                        hold(pool, s["tick"], (s["vr"], at(ci + 1)))
                        pool.tensor_tensor(nrm[:, 1, :], nrm[:, 0, :], expo[:, 0:CT], ALU.pow).then_inc(s["pw2"], 1)
                        hold(pool, s["tick"], (s["xnd"], at(ci + 1)))
                        pool.tensor_tensor(x[:, ds(c * CT, CT), :], x[:, ds(c * CT, CT), :],
                                           b2[:].unsqueeze(1).broadcast_to([P, CT, D]), ALU.add).then_inc(s["b2_done"], 1)
                        for i in range(HT):
                            hold(pool, s["tick"], (s["uf_done"], at(ci * HT + i + 1)), (s["y_mm"], at(ci)))
                            pool.tensor_copy(uT[:, 0, i, :], uf[:, i % 2, :]).then_inc(s["u_hi"], 1)

            @block.scalar
            def _(act):
                start(act, ACT_SEMS)
                act.wait_ge(s["ld_const"], 32)
                act.wait_ge(s["zeroed"], 3)

                def split_weights(n, ld, ld_n, cols):
                    hold(act, s["tick"], (s[ld], ld_n))
                    for i in range(2):
                        part = slice(i * cols // 2, (i + 1) * cols // 2)
                        act.activation(w_hi[:, part], raw[:, part], ACT.Copy).then_inc(s["w_hi_done"], 1)

                def stream_hi(pi, par):
                    hold(act, s["tick"], (s["xT_mm"], at(pi + 1)), (s["qkv_mm"], at(3 * pi - 3)))
                    act.activation(hT[:, par, 0, 0, 0:P], ps_misc[:, 0:P], ACT.Copy)
                    act.activation(hT[:, par, 0, 1, 1:P + 1], ps_misc[:, P:2 * P], ACT.Copy).then_inc(s["h_hi"], 1)

                def squares(pi):
                    hold(act, s["tick"], (s["qkv_mm"], at(3 * pi + 2)), (s["red_done"], at(pi)))
                    for i in range(2):
                        step = act.activation(sq[:, i, :], ps_qkv[i][:], ACT.Square)
                    step.then_inc(s["sq_done"], 1)

                def qk_hi(pi, par, i):
                    hold(act, s["tick"], (s["qkT_mm"], at(2 * pi + i + 1)))
                    if i == 0:
                        act.activation(qT[:, par, 0], ps_misc[:].rearrange("p (j q) -> p j q", j=LP), ACT.Copy).then_inc(s["qkT_hi"], 1)
                    else:
                        act.activation(kT[:, 0, :, par * P:(par + 1) * P], ps_pt[:].rearrange("p (j q) -> p j q", j=LP),
                                       ACT.Copy).then_inc(s["qkT_hi"], 1)

                def v_high(pi, par, g):
                    hold(act, s["tick"], (s["qkv_mm"], at(3 * pi + 3)), (s["pv_mm"], at(4 * g)))
                    act.activation(vv[:, par, 0, :], ps_qkv[2][:], ACT.Copy).then_inc(s["v_hi"], 1)

                def exps(g, j, par):
                    hold(act, s["tick"], (s["nb_done"], at(4 * g + j + 1)))
                    for h in range(2):
                        step = act.activation(pr[:, j % 2, h, :], sm[:, j % 2, h, :], ACT.Exp,
                                              bias=small[:, j % 2, 1, h:h + 1], scale=rq[:, par, 2 * j + h:2 * j + h + 1],
                                              accum_out=small[:, j % 2, 2, h:h + 1])
                    step.then_inc(s["ex_done"], 1)

                def probs_hi(g, j):
                    hold(act, s["tick"], (s["pt_mm"], at(4 * g + j + 1)), (s["pv_mm"], at(4 * g + j)))
                    act.activation(pT[:, 0].rearrange("p a b -> p (a b)"), ps_pt[:], ACT.Copy).then_inc(s["pt_hi"], 1)

                def out_hi(g, half):
                    hold(act, s["tick"], (s["pv_mm"], at(4 * g + 2 * half + 2)), (s["wo_mm"], at(g)))
                    for h in range(2):
                        rws = slice(h * DH, (h + 1) * DH)
                        src = ps_pv[rws, :].rearrange("p (j h q) -> p j h q", j=2, h=2)[:, :, h, :]
                        step = act.activation(oT[rws, 0, 2 * half:2 * half + 2, :], src, ACT.Copy)
                    step.then_inc(s["o_hi"], 1)

                with act.Fori(0, L) as l:
                    after(act, "y_mm", NCH * l)
                    split_weights(0, "ld_attn", 64 * l + 64, A_COLS)
                    stream_hi(l * PREPS, 0)
                    squares(l * PREPS)
                    v_high(l * PREPS, 0, l * NT)
                    qk_hi(l * PREPS, 0, 0)
                    qk_hi(l * PREPS, 0, 1)
                    with act.Fori(0, B) as b, act.Fori(0, TB // 2) as jj:
                        for par in range(2):
                            t, g, pi = tiles_of(l, jj, par, b)
                            stream_hi(pi, 1 - par)
                            exps(g, 0, par)
                            exps(g, 1, par)
                            squares(pi)
                            probs_hi(g, 0)
                            exps(g, 2, par)
                            probs_hi(g, 1)
                            exps(g, 3, par)
                            out_hi(g, 0)
                            probs_hi(g, 2)
                            probs_hi(g, 3)
                            out_hi(g, 1)
                            qk_hi(pi, 1 - par, 0)
                            qk_hi(pi, 1 - par, 1)
                            v_high(pi, 1 - par, g + 1)
                    after(act, "wo_mm", NT * (l + 1))
                    after(act, "qkT_mm", 2 * PREPS * (l + 1))
                    after(act, "ca_out", PREPS * (l + 1))
                    split_weights(1, "ld_ffn", 80 * l + 80, F_COLS)
                    with act.Fori(0, NCH) as c:
                        ci = l * NCH + c
                        hold(act, s["tick"], (s["fT_mm"], at(ci + 1)), (s["f_lo"], at(ci)), (s["gu_mm"], at(2 * HT * ci)))
                        for k in range(KT):
                            step = act.activation(ffull[:, k, :], bank[4 + k][:], ACT.Identity,
                                                  scale=lncol[:, 0, k:k + 1], bias=lncol[:, 1, k:k + 1])
                        step.then_inc(s["ff_done"], 1)
                        for k in range(KT):
                            step = act.activation(fT[:, 0, k, :], bank[4 + k][:], ACT.Identity,
                                                  scale=lncol[:, 0, k:k + 1], bias=lncol[:, 1, k:k + 1])
                        step.then_inc(s["f_hi"], 1)
                        for i in range(HT):
                            hold(act, s["tick"], (s["gu_mm"], at(2 * (ci * HT + i) + 2)), (s["uf_done"], at(ci * HT + i - 1)))
                            act.activation(gl[:, i % 2, :], bank[2 + i % 2][:], ACT.Gelu,
                                           bias=b1[:, HT + i:HT + i + 1]).then_inc(s["gl_done"], 1)

            @block.vector
            def _(dve):
                start(dve, DVE_SEMS)
                dve.wait_ge(s["ld_const"], 32)
                dve.wait_ge(s["zeroed"], 3)

                def split_weights(n, cols):
                    for i in range(2):
                        part = slice(i * cols // 2, (i + 1) * cols // 2)
                        after(dve, "w_hi_done", n + i + 1)
                        dve.tensor_tensor(w_lo[:, part], raw[:, part], f32(w_hi[:, part]), ALU.subtract).then_inc(s["w_lo_done"], 1)

                def stream_lo(pi, par):
                    after(dve, "h_hi", pi + 1)
                    dve.tensor_tensor(hT[:, par, 1, 0, 0:P], ps_misc[:, 0:P], f32(hT[:, par, 0, 0, 0:P]), ALU.subtract)
                    dve.tensor_tensor(hT[:, par, 1, 1, 1:P + 1], ps_misc[:, P:2 * P], f32(hT[:, par, 0, 1, 1:P + 1]),
                                      ALU.subtract).then_inc(s["h_lo"], 1)

                def squared_norms(pi):
                    after(dve, "sq_done", pi + 1)
                    dve.tensor_reduce(norm2[:, 0, :], sq[:].rearrange("p a (h d) -> p (a h) d", d=DH), AX.X, ALU.add).then_inc(s["red_done"], 1)
                    after(dve, "red_done", pi + 1)
                    dve.tensor_scalar(norm2[:, 0, :], norm2[:, 0, :], NORM_FLOOR ** 2, None, ALU.max).then_inc(s["fl_done"], 1)

                def rotate(pi, i, z, w):
                    cos, sin = rope[:, 2 * i, w, :], rope[:, 2 * i + 1, w, :]
                    zh = z.rearrange("p (h d) -> p h d", d=DH)
                    th = rt[:, i, :].rearrange("p (h d) -> p h d", d=DH)
                    half = DH // 2
                    after(dve, "qkT_mm", 2 * pi)
                    dve.tensor_tensor(ra[:, i, :].rearrange("p (h d) -> p h d", d=DH), zh,
                                      cos.unsqueeze(1).broadcast_to([P, LH, DH]), ALU.mult).then_inc(s["ra_done"], 1)
                    for a0, b0 in ((0, half), (half, 0)):
                        dve.tensor_tensor(th[:, :, a0:a0 + half], zh[:, :, b0:b0 + half],
                                          sin[:, a0:a0 + half].unsqueeze(1).broadcast_to([P, LH, half]), ALU.mult).then_inc(s["ra_done"], 1)

                def normalise_keys(pi):
                    after(dve, "pw_done", pi + 1)
                    dve.tensor_tensor(kn[:].rearrange("p (h d) -> p h d", d=DH), ps_qkv[1][:].rearrange("p (h d) -> p h d", d=DH),
                                      norm2[:, 1, LH:2 * LH].unsqueeze(2).broadcast_to([P, LH, DH]), ALU.mult).then_inc(s["kn_done"], 1)
                    after(dve, "kn_done", pi + 1)

                def qk_lo(pi, par, i):
                    after(dve, "qkT_hi", 2 * pi + i + 1)
                    if i == 0:
                        hi, lo, src = qT[:, par, 0], qT[:, par, 1], ps_misc
                    else:
                        hi, lo, src = kT[:, 0, :, par * P:(par + 1) * P], kT[:, 1, :, par * P:(par + 1) * P], ps_pt
                    dve.tensor_tensor(lo, src[:].rearrange("p (j q) -> p j q", j=LP), f32(hi), ALU.subtract).then_inc(s["qkT_lo"], 1)

                def v_low(pi, par):
                    after(dve, "v_hi", pi + 1)
                    dve.tensor_tensor(vv[:, par, 1, :], ps_qkv[2][:], f32(vv[:, par, 0, :]), ALU.subtract).then_inc(s["v_lo"], 1)

                def maxima(g, pi, j, par):
                    hold(dve, s["tick"], (s["sc_mm"], at(4 * g + j + 1)), (s["ex_done"], at(4 * g + j - 1)))
                    for h in range(2):
                        dve.tensor_tensor_reduce(sm[:, j % 2, h, :], ps_s[h][:, 0:2 * P], mask[:, par].rearrange("p a b -> p (a b)"),
                                                 1.0, -3.0e38, ALU.add, ALU.max, small[:, j % 2, 0, h:h + 1]).then_inc(s["mx_done"], 1)
                    after(dve, "mx_done", 2 * (4 * g + j) + 2)
                    after(dve, "rq_done", pi)
                    dve.scalar_tensor_tensor(small[:, j % 2, 1, :], small[:, j % 2, 0, :], -1.0, rq[:, par, 2 * j:2 * j + 2],
                                             ALU.mult, ALU.mult).then_inc(s["nb_done"], 1)

                def normalise_probs(g, j):
                    after(dve, "ex_done", 4 * g + j + 1)
                    dve.reciprocal(small[:, j % 2, 3, :], small[:, j % 2, 2, :]).then_inc(s["rc_done"], 1)
                    after(dve, "rc_done", 4 * g + j + 1)
                    for h in range(2):
                        step = dve.tensor_scalar(pr[:, j % 2, h, :], pr[:, j % 2, h, :], small[:, j % 2, 3, h:h + 1], None, ALU.mult)
                    step.then_inc(s["nm_done"], 1)

                def probs_lo(g, j):
                    after(dve, "pt_hi", 4 * g + j + 1)
                    dve.tensor_tensor(pT[:, 1].rearrange("p a b -> p (a b)"), ps_pt[:], f32(pT[:, 0]).rearrange("p a b -> p (a b)"),
                                      ALU.subtract).then_inc(s["pt_lo"], 1)

                def out_lo(g, half):
                    after(dve, "o_hi", 2 * g + half + 1)
                    for h in range(2):
                        rws = slice(h * DH, (h + 1) * DH)
                        src = ps_pv[rws, :].rearrange("p (j h q) -> p j h q", j=2, h=2)[:, :, h, :]
                        step = dve.tensor_tensor(oT[rws, 1, 2 * half:2 * half + 2, :], src,
                                                 f32(oT[rws, 0, 2 * half:2 * half + 2, :]), ALU.subtract)
                    step.then_inc(s["o_lo"], 1)

                with dve.Fori(0, L) as l:
                    split_weights(4 * l, A_COLS)
                    for i in range(4):
                        dve.tensor_tensor(rope[:, i], raw[:, A_COLS + i * TB * DH:A_COLS + (i + 1) * TB * DH].rearrange("p (t d) -> p t d", d=DH),
                                          rows[:, i, :].unsqueeze(1).broadcast_to([P, TB, DH]), ALU.mult).then_inc(s["rope_q"], 1)
                    hold(dve, s["tick"], (s["rope_q"], at(4 * l + 4)))
                    pi = l * PREPS
                    stream_lo(pi, 0)
                    squared_norms(pi)
                    rotate(pi, 0, ps_qkv[0][:], 0)
                    normalise_keys(pi)
                    rotate(pi, 1, kn[:], 0)
                    v_low(pi, 0)
                    qk_lo(pi, 0, 0)
                    qk_lo(pi, 0, 1)
                    with dve.Fori(0, B) as b, dve.Fori(0, TB // 2) as jj:
                        for par in range(2):
                            t, g, pi = tiles_of(l, jj, par, b)
                            nw = (jj * 2 + par + 1) % TB
                            if par == 0:
                                dve.tensor_copy(mask[:, 0, 1, :], prev_mask[:, jj, :]).then_inc(s["msk"], 1)
                                after(dve, "msk", g // 2 + 1)
                            maxima(g, pi, 0, par)
                            stream_lo(pi, 1 - par)
                            normalise_probs(g, 0)
                            maxima(g, pi, 1, par)
                            normalise_probs(g, 1)
                            probs_lo(g, 0)
                            squared_norms(pi)
                            maxima(g, pi, 2, par)
                            rotate(pi, 0, ps_qkv[0][:], nw)
                            probs_lo(g, 1)
                            normalise_probs(g, 2)
                            maxima(g, pi, 3, par)
                            normalise_keys(pi)
                            out_lo(g, 0)
                            probs_lo(g, 2)
                            normalise_probs(g, 3)
                            rotate(pi, 1, kn[:], nw)
                            probs_lo(g, 3)
                            out_lo(g, 1)
                            qk_lo(pi, 1 - par, 0)
                            qk_lo(pi, 1 - par, 1)
                            v_low(pi, 1 - par)
                            after(dve, "wo_mm", g + 1)
                            dve.tensor_tensor(x[:, t, :], x[:, t, :], ps_s[0][:, 0:D], ALU.add).then_inc(s["xa_done"], 1)
                    split_weights(4 * l + 2, F_COLS)
                    hold(dve, s["tick"], (s["shift_in"], 128 * l + 128))
                    with dve.Fori(0, NCH) as c:
                        ci = l * NCH + c
                        for t in range(CT):
                            dve.bn_stats(st[:, t, 0:6], x[:, c * CT + t, 0:P]).then_inc(s["bn"], 1)
                            dve.bn_stats(st[:, t, 6:12], shifted[:, c * CT + t, :]).then_inc(s["bn"], 1)
                        after(dve, "bn", 2 * CT * (ci + 1))
                        dve.sem_inc(s["tick"], 1)
                        for t in range(CT):
                            dve.bn_aggr(mv[:, t, :], st[:, t, :]).then_inc(s["ag"], 1)
                        after(dve, "ag", CT * (ci + 1))
                        dve.tensor_scalar(nrm[:, 0, :], mv[:, :, 1], EPS, None, ALU.add).then_inc(s["vr"], 1)
                        after(dve, "pw2", ci + 1)
                        dve.scalar_tensor_tensor(nrm[:, 2, :], mv[:, :, 0], -1.0, nrm[:, 1, :], ALU.mult, ALU.mult).then_inc(s["nr"], 1)
                        after(dve, "nr", ci + 1)
                        after(dve, "fT_mm", ci)
                        for t in range(CT):
                            for k, src in enumerate((x[:, c * CT + t, 0:P], shifted[:, c * CT + t, :])):
                                step = dve.tensor_scalar(xn[:, t, k * P:(k + 1) * P], src, nrm[:, 1, t:t + 1], nrm[:, 2, t:t + 1],
                                                         ALU.mult, ALU.add)
                        step.then_inc(s["xnd"], 1)
                        after(dve, "f_hi", ci + 1)
                        dve.tensor_tensor(fT[:, 1], ffull[:], f32(fT[:, 0]), ALU.subtract).then_inc(s["f_lo"], 1)
                        for i in range(HT):
                            n = ci * HT + i
                            after(dve, "gl_done", n + 1)
                            after(dve, "u_lo", n - 1)
                            dve.scalar_tensor_tensor(uf[:, i % 2, :], bank[i % 2][:], b1[:, i:i + 1], gl[:, i % 2, :],
                                                     ALU.add, ALU.mult).then_inc(s["uf_done"], 1)
                            after(dve, "u_hi", n + 1)
                            dve.tensor_tensor(uT[:, 1, i, :], uf[:, i % 2, :], f32(uT[:, 0, i, :]), ALU.subtract).then_inc(s["u_lo"], 1)
                        after(dve, "y_mm", ci + 1)
                        after(dve, "b2_done", ci + 1)
                        for i in range(2):
                            step = dve.tensor_tensor(x[:, ds(c * CT + 2 * i, 2), :], x[:, ds(c * CT + 2 * i, 2), :],
                                                     bank[6 + i][:].rearrange("p (t d) -> p t d", d=D), ALU.add)
                        step.then_inc(s["ya_done"], 1)

            @block.tensor
            def _(pe):
                start(pe, PE_SEMS)
                pe.wait_ge(s["zeroed"], 3)

                def stream_T(l, pi, par):
                    after(pe, "xs_done", pi + l + 1)
                    after(pe, "qkT_lo", 2 * pi - 1)
                    for k in range(KT):
                        step = pe.transpose(ps_misc[:, k * P:(k + 1) * P], xs[:, par, k * P:(k + 1) * P], ident[:])
                    step.then_inc(s["xT_mm"], 1)

                def project(pi, par, i):
                    if i == 0:
                        after(pe, "h_lo", pi + 1)
                        after(pe, "ca_in", pi + 1)
                        after(pe, "ra_done", 6 * pi)
                    if i == 1:
                        after(pe, "kn_done", pi)
                    if i == 2:
                        after(pe, "v_lo", pi)
                    cols = slice(i * INNER, (i + 1) * INNER)
                    for k in range(KT):
                        step = three_products(pe, ps_qkv[i][:], hT[:, par, 0, k, 0:P], hT[:, par, 1, k, 0:P],
                                              wqkv[0][:, k, cols], wqkv[1][:, k, cols], k == 0, k == KT - 1)
                    step.then_inc(s["qkv_mm"], 1)

                def qk_T(pi, i):
                    after(pe, "add_done", 2 * pi + i + 1)
                    if i == 0:
                        after(pe, "h_lo", pi + 1)
                    for j in range(LP):
                        dst = (ps_misc, ps_pt)[i]
                        step = pe.transpose(dst[:, j * P:(j + 1) * P], ra[:, i, j * P:(j + 1) * P], ident[:])
                    step.then_inc(s["qkT_mm"], 1)

                def scores(g, j, par):
                    after(pe, "mx_done", 2 * (4 * g + j))
                    for n, (qx, kx) in enumerate(((0, 0), (0, 1), (1, 0))):
                        for h in range(2):
                            rws = slice(h * DH, (h + 1) * DH)
                            step = pe.matmul(ps_s[h][:, 0:2 * P], qT[rws, par, qx, j, :], kT[rws, kx, j, :], start=(n == 0),
                                             stop=(n == 2), skip_group_check=True)
                    step.then_inc(s["sc_mm"], 1)

                def probs_T(g, j):
                    after(pe, "nm_done", 4 * g + j + 1)
                    after(pe, "pt_lo", 4 * g + j)
                    for slot in range(2):
                        for h in range(2):
                            step = pe.transpose(ps_pt[:, (2 * slot + h) * P:(2 * slot + h + 1) * P],
                                                pr[:, j % 2, h, slot * P:(slot + 1) * P], ident[:])
                    step.then_inc(s["pt_mm"], 1)

                def values(g, j):
                    after(pe, "pt_lo", 4 * g + j + 1)
                    if j == 0:
                        after(pe, "o_lo", 2 * g)
                    if j == 2:
                        after(pe, "o_lo", 2 * g + 1)
                    out = ps_pv[:, (j % 2) * 2 * P:(j % 2 + 1) * 2 * P]
                    cols = slice(j * P, (j + 1) * P)
                    for slot in range(2):
                        step = three_products(pe, out, vv[:, slot, 0, cols], vv[:, slot, 1, cols], pT[:, 0, slot, :],
                                              pT[:, 1, slot, :], slot == 0 and j % 2 == 0, slot == 1)
                    step.then_inc(s["pv_mm"], 1)

                def project_out(g):
                    after(pe, "o_lo", 2 * g + 2)
                    after(pe, "mx_done", 2 * (4 * g + 4))
                    for k in range(LP):
                        step = three_products(pe, ps_s[0][:, 0:D], oT[:, 0, k, :], oT[:, 1, k, :], wo[0][:, k, :], wo[1][:, k, :],
                                              k == 0, k == LP - 1)
                    step.then_inc(s["wo_mm"], 1)

                with pe.Fori(0, L) as l:
                    after(pe, "w_lo_done", 4 * l + 2)
                    after(pe, "ya_done", NCH * l)
                    pi = l * PREPS
                    stream_T(l, pi, 0)
                    for i in range(3):
                        project(pi, 0, i)
                    qk_T(pi, 0)
                    qk_T(pi, 1)
                    with pe.Fori(0, B) as b, pe.Fori(0, TB // 2) as jj:
                        for par in range(2):
                            t, g, pi = tiles_of(l, jj, par, b)
                            nxt = 1 - par
                            after(pe, "qkT_lo", 2 * pi)
                            after(pe, "xa_done", g)
                            scores(g, 0, par)
                            stream_T(l, pi, nxt)
                            project(pi, nxt, 0)
                            scores(g, 1, par)
                            project(pi, nxt, 1)
                            probs_T(g, 0)
                            scores(g, 2, par)
                            after(pe, "v_lo", pi)
                            values(g, 0)
                            probs_T(g, 1)
                            project(pi, nxt, 2)
                            scores(g, 3, par)
                            values(g, 1)
                            probs_T(g, 2)
                            values(g, 2)
                            probs_T(g, 3)
                            values(g, 3)
                            qk_T(pi, 0)
                            qk_T(pi, 1)
                            project_out(g)
                    hold(pe, s["tick"], (s["w_lo_done"], at(4 * l + 4)), (s["qkT_lo"], at(2 * PREPS * (l + 1))),
                         (s["v_lo"], at(PREPS * (l + 1))), (s["xa_done"], at(NT * (l + 1))))
                    with pe.Fori(0, NCH) as c:
                        ci = l * NCH + c
                        after(pe, "xnd", ci + 1)
                        after(pe, "f_hi", ci)
                        for t in range(CT):
                            for k in range(KT):
                                step = pe.transpose(bank[4 + k][:, t * P:(t + 1) * P], xn[:, t, k * P:(k + 1) * P], ident[:])
                        step.then_inc(s["fT_mm"], 1)
                        after(pe, "f_lo", ci + 1)
                        for i in range(HT):
                            n = ci * HT + i
                            after(pe, "uf_done", n - 1)
                            for gate in range(2):
                                cols = slice((gate * HT + i) * P, (gate * HT + i + 1) * P)
                                for k in range(KT):
                                    step = three_products(pe, bank[2 * gate + i % 2][:], w1[0][:, k, cols], w1[1][:, k, cols],
                                                          fT[:, 0, k, :], fT[:, 1, k, :], k == 0, k == KT - 1)
                                step.then_inc(s["gu_mm"], 1)
                        after(pe, "ya_done", ci)
                        for i in range(HT):
                            after(pe, "u_lo", ci * HT + i + 1)
                            for t in range(CT):
                                step = three_products(pe, bank[6 + t // 2][:, (t % 2) * D:(t % 2 + 1) * D],
                                                      uT[:, 0, i, t * P:(t + 1) * P], uT[:, 1, i, t * P:(t + 1) * P],
                                                      w2[0][:, i, :], w2[1][:, i, :], i == 0 and t % 2 == 0, i == HT - 1)
                        step.then_inc(s["y_mm"], 1)



def constants():
    k, q = np.arange(P)[:, None], np.arange(P)[None, :]
    return {
        "ident": np.eye(P, dtype=np.float32),
        "ident16": np.eye(P, dtype=np.float16),
        "causal16": np.where(q >= k, 0.0, -60000.0).astype(np.float16),
        "rope": rope_tables(),
        **local_masks(),
    }


def rope_tables():
    half = np.arange(0, DH, 2, dtype=np.float32)
    inv_freq = np.float32(1.0) / np.float32(10000.0) ** (half / np.float32(DH))
    t = np.arange(S, dtype=np.float32)
    freqs = np.concatenate([t[:, None] * inv_freq[None, :]] * 2, axis=-1)
    base = (half + np.float32(0.4 * DH)) / np.float32(1.4 * DH)
    power = (t - np.float32(S // 2)) / np.float32(P // 2)
    scale = base[None, :] ** power[:, None]
    scale = np.concatenate([scale, scale], axis=-1)
    sign = np.where(np.arange(DH) < DH // 2, -1.0, 1.0).astype(np.float32)
    cos, sin = np.cos(freqs), np.sin(freqs) * sign
    tables = np.stack([cos * scale, sin * scale, cos / scale, sin / scale]).astype(np.float32)
    return np.ascontiguousarray(tables.reshape(4, TB, P, DH).transpose(2, 0, 1, 3).reshape(P, -1))


def local_masks():
    q, k = np.arange(P)[:, None], np.arange(P)[None, :]
    own = np.where(k <= q, 0.0, MASKED).astype(np.float32)
    before = np.where(k >= q, 0.0, MASKED).astype(np.float32)
    none = np.full((P, P), MASKED, np.float32)
    mask = np.stack([np.stack([own, before], axis=1), np.stack([before, own], axis=1)], axis=1)
    return {"mask": mask, "prev_mask": np.stack([none] + [before] * (TB // 2 - 1), axis=1)}


def build(nc, io):
    scr = {
        "hT_hi": nc.dram_tensor("hT_hi", [B, P, KT, S], F32, kind="Internal").ap(),
        "hT_lo": nc.dram_tensor("hT_lo", [B, P, KT, S], F32, kind="Internal").ap(),
        "x1": nc.dram_tensor("x1", [B, S, D], F32, kind="Internal").ap(),
    }
    with ExitStack() as ctx:
        a = Allocator(nc, ctx)
        keep = {
            "ident": a.sb("ident", [P, P]),
            "modT": a.sb("modT", [P, 6, B]),
            "modB": a.sb("modB", [P, B, 3 * D]),
        }
        phase_modulation_and_norm1(nc, io, scr, keep)
        phase_attention(nc, io, scr, keep)
        keep["stream"] = a.sb("stream", [P, NT, D])
        phase_norm2(nc, io, scr, keep)
        phase_layers(nc, io, scr, keep)
        phase_output(nc, io, scr, keep)


def kernel(**inputs):
    import concourse.bacc as _bacc
    from concourse.bass_utils import run_bass_kernel_spmd as _run

    nc = _bacc.Bacc("TRN2", target_bir_lowering=False, num_devices=1)
    arrays = {n.removeprefix("L0_attn_").removeprefix("L0_"): np.ascontiguousarray(v) for n, v in inputs.items()}
    arrays["cT"] = np.ascontiguousarray(arrays.pop("c").T)
    arrays["b_vqk"] = np.stack([arrays.pop(n).reshape(HP, P).T for n in ("bv", "bq", "bk")], axis=1)
    arrays["bo_col"] = np.ascontiguousarray(arrays.pop("bo").reshape(KT, P).T)
    qs, ks = arrays.pop("ffn_q_scale"), arrays.pop("ffn_k_scale")
    arrays["qk_rows"] = np.stack([qs, np.roll(qs, DH // 2, axis=1), ks, np.roll(ks, DH // 2, axis=1)], axis=1)
    arrays["ln_col"] = np.ascontiguousarray(
        np.stack([arrays.pop("ffn_ln_g"), arrays.pop("ffn_ln_b")], axis=1).reshape(L, 2, KT, P).transpose(0, 3, 1, 2))
    w1, w2, b1 = arrays.pop("ffn_w1"), arrays.pop("ffn_w2"), arrays.pop("ffn_b1")
    arrays["w1"] = np.zeros((L, D, 2, HT * P), w1.dtype)
    arrays["w1"][:, :, :, :HID] = w1.reshape(L, D, 2, HID)
    arrays["w2"] = np.zeros((L, HT * P, D), w2.dtype)
    arrays["w2"][:, :HID] = w2
    b1_pad = np.zeros((L, 2, HT * P), b1.dtype)
    b1_pad[:, :, :HID] = b1.reshape(L, 2, HID)
    arrays["b1_col"] = np.ascontiguousarray(b1_pad.reshape(L, 2 * HT, P).transpose(0, 2, 1))
    arrays.update(constants())
    io = {n: nc.dram_tensor("in_" + n, v.shape, mybir.dt.from_np(v.dtype), kind="ExternalInput").ap()
          for n, v in arrays.items()}
    io["out"] = nc.dram_tensor("out", (B, S, D), F32, kind="ExternalOutput").ap()
    build(nc, io)
    r = _run(nc, [{"in_" + n: v for n, v in arrays.items()}], core_ids=[0])
    return r.results[0]["out"]
```

```python
import numpy as np
import concourse.bass as bass
from concourse import mybir
from contextlib import ExitStack

F32 = mybir.dt.float32
F32R = mybir.dt.float32r
F16 = mybir.dt.float16
ALU = mybir.AluOpType
ACT = mybir.ActivationFunctionType
AX = mybir.AxisListType
ds = bass.ds

P = 128
B, S, D = 4, 1024, 256
KT = D // P
NT = B * S // P
TB = S // P
H, DH = 16, 64
HP = H // 2
CH = 512
NC = S // CH
CT = CH // P
EPS = 1e-5
SCORE_SCALE = DH ** -0.5
SCORE_SHIFT = 3.0
VW = 2 * DH + 2
MASKED = -1.0e30
CREDIT = 4


def at(n):
    return n + CREDIT


def hold(eng, tick, *waits):
    for sem, value in waits:
        eng.wait_ge(sem, value)
    eng.sem_inc(tick, 1)


def f32(ap):
    return ap.bitcast(F32)


class Allocator:
    def __init__(self, nc, ctx):
        self.nc, self.ctx = nc, ctx

    def sb(self, name, shape, dt=F32):
        return self.ctx.enter_context(self.nc.sbuf_tensor(name, shape, dt))

    def ps(self, name, shape, dt=F32):
        return self.ctx.enter_context(self.nc.psum_tensor(name, shape, dt))

    def sems(self, prefix, names):
        return [self.ctx.enter_context(self.nc.semaphore(prefix + n)) for n in names.split()]


def three_products(pe, out, w_hi, w_lo, x_hi, x_lo, first, last):
    pe.matmul(out, w_hi, x_hi, start=first, stop=False, skip_group_check=True)
    pe.matmul(out, w_hi, x_lo, start=False, stop=False, skip_group_check=True)
    return pe.matmul(out, w_lo, x_hi, start=False, stop=last, skip_group_check=True)


def variance_steps(dve, chain, n, st, mean2, tmp, var, var_ready):
    dve.tensor_tensor(tmp[:, 0, :], st[:, :, 1], st[:, :, 4], ALU.subtract).then_inc(chain, 1)
    dve.tensor_tensor(tmp[:, 1, :], st[:, :, 2], st[:, :, 5], ALU.add).then_inc(chain, 1)
    dve.tensor_tensor(mean2, st[:, :, 1], st[:, :, 4], ALU.add).then_inc(chain, 1)
    dve.wait_ge(chain, n + 2)
    dve.tensor_tensor(tmp[:, 2, :], tmp[:, 0, :], tmp[:, 0, :], ALU.mult).then_inc(chain, 1)
    dve.tensor_scalar(tmp[:, 3, :], tmp[:, 1, :], 1.0 / D, EPS, ALU.mult, ALU.add).then_inc(chain, 1)
    dve.wait_ge(chain, n + 5)
    dve.scalar_tensor_tensor(var, tmp[:, 2, :], 0.25, tmp[:, 3, :], ALU.mult, ALU.add).then_inc(var_ready, 1)
    return n + 5


def phase_modulation_and_norm1(nc, io, scr, keep):
    with ExitStack() as ctx:
        a = Allocator(nc, ctx)
        x = a.sb("n1_x", [P, NT, D])
        ident, modT, modB = keep["ident"], keep["modT"], keep["modB"]
        cT = a.sb("n1_cT", [P, KT, B])
        silu = a.sb("n1_silu", [P, 4, KT, B])
        silu_rows = a.sb("n1_silu_rows", [P, KT, B, P])
        wmod = a.sb("n1_wmod", [P, KT, 6 * D])
        gate = a.sb("n1_gate", [P, 3, D])
        st = a.sb("n1_stats", [P, NT, 6])
        tmp = a.sb("n1_tmp", [P, 4, NT])
        col = a.sb("n1_columns", [P, 5, NT])
        xn = a.sb("n1_xn", [P, NC, CT, D])
        full = a.sb("n1_full", [P, NC, KT, CH])
        hi = a.sb("n1_hi", [P, NC, KT, CH], F32R)
        lo = a.sb("n1_lo", [P, NC, KT, CH], F32R)
        ps_mod = a.ps("n1_ps_mod", [P, 12, B])
        ps_row = a.ps("n1_ps_row", [P, 2, CH])
        ps_t = [a.ps(f"n1_ps_t{i}", [P, KT, CH]) for i in range(NC)]
        (ld_c, ld_w, ld_i, ld_x, exp_done, silu_done, silu_bc, mod_mm, mod_ev, row_mm, row_ev, bn, chain, var_ready,
         std_ready, norm_ready, xn_ready, t_done, full_done, hi_done, lo_done, tick) = a.sems(
            "n1_", "ld_c ld_w ld_i ld_x exp_done silu_done silu_bc mod_mm mod_ev row_mm row_ev bn chain var_ready "
            "std_ready norm_ready xn_ready t_done full_done hi_done lo_done tick")
        out_hi = a.sems("n1_", "out_hi0 out_hi1")
        out_lo = a.sems("n1_", "out_lo0 out_lo1")
        with nc.Block() as block:

            @block.sync
            def _(sp):
                for s in out_hi + out_lo:
                    sp.sem_inc(s, 16)
                sp.dma_start(cT[:], io["cT"].rearrange("(k p) b -> p k b", p=P)).then_inc(ld_c, 16)
                sp.dma_start(wmod[:], io["wmod"].rearrange("(k p) n -> p k n", p=P)).then_inc(ld_w, 16)
                for b in range(B):
                    sp.dma_start(x[:, b * TB:(b + 1) * TB, :],
                                 io["states"][b].rearrange("(t p) d -> p t d", p=P)).then_inc(ld_x, 16)
                sp.dma_start(ident[:], io["ident"]).then_inc(ld_i, 16)
                with sp.Fori(0, B) as b:
                    for c in range(NC):
                        cols = slice(c * CH, (c + 1) * CH)
                        sp.wait_ge(hi_done, at(b * NC + c + 1))
                        sp.dma_start(scr["hT_hi"][b, :, :, cols], f32(hi[:, c])).then_inc(out_hi[c], 16)
                        sp.wait_ge(lo_done, at(b * NC + c + 1))
                        sp.dma_start(scr["hT_lo"][b, :, :, cols], f32(lo[:, c])).then_inc(out_lo[c], 16)
                for s in out_hi + out_lo:
                    sp.wait_ge(s, 16 * (B + 1))

            @block.scalar
            def _(act):
                act.sem_inc(full_done, CREDIT)
                act.wait_ge(ld_c, 16)
                act.activation(silu[:, 0], cT[:], ACT.Exp, scale=-1.0).then_inc(exp_done, 1)
                act.wait_ge(var_ready, 1)
                act.activation(col[:, 2, :], col[:, 1, :], ACT.Sqrt).then_inc(std_ready, 1)
                act.wait_ge(mod_ev, 2)
                with act.Fori(0, B) as b:
                    for c in range(NC):
                        hold(act, tick, (t_done, b * NC + c + 1), (lo_done, at(b * NC + c - 1)))
                        for k in range(KT):
                            step = act.activation(full[:, c, k, :], ps_t[c][:, k, :], ACT.Identity,
                                                  scale=modT[:, KT + k, ds(b, 1)], bias=modT[:, k, ds(b, 1)])
                        step.then_inc(full_done, 1)

            @block.gpsimd
            def _(pool):
                pool.sem_inc(hi_done, CREDIT)
                with pool.Fori(0, B) as b:
                    for c in range(NC):
                        hold(pool, tick, (full_done, at(b * NC + c + 1)), (out_hi[c], 16 * b + 16))
                        pool.tensor_copy(hi[:, c], full[:, c]).then_inc(hi_done, 1)

            @block.vector
            def _(dve):
                dve.sem_inc(lo_done, CREDIT)
                dve.wait_ge(exp_done, 1)
                dve.tensor_scalar(silu[:, 1], silu[:, 0], 1.0, None, ALU.add).then_inc(silu_done, 1)
                dve.wait_ge(silu_done, 1)
                dve.reciprocal(silu[:, 2], silu[:, 1]).then_inc(silu_done, 1)
                dve.wait_ge(silu_done, 2)
                dve.tensor_tensor(silu[:, 3], silu[:, 2], cT[:], ALU.mult).then_inc(silu_done, 1)
                dve.wait_ge(silu_done, 3)
                for k in range(KT):
                    dve.tensor_copy(silu_rows[:, k], silu[:, 3, k].unsqueeze(2).broadcast_to([P, B, P])).then_inc(silu_bc, 1)
                with dve.Fori(0, B) as b:
                    dve.wait_ge(ld_x, 16 * B)
                    with dve.Fori(0, TB) as t:
                        dve.bn_stats(st[:, b * TB + t, :], x[:, b * TB + t, :]).then_inc(bn, 1)
                dve.wait_ge(bn, NT)
                variance_steps(dve, chain, 0, st, col[:, 0, :], tmp, col[:, 1, :], var_ready)
                dve.wait_ge(mod_mm, 1)
                dve.tensor_copy(modT[:, 0:2, :], ps_mod[:, 0:2, :]).then_inc(mod_ev, 1)
                dve.tensor_scalar(modT[:, 2:4, :], ps_mod[:, 2:4, :], 1.0, None, ALU.add).then_inc(mod_ev, 1)
                dve.tensor_scalar(gate[:, 0, 0:8], ps_mod[:, 4:6, :].rearrange("p a b -> p (a b)"), 0.0, 2.0,
                                  ALU.is_ge, ALU.mult).then_inc(mod_ev, 1)
                dve.tensor_scalar(gate[:, 2, 0:8], ps_mod[:, 4:6, :].rearrange("p a b -> p (a b)"), -1.0, 0.25,
                                  ALU.mult, ALU.max).then_inc(mod_ev, 1)
                dve.wait_ge(mod_ev, 4)
                dve.tensor_tensor(gate[:, 1, 0:8], ps_mod[:, 4:6, :].rearrange("p a b -> p (a b)"), gate[:, 2, 0:8],
                                  ALU.max).then_inc(mod_ev, 1)
                dve.wait_ge(mod_ev, 5)
                dve.scalar_tensor_tensor(modT[:, 4:6, :].rearrange("p a b -> p (a b)"), gate[:, 0, 0:8], -1.0,
                                         gate[:, 1, 0:8], ALU.add, ALU.mult).then_inc(mod_ev, 1)
                dve.wait_ge(std_ready, 1)
                dve.reciprocal(col[:, 3, :], col[:, 2, :]).then_inc(norm_ready, 1)
                dve.wait_ge(norm_ready, 1)
                dve.scalar_tensor_tensor(col[:, 4, :], col[:, 0, :], -0.5, col[:, 3, :], ALU.mult,
                                         ALU.mult).then_inc(norm_ready, 1)
                dve.wait_ge(norm_ready, 2)
                for b in range(B):
                    dve.wait_ge(row_mm, b + 1)
                    dve.tensor_copy(modB[:, b, 0:D], ps_row[:, 0, 0:D]).then_inc(row_ev, 1)
                    dve.tensor_scalar(modB[:, b, D:2 * D], ps_row[:, 0, D:2 * D], 1.0, None, ALU.add).then_inc(row_ev, 1)
                    if b:
                        dve.wait_ge(row_ev, 6 * b)
                    dve.tensor_scalar(gate[:, 0, 0:D], ps_row[:, 1, 0:D], 0.0, 2.0, ALU.is_ge, ALU.mult).then_inc(row_ev, 1)
                    dve.tensor_scalar(gate[:, 2, 0:D], ps_row[:, 1, 0:D], -1.0, 0.25, ALU.mult, ALU.max).then_inc(row_ev, 1)
                    dve.wait_ge(row_ev, 6 * b + 4)
                    dve.tensor_tensor(gate[:, 1, 0:D], ps_row[:, 1, 0:D], gate[:, 2, 0:D], ALU.max).then_inc(row_ev, 1)
                    dve.wait_ge(row_ev, 6 * b + 5)
                    dve.scalar_tensor_tensor(modB[:, b, 2 * D:3 * D], gate[:, 0, 0:D], -1.0, gate[:, 1, 0:D],
                                             ALU.add, ALU.mult).then_inc(row_ev, 1)
                with dve.Fori(0, B) as b:
                    for c in range(NC):
                        dve.wait_ge(full_done, at(b * NC + c - 1))
                        for t in range(CT):
                            n = b * TB + c * CT + t
                            step = dve.tensor_scalar(xn[:, c, t, :], x[:, n, :], col[:, 3, ds(n, 1)], col[:, 4, ds(n, 1)],
                                                     ALU.mult, ALU.add)
                        step.then_inc(xn_ready, 1)
                        dve.wait_ge(hi_done, at(b * NC + c + 1))
                        dve.wait_ge(out_lo[c], 16 * b + 16)
                        dve.tensor_tensor(lo[:, c], full[:, c], f32(hi[:, c]), ALU.subtract).then_inc(lo_done, 1)

            @block.tensor
            def _(pe):
                pe.wait_ge(silu_bc, KT)
                pe.wait_ge(ld_w, 16)
                for m in range(12):
                    for k in range(KT):
                        step = pe.matmul(ps_mod[:, m, :], wmod[:, k, m * P:(m + 1) * P], silu[:, 3, k, :],
                                         start=(k == 0), stop=(k == KT - 1))
                step.then_inc(mod_mm, 1)
                for b in range(B):
                    if b:
                        pe.wait_ge(row_ev, 6 * b)
                    for half in range(2):
                        lo_c = 3 * D + half * CH
                        hi_c = min(lo_c + CH, 6 * D)
                        for k in range(KT):
                            step = pe.matmul(ps_row[:, half, 0:hi_c - lo_c], silu_rows[:, k, b, :], wmod[:, k, lo_c:hi_c],
                                             start=(k == 0), stop=(k == KT - 1))
                    step.then_inc(row_mm, 1)
                pe.wait_ge(ld_i, 16)
                with pe.Fori(0, B) as b:
                    for c in range(NC):
                        pe.wait_ge(xn_ready, b * NC + c + 1)
                        pe.wait_ge(full_done, at(b * NC + c - 1))
                        for t in range(CT):
                            for k in range(KT):
                                step = pe.transpose(ps_t[c][:, k, t * P:(t + 1) * P], xn[:, c, t, k * P:(k + 1) * P], ident[:])
                        step.then_inc(t_done, 1)


UNITS = [(qc, kt) for qc in range(NC) for kt in range((qc + 1) * CT)]
NU = len(UNITS)
LAG = 2
V_, Q_, K_ = range(3)
PROJ = [(w, c) for w in (V_, Q_, K_) for c in range(NC)]
NPJ = len(PROJ)
PROJ_AT = {0: 0, 1: 1, 3: 2, 4: 3, 6: 4, 7: 5}
SPLIT_W_AT = 8
CTX_AT = 9


def phase_attention(nc, io, scr, keep):
    with ExitStack() as ctx:
        a = Allocator(nc, ctx)
        ident, modT = keep["ident"], keep["modT"]
        ident16 = a.sb("at_ident16", [P, P], F16)
        causal = a.sb("at_causal", [P, P], F16)
        bias = a.sb("at_bias", [P, 3, HP])
        bo = a.sb("at_bo", [P, KT])
        shift = a.sb("at_shift", [P, 1])
        hT = a.sb("at_hT", [P, 2, 2, KT, S], F32R)
        w_raw = a.sb("at_w_raw", [P, 3, KT, P])
        w_hi = a.sb("at_w_hi", [P, 3, KT, P], F32R)
        w_lo = a.sb("at_w_lo", [P, 3, KT, P], F32R)
        stage = a.sb("at_stage", [P, 2, CH])
        qk = [[[a.sb(f"at_{n}{i}{part}", [P, S], F16) for part in ("hi", "lo")] for n in "qk"] for i in range(2)]
        vT = [a.sb(f"at_vT_{part}", [P, S], F16) for part in ("hi", "lo")]
        v = [a.sb(f"at_v{i}", [P, TB, 2, VW], F16) for i in range(2)]
        probs = [a.sb(f"at_p{i}", [P, 2, CH]) for i in range(2)]
        p_hi = [a.sb(f"at_p_hi{i}", [P, 2, CH], F16) for i in range(2)]
        p_lo = [a.sb(f"at_p_lo{i}", [P, 2, CH], F16) for i in range(2)]
        rsum = a.sb("at_rsum", [P, 2, CT])
        ctx_tok = a.sb("at_ctx_tok", [P, CT, 2, DH])
        cT_hi = a.sb("at_cT_hi", [P, HP, S], F32R)
        cT_lo = a.sb("at_cT_lo", [P, HP, S], F32R)
        xio = a.sb("at_xio", [P, TB, D])
        wo_hi = a.sb("at_wo_hi", [P, HP, D], F32R)
        wo_lo = a.sb("at_wo_lo", [P, HP, D], F32R)
        y = a.sb("at_y", [P, KT, CH])
        ps_s = [a.ps(f"at_ps_s{i}", [P, 2, CH]) for i in range(2)]
        ps_o = a.ps("at_ps_o", [P, 2, CH])
        ps_m = [a.ps(f"at_ps_m{i}", [P, CH]) for i in range(2)]
        ps_m16 = [m[:].bitcast(F16).rearrange("p (t h d) -> p t h d", t=TB, h=2) for m in ps_m]
        (ld_const, ld_wo, ld_hT, ld_w, ld_x, st_x, const_done, wo_done, sc_done, pv_done, pj_mm, vt_mm, ct_mm, op_mm, yt_mm,
         exp_done, pj_full, vt_hi, ct_hi, y_done, p_hi_done, pj_hi, wh_done, p_lo_done, pj_lo, wl_done, r_done, cx_done,
         vt_lo, ct_lo, yg_done, x1_done, tick) = a.sems(
            "at_", "ld_const ld_wo ld_hT ld_w ld_x st_x const_done wo_done sc_done pv_done pj_mm vt_mm ct_mm op_mm yt_mm "
            "exp_done pj_full vt_hi ct_hi y_done p_hi_done pj_hi wh_done p_lo_done pj_lo wl_done r_done cx_done "
            "vt_lo ct_lo yg_done x1_done tick")
        w_dram = [io[n].rearrange("(k p) n -> p k n", p=P) for n in ("Wv", "Wq", "Wk")]
        NPAIR = B * HP

        def o_view():
            return ps_o[:, :, 0:CT * (DH + 1)].rearrange("p h (t c) -> p h t c", c=DH + 1)

        with nc.Block() as block:

            @block.sync
            def _(sp):
                sp.dma_start(ident16[:], io["ident16"]).then_inc(ld_const, 16)
                sp.dma_start(causal[:], io["causal16"]).then_inc(ld_const, 16)
                sp.dma_start(bias[:], io["b_vqk"]).then_inc(ld_const, 16)
                sp.dma_start(bo[:], io["bo_col"]).then_inc(ld_const, 16)

                def load_hT(b):
                    for part, name in enumerate(("hT_hi", "hT_lo")):
                        sp.dma_start(f32(hT[:, b % 2, part]), scr[name][b % B]).then_inc(ld_hT, 16)

                def load_w(n):
                    for i in range(3):
                        sp.dma_start(w_raw[:, i], w_dram[i][:, :, ds((n % HP) * P, P)]).then_inc(ld_w, 16)

                load_w(0)
                load_hT(0)
                sp.wait_ge(wh_done, at(1))
                sp.wait_ge(wl_done, at(1))
                load_w(1)
                sp.dma_start(xio[:], io["Wo"].rearrange("(h p) n -> p h n", p=P)).then_inc(ld_wo, 16)
                sp.wait_ge(wo_done, 2)
                with sp.Fori(0, B) as b:
                    hold(sp, tick, (pj_mm, at(NPJ * HP * b)))
                    load_hT(b + 1)
                    sp.dma_start(xio[:], io["states"][b].rearrange("(t p) d -> p t d", p=P)).then_inc(ld_x, 16)
                    with sp.Fori(0, HP) as j:
                        hold(sp, tick, (wh_done, at(b * HP + j + 2)), (wl_done, at(b * HP + j + 2)))
                        load_w(b * HP + j + 2)
                    hold(sp, tick, (x1_done, at(NC * (b + 1))))
                    sp.dma_start(scr["x1"][b].rearrange("(t p) d -> p t d", p=P), xio[:]).then_inc(st_x, 16)
                    hold(sp, tick, (st_x, 16 * b + 16))

            @block.gpsimd
            def _(pool):
                for s in (pj_lo, wh_done):
                    pool.sem_inc(s, CREDIT)
                pool.memset(shift[:], SCORE_SHIFT).then_inc(const_done, 1)
                for i in range(2):
                    pool.memset(v[i][:, :, :, DH:DH + 2], 1.0).then_inc(const_done, 1)

                def split_weights(n):
                    hold(pool, tick, (ld_w, 48 * n + 48))
                    pool.tensor_copy(w_hi[:], w_raw[:]).then_inc(wh_done, 1)

                def split_projection(base, i, dst):
                    w, c = PROJ[i]
                    cols = slice(c * CH, (c + 1) * CH)
                    hi, lo = vT if w == V_ else qk[dst][w - 1]
                    hold(pool, tick, (pj_hi, at(base + i + 1)))
                    pool.tensor_tensor(lo[:, cols], stage[:, i % 2, :], hi[:, cols], ALU.subtract).then_inc(pj_lo, 1)

                split_weights(0)
                for i in range(NPJ):
                    split_projection(0, i, 0)
                pool.wait_ge(pj_mm, at(NPJ))
                split_weights(1)
                hold(pool, tick, (ld_wo, 16))
                pool.tensor_copy(wo_hi[:], xio[:]).then_inc(wo_done, 1)
                with pool.Fori(0, B) as b, pool.Fori(0, HP // 2) as j:
                    for par in range(2):
                        it = b * HP + j * 2 + par
                        for i in range(NPJ):
                            split_projection(NPJ * (it + 1), i, 1 - par)
                        pool.wait_ge(pj_mm, at(NPJ * (it + 2)))
                        split_weights(it + 2)

            @block.vector
            def _(dve):
                for s in (p_hi_done, p_lo_done, wl_done, r_done, cx_done, vt_lo, ct_lo, yg_done, x1_done):
                    dve.sem_inc(s, CREDIT)

                def split_weights(n):
                    dve.wait_ge(wh_done, at(n + 1))
                    dve.tensor_tensor(w_lo[:], w_raw[:], f32(w_hi[:]), ALU.subtract).then_inc(wl_done, 1)

                def low_values(n, dst):
                    dve.wait_ge(vt_mm, 2 * n + 2)
                    dve.tensor_copy(v[dst][:, :, :, DH + 2:VW], ps_m16[0]).then_inc(vt_lo, 1)

                def normalise(n, count):
                    dve.wait_ge(pv_done, at(count))
                    dve.reciprocal(rsum[:], o_view()[:, :, :, DH]).then_inc(r_done, 1)
                    dve.wait_ge(r_done, at(n + 1))
                    dve.tensor_tensor(ctx_tok[:].rearrange("p t h d -> p h t d"), o_view()[:, :, :, 0:DH],
                                      rsum[:].unsqueeze(3).broadcast_to([P, 2, CT, DH]), ALU.mult).then_inc(cx_done, 1)

                def low_context(n, hp, c):
                    dve.wait_ge(ct_hi, at(n + 1))
                    cols = slice(c * CH, (c + 1) * CH)
                    dve.tensor_tensor(cT_lo[:, hp, cols], ps_m[c][:], f32(cT_hi[:, hp, cols]), ALU.subtract).then_inc(ct_lo, 1)

                split_weights(0)
                dve.wait_ge(pj_mm, at(NPJ))
                split_weights(1)
                dve.wait_ge(const_done, 3)
                low_values(0, 0)
                dve.wait_ge(wo_done, 1)
                dve.tensor_tensor(wo_lo[:], xio[:], f32(wo_hi[:]), ALU.subtract).then_inc(wo_done, 1)
                with dve.Fori(0, B) as b:
                    with dve.Fori(0, HP // 2) as j:
                        for par in range(2):
                            hp = j * 2 + par
                            it = b * HP + hp
                            for u, (qc, kt) in enumerate(UNITS):
                                off = max(0, kt * P - qc * CH)
                                dve.wait_ge(exp_done, at(it * NU + u + 1))
                                dve.wait_ge(pv_done, at(it * NU + u - 1))
                                dve.tensor_copy(p_hi[u % 2][:, :, off:], probs[u % 2][:, :, off:]).then_inc(p_hi_done, 1)
                                dve.wait_ge(p_hi_done, at(it * NU + u + 1))
                                dve.tensor_tensor(p_lo[u % 2][:, :, off:], probs[u % 2][:, :, off:],
                                                  p_hi[u % 2][:, :, off:], ALU.subtract).then_inc(p_lo_done, 1)
                                if u == CT - 1 + LAG:
                                    normalise(it * NC, it * NU + CT)
                                if u == SPLIT_W_AT:
                                    split_weights(it + 2)
                                if u == CTX_AT:
                                    low_context(it * NC, hp, 0)
                            normalise(it * NC + 1, it * NU + NU)
                            low_values(it + 1, 1 - par)
                            low_context(it * NC + 1, hp, 1)
                    for c in range(NC):
                        for m in range(KT):
                            dve.wait_ge(y_done, at(b * NC * KT + c * KT + m + 1))
                            dve.tensor_scalar(y[:, m, :], y[:, m, :], modT[:, 2 * KT + m, ds(b, 1)], None,
                                              ALU.mult).then_inc(yg_done, 1)
                        if c == 0:
                            dve.wait_ge(ld_x, 16 * b + 16)
                        dve.wait_ge(yt_mm, at(b * NC + c + 1))
                        tiles = slice(c * CT, (c + 1) * CT)
                        dve.tensor_tensor(xio[:, tiles, :], xio[:, tiles, :],
                                          ps_o[:].rearrange("p h (t d) -> p (h t) d", d=D), ALU.add).then_inc(x1_done, 1)

            @block.scalar
            def _(act):
                for s in (exp_done, pj_full, pj_hi, vt_hi, ct_hi, y_done):
                    act.sem_inc(s, CREDIT)

                def project(base, i, hp, dst):
                    w, c = PROJ[i]
                    hold(act, tick, (pj_mm, at(base + i + 1)), (pj_lo, at(base + i - 1)))
                    act.activation(stage[:, i % 2, :], ps_m[i % 2][:], ACT.Tanh, bias=bias[:, w, ds(hp, 1)]).then_inc(pj_full, 1)
                    hi = vT[0] if w == V_ else qk[dst][w - 1][0]
                    act.activation(hi[:, c * CH:(c + 1) * CH], ps_m[i % 2][:], ACT.Tanh,
                                   bias=bias[:, w, ds(hp, 1)]).then_inc(pj_hi, 1)

                def high_values(n, dst):
                    act.wait_ge(vt_mm, 2 * n + 1)
                    act.activation(v[dst][:, :, :, 0:DH], ps_m16[1], ACT.Copy).then_inc(vt_hi, 1)

                def high_context(n, hp, c):
                    hold(act, tick, (ct_mm, n + 1))
                    act.activation(cT_hi[:, hp, c * CH:(c + 1) * CH], ps_m[c][:], ACT.Copy).then_inc(ct_hi, 1)

                act.wait_ge(ld_const, 16 * 4)
                for i in range(NPJ):
                    project(0, i, 0, 0)
                act.wait_ge(const_done, 3)
                high_values(0, 0)
                with act.Fori(0, B) as b:
                    with act.Fori(0, HP // 2) as j:
                        for par in range(2):
                            hp = j * 2 + par
                            it = b * HP + hp
                            for u, (qc, kt) in enumerate(UNITS):
                                off = max(0, kt * P - qc * CH)
                                act.wait_ge(sc_done, it * NU + u + 1)
                                act.wait_ge(p_lo_done, at(it * NU + u - 1))
                                act.activation(probs[u % 2][:, :, off:], ps_s[u % 2][:, :, off:], ACT.Exp,
                                               bias=shift[:], scale=SCORE_SCALE).then_inc(exp_done, 1)
                                if u in PROJ_AT:
                                    project(NPJ * (it + 1), PROJ_AT[u], (hp + 1) % HP, 1 - par)
                                if u == CTX_AT:
                                    high_context(it * NC, hp, 0)
                            high_values(it + 1, 1 - par)
                            high_context(it * NC + 1, hp, 1)
                    for c in range(NC):
                        for m in range(KT):
                            act.wait_ge(op_mm, b * NC * KT + c * KT + m + 1)
                            if m == 0:
                                act.wait_ge(yt_mm, at(b * NC + c))
                            act.activation(y[:, m, :], ps_s[c][:, m, :], ACT.Tanh, bias=bo[:, m:m + 1]).then_inc(y_done, 1)

            @block.tensor
            def _(pe):
                for s in (pv_done, pj_mm, yt_mm):
                    pe.sem_inc(s, CREDIT)

                def project(i, buf):
                    w, c = PROJ[i]
                    cols = slice(c * CH, (c + 1) * CH)
                    for k in range(KT):
                        step = three_products(pe, ps_m[i % 2][:], w_hi[:, w, k, :], w_lo[:, w, k, :],
                                              hT[:, buf, 0, k, cols], hT[:, buf, 1, k, cols], k == 0, k == KT - 1)
                    step.then_inc(pj_mm, 1)

                def values(part, base):
                    pe.wait_ge(pj_lo if part else pj_hi, at(base + NC))
                    for t in range(TB):
                        step = pe.transpose(ps_m16[1 - part][:, t, :, :].rearrange("p h d -> p (h d)"),
                                            vT[part][:, t * P:(t + 1) * P], ident16[:])
                    step.then_inc(vt_mm, 1)

                def scores(par, u):
                    qc, kt = UNITS[u]
                    off = max(0, kt * P - qc * CH)
                    cols = slice(qc * CH + off, (qc + 1) * CH)
                    diagonal = kt * P >= qc * CH
                    (q_hi, q_lo), (k_hi, k_lo) = qk[par]
                    keys = slice(kt * P, (kt + 1) * P)
                    pairs = [(k_hi, q_hi), (k_hi, q_lo), (k_lo, q_hi)]
                    for n, (kx, qx) in enumerate(pairs):
                        for h in range(2):
                            rows = slice(h * DH, (h + 1) * DH)
                            step = pe.matmul(ps_s[u % 2][:, h, off:], kx[rows, keys], qx[rows, cols], start=(n == 0),
                                             stop=(n == 2 and not diagonal), skip_group_check=True)
                    if diagonal:
                        for h in range(2):
                            step = pe.matmul(ps_s[u % 2][:, h, off:off + P], ident16[:], causal[:], start=False, stop=True,
                                             skip_group_check=True)
                    step.then_inc(sc_done, 1)

                def value_products(par, u):
                    qc, kt = UNITS[u]
                    first = max(0, kt - qc * CT)
                    for h in range(2):
                        ones_hi, lo = v[par][:, kt, h, 0:DH + 1], v[par][:, kt, h, DH + 2:VW]
                        for t in range(first, CT):
                            ph, pl = (p[u % 2][:, h, t * P:(t + 1) * P] for p in (p_hi, p_lo))
                            out = ps_o[:, h, t * (DH + 1):(t + 1) * (DH + 1)]
                            pe.matmul(out, ph, ones_hi, start=(kt == 0 and t == 0), stop=False, skip_group_check=True)
                            pe.matmul(out[:, 0:DH], ph, lo, start=False, stop=False, skip_group_check=True)
                            step = pe.matmul(out, pl, ones_hi, start=False, stop=(kt == qc * CT + t), skip_group_check=True)
                    step.then_inc(pv_done, 1)

                def context(n, c):
                    pe.wait_ge(cx_done, at(n + 1))
                    for t in range(CT):
                        step = pe.transpose(ps_m[c][:, t * P:(t + 1) * P], ctx_tok[:, t].rearrange("p h d -> p (h d)"),
                                            ident[:])
                    step.then_inc(ct_mm, 1)

                pe.wait_ge(ld_hT, 32)
                pe.wait_ge(wl_done, at(1))
                for i in range(NPJ):
                    if i >= 2:
                        pe.wait_ge(pj_hi, at(i - 1))
                    project(i, 0)
                pe.wait_ge(ld_const, 16 * 4)
                pe.wait_ge(pj_hi, at(NPJ))
                values(0, 0)
                values(1, 0)
                with pe.Fori(0, B) as b:
                    with pe.Fori(0, HP // 2) as j:
                        for par in range(2):
                            it = b * HP + j * 2 + par
                            nxt = it + 1
                            buf = (nxt // HP) % 2
                            base = NPJ * nxt
                            for s in range(NU + LAG):
                                if s < NU:
                                    if s == 0:
                                        pe.wait_ge(pj_lo, at(base))
                                        pe.wait_ge(y_done, at(b * NC * KT))
                                    pe.wait_ge(exp_done, at(it * NU + s - 1))
                                    scores(par, s)
                                if s in PROJ_AT:
                                    i = PROJ_AT[s]
                                    if i == 0:
                                        pe.wait_ge(ld_hT, 32 * (nxt // HP) + 32)
                                        pe.wait_ge(wl_done, at(nxt + 1))
                                        pe.wait_ge(vt_lo, at(it + 1))
                                    elif i == 1:
                                        pe.wait_ge(vt_hi, at(it + 1))
                                        pe.wait_ge(ct_lo, at(NC * it))
                                    else:
                                        pe.wait_ge(pj_hi, at(base + i - 1))
                                    project(i, buf)
                                if s == CTX_AT:
                                    pe.wait_ge(pj_hi, at(base + 5))
                                    context(it * NC, 0)
                                if s >= LAG:
                                    u = s - LAG
                                    if u == 0:
                                        pe.wait_ge(vt_hi, at(it + 1))
                                        pe.wait_ge(vt_lo, at(it + 1))
                                        pe.wait_ge(cx_done, at(it * NC))
                                        pe.wait_ge(x1_done, at(b * NC))
                                    if u == CT:
                                        pe.wait_ge(cx_done, at(it * NC + 1))
                                    pe.wait_ge(p_lo_done, at(it * NU + u + 1))
                                    value_products(par, u)
                            pe.wait_ge(pj_hi, at(base + NPJ))
                            values(0, base)
                            pe.wait_ge(ct_lo, at(it * NC + 1))
                            values(1, base)
                            pe.wait_ge(vt_hi, at(it + 2))
                            context(it * NC + 1, 1)
                    pe.wait_ge(exp_done, at((b + 1) * HP * NU))
                    pe.wait_ge(wo_done, 2)
                    for c in range(NC):
                        pe.wait_ge(ct_lo, at((b + 1) * HP * NC - 1 + c))
                        for m in range(KT):
                            outs = slice(m * P, (m + 1) * P)
                            for hp in range(HP):
                                step = three_products(pe, ps_s[c][:, m, :], wo_hi[:, hp, outs], wo_lo[:, hp, outs],
                                                      cT_hi[:, hp, c * CH:(c + 1) * CH], cT_lo[:, hp, c * CH:(c + 1) * CH],
                                                      hp == 0, hp == HP - 1)
                            step.then_inc(op_mm, 1)
                    for c in range(NC):
                        pe.wait_ge(yg_done, at(b * NC * KT + (c + 1) * KT))
                        if c == 0:
                            pe.wait_ge(cx_done, at((b + 1) * HP * NC))
                        else:
                            pe.wait_ge(x1_done, at(b * NC + 1))
                        for t in range(CT):
                            for m in range(KT):
                                step = pe.transpose(ps_o[:, t // 2, (t % 2) * D + m * P:(t % 2) * D + (m + 1) * P],
                                                    y[:, m, t * P:(t + 1) * P], ident[:])
                        step.then_inc(yt_mm, 1)


def phase_norm2(nc, io, scr, keep):
    with ExitStack() as ctx:
        a = Allocator(nc, ctx)
        h, modB = keep["stream"], keep["modB"]
        st = a.sb("n2_stats", [P, NT, 6])
        tmp = a.sb("n2_tmp", [P, 4, NT])
        col = a.sb("n2_columns", [P, 5, NT])
        (ld_x, bn, chain, var_ready, std_ready, norm_ready, xn_done, scaled) = a.sems(
            "n2_", "ld_x bn chain var_ready std_ready norm_ready xn_done scaled")
        with nc.Block() as block:

            @block.sync
            def _(sp):
                for b in range(B):
                    sp.dma_start(h[:, b * TB:(b + 1) * TB, :],
                                 scr["x1"][b].rearrange("(t p) d -> p t d", p=P)).then_inc(ld_x, 16)

            @block.scalar
            def _(act):
                act.wait_ge(var_ready, 1)
                act.activation(col[:, 2, :], col[:, 1, :], ACT.Sqrt).then_inc(std_ready, 1)

            @block.vector
            def _(dve):
                dve.wait_ge(ld_x, 16 * B)
                with dve.Fori(0, NT) as t:
                    dve.bn_stats(st[:, t, :], h[:, t, :]).then_inc(bn, 1)
                dve.wait_ge(bn, NT)
                variance_steps(dve, chain, 0, st, col[:, 0, :], tmp, col[:, 1, :], var_ready)
                dve.wait_ge(std_ready, 1)
                dve.reciprocal(col[:, 3, :], col[:, 2, :]).then_inc(norm_ready, 1)
                dve.wait_ge(norm_ready, 1)
                dve.scalar_tensor_tensor(col[:, 4, :], col[:, 0, :], -0.5, col[:, 3, :], ALU.mult,
                                         ALU.mult).then_inc(norm_ready, 1)
                dve.wait_ge(norm_ready, 2)
                with dve.Fori(0, NT) as t:
                    dve.tensor_scalar(h[:, t, :], h[:, t, :], col[:, 3, ds(t, 1)], col[:, 4, ds(t, 1)],
                                      ALU.mult, ALU.add).then_inc(xn_done, 1)
                dve.wait_ge(xn_done, NT)
                for b in range(B):
                    part = h[:, b * TB:(b + 1) * TB, :]
                    rows = [modB[:, b, i * D:(i + 1) * D].unsqueeze(1).broadcast_to([P, TB, D]) for i in range(2)]
                    dve.tensor_tensor(part, part, rows[1], ALU.mult).then_inc(scaled, 1)
                    dve.wait_ge(scaled, 2 * b + 1)
                    dve.tensor_tensor(part, part, rows[0], ALU.add).then_inc(scaled, 1)


def phase_output(nc, io, scr, keep):
    with ExitStack() as ctx:
        a = Allocator(nc, ctx)
        h, modB = keep["stream"], keep["modB"]
        x1 = a.sb("out_x1", [P, NT, D])
        ld, gated, added, stored = a.sems("out_", "ld gated added stored")
        with nc.Block() as block:

            @block.sync
            def _(sp):
                for b in range(B):
                    sp.dma_start(x1[:, b * TB:(b + 1) * TB, :],
                                 scr["x1"][b].rearrange("(t p) d -> p t d", p=P)).then_inc(ld, 16)
                for b in range(B):
                    sp.wait_ge(added, b + 1)
                    sp.dma_start(io["out"][b].rearrange("(t p) d -> p t d", p=P),
                                 h[:, b * TB:(b + 1) * TB, :]).then_inc(stored, 16)
                sp.wait_ge(stored, 16 * B)

            @block.vector
            def _(dve):
                for b in range(B):
                    part = h[:, b * TB:(b + 1) * TB, :]
                    gb = modB[:, b, 2 * D:3 * D].unsqueeze(1).broadcast_to([P, TB, D])
                    dve.tensor_tensor(part, part, gb, ALU.mult).then_inc(gated, 1)
                    dve.wait_ge(gated, b + 1)
                    if b == 0:
                        dve.wait_ge(ld, 16 * B)
                    dve.tensor_tensor(part, part, x1[:, b * TB:(b + 1) * TB, :], ALU.add).then_inc(added, 1)


L = 2
LH = 8
LP = LH // 2
INNER = LH * DH
HID = D * 4 * 2 // 3
HT = -(-HID // P)
QK_SCALE = 8.0
NORM_FLOOR = 1e-12
NCH = NT // CT
V_RING = 4


def phase_layers(nc, io, scr, keep):
    with ExitStack() as ctx:
        a = Allocator(nc, ctx)
        x, ident = keep["stream"], keep["ident"]
        raw = a.sb("ly_raw", [P, 6144])
        w_hi = a.sb("ly_w_hi", [P, 4608], F32R)
        w_lo = a.sb("ly_w_lo", [P, 4608], F32R)
        opnd = a.sb("ly_operands", [P, 9232], F32R)
        rope = a.sb("ly_rope", [P, 4, TB, DH])
        rows = a.sb("ly_rows", [P, 4, DH])
        lncol = a.sb("ly_ln", [P, 2, KT])
        b1 = a.sb("ly_b1", [P, 2 * HT])
        b2 = a.sb("ly_b2", [P, D])
        prev_mask = a.sb("ly_prev_mask", [P, TB // 2, P])
        mask = a.sb("ly_mask", [P, 2, 2, P])
        carry = a.sb("ly_carry", [P, 2, TB + 1], F32R)
        shifted = a.sb("ly_shifted", [P, NT, P])
        expo = a.sb("ly_expo", [P, LH])
        sq = a.sb("ly_sq", [P, 2, INNER])
        norm2 = a.sb("ly_norm2", [P, 2, 2, LH])
        rq = a.sb("ly_rq", [P, 2, LH])
        rk = a.sb("ly_rk", [P, LH])
        kn = a.sb("ly_kn", [P, INNER])
        xs = a.sb("ly_xs", [P, 2, D])
        ra = a.sb("ly_rope_a", [P, 2, INNER])
        rt = a.sb("ly_rope_t", [P, 2, INNER])
        sm = a.sb("ly_masked", [P, 2, 2, 2 * P])
        pr = a.sb("ly_probs", [P, 2, 2, 2 * P])
        small = a.sb("ly_small", [P, 2, 2, 2])
        sums = a.sb("ly_sums", [P, 2, LH])
        rsum = a.sb("ly_rsum", [P, LH])
        vv = a.sb("ly_values", [P, V_RING, INNER])
        pT = a.sb("ly_probs_T", [P, 4 * P])
        on = a.sb("ly_on", [P, INNER])
        def cut(start, *shape):
            n = int(np.prod(shape))
            names = "abcd"[:len(shape)]
            v = opnd[:, start:start + n]
            if len(shape) > 1:
                v = v.rearrange(f"p ({' '.join(names)}) -> p {' '.join(names)}", **dict(zip(names, shape)))
            return v, start + n
        hT, o = cut(0, 2, 2, KT, P + 1)
        qT, o = cut(o + o % 2, 2, 2, LP, P)
        kT, o = cut(o, 2, LP, 2 * P)
        oT, o = cut(o, 2, LP, P)
        assert o <= 9232
        fT, o = cut(0, 2, KT, CH)
        uT, o = cut(o, 2, HT, CH)
        assert o <= 9232
        st = a.sb("ly_st", [P, CT, 12])
        mv = a.sb("ly_mv", [P, CT, 2])
        nrm = a.sb("ly_nrm", [P, 3, CT])
        xn = sq[:].rearrange("p a (b d) -> p (a b) d", d=D)
        ffull = ra
        gl = pr[:].rearrange("p a b c -> p a (b c)")
        uf = rt
        bank = [a.ps(f"ly_ps{i}", [P, CH]) for i in range(8)]
        ps_qkv, ps_s, ps_pt, ps_misc, ps_pv = bank[0:3], bank[3:5], bank[5], bank[6], bank[7]
        wqkv = [w[:, 0:KT * 3 * INNER].rearrange("p (k n) -> p k n", k=KT) for w in (w_hi, w_lo)]
        wo = [w[:, KT * 3 * INNER:KT * 3 * INNER + LP * D].rearrange("p (k n) -> p k n", k=LP) for w in (w_hi, w_lo)]
        w1 = [w[:, 0:KT * 2 * HT * P].rearrange("p (k n) -> p k n", k=KT) for w in (w_hi, w_lo)]
        w2 = [w[:, KT * 2 * HT * P:KT * 2 * HT * P + HT * D].rearrange("p (k n) -> p k n", k=HT) for w in (w_hi, w_lo)]
        A_COLS, F_COLS = KT * 3 * INNER + LP * D, KT * 2 * HT * P + HT * D
        T_COLS = 4 * TB * DH
        qkv_cols = slice(0, KT * 3 * INNER)
        names = ("ld_const ld_attn ld_ffn shift_in const_done zeroed "
                 "w_hi_done w_lo_done rope_q "
                 "xT_mm qkv_mm sc_mm pt_mm pv_mm qkT_mm oT_mm wo_mm "
                 "h_hi ex_done sq_done pt_done o_hi qkT_hi v_done "
                 "mx_done nb_done h_lo rc_done on_done red_done fl_done ra_done kn_done o_lo qkT_lo xa_done msk "
                 "ca_in ca_out pw_done add_done xs_done "
                 "bn ag vr nr xnd fT_mm ff_done f_hi f_lo gu_mm gl_done uf_done u_hi u_lo y_mm ya_done pw2 b2_done tick")
        s = dict(zip(names.split(), a.sems("ly_", names)))
        PE_SEMS = "xT_mm qkv_mm sc_mm pt_mm pv_mm qkT_mm oT_mm wo_mm fT_mm gu_mm y_mm"
        ACT_SEMS = "h_hi ex_done sq_done pt_done o_hi qkT_hi v_done w_hi_done ff_done f_hi gl_done"
        DVE_SEMS = ("mx_done nb_done h_lo rc_done on_done red_done fl_done ra_done kn_done o_lo qkT_lo xa_done msk "
                    "w_lo_done rope_q bn ag vr nr xnd f_lo uf_done u_lo ya_done")
        POOL_SEMS = "xs_done ca_in ca_out pw_done add_done u_hi pw2 b2_done"

        def start(eng, which):
            for n in which.split():
                eng.sem_inc(s[n], CREDIT)

        def after(eng, name, n):
            eng.wait_ge(s[name], at(n))

        def nth(l, t):
            return l * NT + t

        def nth_rotated(l, t):
            return l * (NT + 1) + t

        def nth_projected(l, t):
            return l * (NT + 2) + t

        def nth_transposed(l, t):
            return l * (NT + 3) + t

        def nth_staged(l, t):
            return l * (NT + 4) + t

        def nth_scores(l, t, j):
            return l * (LP * NT + 1) + LP * t + j

        def nth_norm(l, c):
            return l * (NCH + 1) + c

        with nc.Block() as block:

            @block.sync
            def _(sp):
                sp.dma_start(prev_mask[:], io["prev_mask"]).then_inc(s["ld_const"], 16)
                sp.dma_start(mask[:], io["mask"]).then_inc(s["ld_const"], 16)
                with sp.Fori(0, L) as l:
                    hold(sp, s["tick"], (s["w_lo_done"], at(4 * l)))
                    hold(sp, s["tick"], (s["rope_q"], at(4 * l)))
                    sp.dma_start(raw[:, qkv_cols].rearrange("p (k n) -> p k n", k=KT),
                                 io["ffn_wqkv"][l].rearrange("(k p) n -> p k n", p=P)).then_inc(s["ld_attn"], 16)
                    sp.dma_start(raw[:, KT * 3 * INNER:A_COLS].rearrange("p (k n) -> p k n", k=LP),
                                 io["ffn_wo"][l].rearrange("(k p) n -> p k n", p=P)).then_inc(s["ld_attn"], 16)
                    sp.dma_start(raw[:, A_COLS:A_COLS + T_COLS], io["rope"]).then_inc(s["ld_attn"], 16)
                    sp.dma_start(rows[:], io["qk_rows"][l].partition_broadcast(P)).then_inc(s["ld_attn"], 16)
                    hold(sp, s["tick"], (s["ya_done"], at(NCH * l)))
                    hold(sp, s["tick"], (s["w_lo_done"], at(4 * l + 2)))
                    hold(sp, s["tick"], (s["rope_q"], at(4 * l + 4)))
                    sp.dma_start(raw[:, 0:KT * 2 * HT * P].rearrange("p (k n) -> p k n", k=KT),
                                 io["w1"][l].rearrange("(k p) a n -> p k (a n)", p=P)).then_inc(s["ld_ffn"], 16)
                    sp.dma_start(raw[:, KT * 2 * HT * P:F_COLS].rearrange("p (k n) -> p k n", k=HT),
                                 io["w2"][l].rearrange("(k p) n -> p k n", p=P)).then_inc(s["ld_ffn"], 16)
                    sp.dma_start(lncol[:], io["ln_col"][l]).then_inc(s["ld_ffn"], 16)
                    sp.dma_start(b1[:], io["b1_col"][l]).then_inc(s["ld_ffn"], 16)
                    sp.dma_start(b2[:], io["ffn_b2"][l].partition_broadcast(P)).then_inc(s["ld_ffn"], 16)
                    with sp.Fori(0, B) as b:
                        hold(sp, s["tick"], (s["xa_done"], at(l * NT + b * TB + TB)))
                        sp.dma_start(shifted[1:P, ds(b * TB, TB), :], x[0:P - 1, ds(b * TB, TB), P:D]).then_inc(s["shift_in"], 16)
                        sp.dma_start(shifted[0:1, ds(b * TB + 1, TB - 1), :],
                                     x[P - 1:P, ds(b * TB, TB - 1), P:D]).then_inc(s["shift_in"], 16)

            @block.gpsimd
            def _(pool):
                start(pool, POOL_SEMS)
                pool.memset(expo[:], -0.5).then_inc(s["const_done"], 1)
                pool.memset(shifted[:], 0.0).then_inc(s["zeroed"], 1)
                pool.memset(f32(opnd[:]), 0.0).then_inc(s["zeroed"], 1)
                pool.memset(f32(carry[:]), 0.0).then_inc(s["zeroed"], 1)
                pool.memset(vv[:], 0.0).then_inc(s["zeroed"], 1)
                pool.wait_ge(s["const_done"], 1)
                pool.wait_ge(s["zeroed"], 4)

                def carry_over(l, t, par, w):
                    n = nth_transposed(l, t)
                    hold(pool, s["tick"], (s["qkv_mm"], at(3 * nth_projected(l, t) - 3)), (s["ca_out"], at(n)))
                    pool.tensor_copy(hT[:, par, :, 1, 0], f32(carry[:, :, ds(w, 1)]).rearrange("p a b -> p (a b)")).then_inc(s["ca_in"], 1)
                    hold(pool, s["tick"], (s["h_lo"], at(n + 1)))
                    pool.tensor_copy(carry[:, :, ds(w + 1, 1)].rearrange("p a b -> p (a b)"), f32(hT[:, par, :, 1, P])).then_inc(s["ca_out"], 1)

                def stage_tile(par, tile):
                    pool.tensor_copy(xs[:, par, :], x[:, tile, :]).then_inc(s["xs_done"], 1)

                def inverse_norms(l, t, par, extra=0):
                    n = nth_rotated(l, t)
                    hold(pool, s["tick"], (s["fl_done"], at(2 * nth_projected(l, t) + 2)), (s["kn_done"], at(n)),
                         (s["ex_done"], at(LP * (nth(l, t) - 1) + extra)))
                    pool.tensor_tensor(rk[:], norm2[:, 1, 1, :], expo[:], ALU.pow).then_inc(s["pw_done"], 1)
                    pool.tensor_tensor(rq[:, par, :], norm2[:, 0, 1, :], expo[:], ALU.pow).then_inc(s["pw_done"], 1)

                def add_rotated(l, t, i):
                    hold(pool, s["tick"], (s["ra_done"], at(6 * nth_rotated(l, t) + 3 * i + 3)))
                    pool.tensor_tensor(ra[:, i, :], ra[:, i, :], rt[:, i, :], ALU.add).then_inc(s["add_done"], 1)

                def inverse_deviation(l, c):
                    n = nth_norm(l, c)
                    hold(pool, s["tick"], (s["vr"], at(n + 1)), (s["nr"], at(n)))
                    pool.tensor_tensor(nrm[:, 1, :], nrm[:, 0, :], expo[:, 0:CT], ALU.pow).then_inc(s["pw2"], 1)

                with pool.Fori(0, L) as l:
                    hold(pool, s["tick"], (s["ya_done"], at(NCH * l)))
                    stage_tile(0, 0)
                    stage_tile(1, 1)
                    carry_over(l, 0, 0, 0)
                    stage_tile(0, 2)
                    inverse_norms(l, 0, 0, LP)
                    add_rotated(l, 0, 0)
                    add_rotated(l, 0, 1)
                    carry_over(l, 1, 1, 1)
                    stage_tile(1, 3)
                    inverse_norms(l, 1, 1)
                    carry_over(l, 2, 0, 2)
                    with pool.Fori(0, B) as b, pool.Fori(0, TB // 2) as jj:
                        for par in range(2):
                            t = b * TB + jj * 2 + par
                            hold(pool, s["tick"], (s["xT_mm"], at(nth_transposed(l, t + 3))))
                            stage_tile(par, (t + 4) % NT)
                            add_rotated(l, t + 1, 0)
                            add_rotated(l, t + 1, 1)
                            carry_over(l, t + 3, 1 - par, (jj * 2 + par + 3) % TB)
                            inverse_norms(l, t + 2, par)
                    inverse_deviation(l, 0)
                    with pool.Fori(0, NCH) as c:
                        hold(pool, s["tick"], (s["xnd"], at(nth_norm(l, c) + 1)))
                        pool.tensor_tensor(x[:, ds(c * CT, CT), :], x[:, ds(c * CT, CT), :],
                                           b2[:].unsqueeze(1).broadcast_to([P, CT, D]), ALU.add).then_inc(s["b2_done"], 1)
                        inverse_deviation(l, c + 1)

            @block.scalar
            def _(act):
                start(act, ACT_SEMS)
                act.wait_ge(s["ld_const"], 32)
                act.wait_ge(s["zeroed"], 4)

                def split_weights(n, ld, ld_n, cols):
                    hold(act, s["tick"], (s[ld], ld_n))
                    for i in range(2):
                        part = slice(i * cols // 2, (i + 1) * cols // 2)
                        act.activation(w_hi[:, part], raw[:, part], ACT.Copy).then_inc(s["w_hi_done"], 1)

                def stream_hi(l, t, par):
                    n = nth_transposed(l, t)
                    hold(act, s["tick"], (s["xT_mm"], at(n + 1)), (s["qkv_mm"], at(3 * nth_projected(l, t) - 3)), (s["ca_out"], at(n - 1)))
                    act.activation(hT[:, par, 0, 0, 0:P], ps_misc[:, 0:P], ACT.Copy)
                    act.activation(hT[:, par, 0, 1, 1:P + 1], ps_misc[:, P:2 * P], ACT.Copy).then_inc(s["h_hi"], 1)

                def squares(l, t, i):
                    n = nth_projected(l, t)
                    hold(act, s["tick"], (s["qkv_mm"], at(3 * n + 2 + i)), (s["red_done"], at(2 * n + i - 1)))
                    act.activation(sq[:, i, :], ps_qkv[i][:], ACT.Square, scale=(1 / QK_SCALE, 1.0)[i]).then_inc(s["sq_done"], 1)

                def qk_hi(l, t, par, i):
                    hold(act, s["tick"], (s["qkT_mm"], at(2 * nth_rotated(l, t) + i + 1)))
                    if i == 0:
                        act.activation(qT[:, par, 0], ps_misc[:].rearrange("p (j q) -> p j q", j=LP), ACT.Copy).then_inc(s["qkT_hi"], 1)
                    else:
                        act.activation(kT[:, 0, :, par * P:(par + 1) * P], ps_qkv[2][:].rearrange("p (j q) -> p j q", j=LP),
                                       ACT.Copy).then_inc(s["qkT_hi"], 1)

                def copy_values(l, t, slot):
                    hold(act, s["tick"], (s["qkv_mm"], at(3 * nth_projected(l, t) + 1)))
                    act.activation(vv[:, slot, :], ps_qkv[2][:], ACT.Copy).then_inc(s["v_done"], 1)

                def exps(l, t, g, j, par):
                    hold(act, s["tick"], (s["nb_done"], at(nth_scores(l, t, j) + 1)), (s["pt_mm"], at(LP * g + j - 1)))
                    for h in range(2):
                        step = act.activation(pr[:, j % 2, h, :], sm[:, j % 2, h, :], ACT.Exp,
                                              bias=small[:, j % 2, 1, h:h + 1], scale=rq[:, par, 2 * j + h:2 * j + h + 1],
                                              accum_out=sums[:, par, 2 * j + h:2 * j + h + 1])
                    step.then_inc(s["ex_done"], 1)

                def copy_probs(g, j):
                    hold(act, s["tick"], (s["pt_mm"], at(LP * g + j + 1)), (s["pv_mm"], at(LP * g + j)))
                    act.activation(pT[:], ps_pt[:], ACT.Copy).then_inc(s["pt_done"], 1)

                def out_hi(g):
                    hold(act, s["tick"], (s["oT_mm"], at(g + 1)), (s["wo_mm"], at(g)))
                    act.activation(oT[:, 0].rearrange("p j q -> p (j q)"), ps_pv[:], ACT.Copy).then_inc(s["o_hi"], 1)

                def chunk_full(l, c):
                    n = nth_norm(l, c)
                    hold(act, s["tick"], (s["fT_mm"], at(n + 1)), (s["f_lo"], at(n)))
                    for k in range(KT):
                        step = act.activation(ffull[:, k, :], bank[4 + k][:], ACT.Identity,
                                              scale=lncol[:, 0, k:k + 1], bias=lncol[:, 1, k:k + 1])
                    step.then_inc(s["ff_done"], 1)

                def chunk_hi(l, c):
                    hold(act, s["tick"], (s["gu_mm"], at(2 * HT * (l * NCH + c))))
                    for k in range(KT):
                        step = act.activation(fT[:, 0, k, :], bank[4 + k][:], ACT.Identity,
                                              scale=lncol[:, 0, k:k + 1], bias=lncol[:, 1, k:k + 1])
                    step.then_inc(s["f_hi"], 1)

                def gelu(n, i):
                    hold(act, s["tick"], (s["gu_mm"], at(2 * (n + i) + 2)), (s["uf_done"], at(n + i - 1)))
                    act.activation(gl[:, i % 2, :], bank[2 + i % 2][:], ACT.Gelu, bias=b1[:, HT + i:HT + i + 1]).then_inc(s["gl_done"], 1)

                def u_high(n, i):
                    hold(act, s["tick"], (s["uf_done"], at(n + i + 1)), (s["y_mm"], at(n)))
                    act.activation(uT[:, 0, i, :], uf[:, i % 2, :], ACT.Copy).then_inc(s["u_hi"], 1)

                with act.Fori(0, L) as l:
                    after(act, "y_mm", HT * NCH * l)
                    after(act, "f_lo", nth_norm(l, 0))
                    split_weights(0, "ld_attn", 64 * l + 64, A_COLS)
                    stream_hi(l, 0, 0)
                    squares(l, 0, 0)
                    squares(l, 0, 1)
                    copy_values(l, 0, 0)
                    qk_hi(l, 0, 0, 0)
                    qk_hi(l, 0, 0, 1)
                    stream_hi(l, 1, 1)
                    squares(l, 1, 0)
                    squares(l, 1, 1)
                    copy_values(l, 1, 1)
                    stream_hi(l, 2, 0)
                    with act.Fori(0, B) as b, act.Fori(0, TB // 2) as jj:
                        for par in range(2):
                            t = b * TB + jj * 2 + par
                            g = nth(l, t)
                            exps(l, t, g, 0, par)
                            exps(l, t, g, 1, par)
                            copy_probs(g, 0)
                            copy_values(l, t + 2, (jj * 2 + par + 2) % V_RING)
                            exps(l, t, g, 2, par)
                            copy_probs(g, 1)
                            copy_probs(g, 2)
                            exps(l, t, g, 3, par)
                            qk_hi(l, t + 1, 1 - par, 0)
                            copy_probs(g, 3)
                            qk_hi(l, t + 1, 1 - par, 1)
                            squares(l, t + 2, 0)
                            stream_hi(l, t + 3, 1 - par)
                            squares(l, t + 2, 1)
                            out_hi(g)
                    after(act, "wo_mm", NT * (l + 1))
                    after(act, "sc_mm", (LP * NT + 1) * (l + 1))
                    after(act, "ca_out", (NT + 3) * (l + 1))
                    split_weights(1, "ld_ffn", 80 * l + 80, F_COLS)
                    chunk_full(l, 0)
                    chunk_hi(l, 0)
                    with act.Fori(0, NCH) as c:
                        n = (l * NCH + c) * HT
                        for i in range(HT):
                            gelu(n, i)
                            if i == HT - 2:
                                u_high(n, i - 1)
                                chunk_full(l, c + 1)
                            elif i == HT - 1:
                                u_high(n, i - 1)
                                chunk_hi(l, c + 1)
                            elif i:
                                u_high(n, i - 1)
                        u_high(n, HT - 1)

            @block.vector
            def _(dve):
                start(dve, DVE_SEMS)
                dve.wait_ge(s["ld_const"], 32)
                dve.wait_ge(s["zeroed"], 4)

                def split_weights(n, cols):
                    for i in range(2):
                        part = slice(i * cols // 2, (i + 1) * cols // 2)
                        after(dve, "w_hi_done", n + i + 1)
                        dve.tensor_tensor(w_lo[:, part], raw[:, part], f32(w_hi[:, part]), ALU.subtract).then_inc(s["w_lo_done"], 1)

                def stream_lo(l, t, par):
                    after(dve, "h_hi", nth_transposed(l, t) + 1)
                    dve.tensor_tensor(hT[:, par, 1, 0, 0:P], ps_misc[:, 0:P], f32(hT[:, par, 0, 0, 0:P]), ALU.subtract)
                    dve.tensor_tensor(hT[:, par, 1, 1, 1:P + 1], ps_misc[:, P:2 * P], f32(hT[:, par, 0, 1, 1:P + 1]),
                                      ALU.subtract).then_inc(s["h_lo"], 1)

                def squared_norms(l, t, i):
                    n = 2 * nth_projected(l, t) + i
                    after(dve, "sq_done", n + 1)
                    after(dve, "red_done", n)
                    after(dve, "pw_done", 2 * nth_projected(l, t))
                    dve.tensor_reduce(norm2[:, i, 0, :], sq[:, i, :].rearrange("p (h d) -> p h d", d=DH), AX.X, ALU.add).then_inc(s["red_done"], 1)
                    after(dve, "red_done", n + 1)
                    after(dve, "fl_done", n)
                    dve.tensor_scalar(norm2[:, i, 1, :], norm2[:, i, 0, :], (NORM_FLOOR / (QK_SCALE, 1.0)[i]) ** 2, None,
                                      ALU.max).then_inc(s["fl_done"], 1)

                def rotate(l, t, i, z, w):
                    cos, sin = rope[:, 2 * i, w, :], rope[:, 2 * i + 1, w, :]
                    zh = z.rearrange("p (h d) -> p h d", d=DH)
                    th = rt[:, i, :].rearrange("p (h d) -> p h d", d=DH)
                    half = DH // 2
                    hold(dve, s["tick"], (s["qkT_mm"], at(2 * nth_rotated(l, t) + i - 1)))
                    dve.tensor_tensor(ra[:, i, :].rearrange("p (h d) -> p h d", d=DH), zh,
                                      cos.unsqueeze(1).broadcast_to([P, LH, DH]), ALU.mult).then_inc(s["ra_done"], 1)
                    for a0, b0 in ((0, half), (half, 0)):
                        dve.tensor_tensor(th[:, :, a0:a0 + half], zh[:, :, b0:b0 + half],
                                          sin[:, a0:a0 + half].unsqueeze(1).broadcast_to([P, LH, half]), ALU.mult).then_inc(s["ra_done"], 1)

                def rotate_q(l, t, w):
                    after(dve, "qkv_mm", 3 * nth_projected(l, t) + 2)
                    rotate(l, t, 0, ps_qkv[0][:], w)

                def rotate_k(l, t, w):
                    after(dve, "kn_done", nth_rotated(l, t) + 1)
                    rotate(l, t, 1, kn[:], w)

                def normalise_keys(l, t):
                    after(dve, "pw_done", 2 * nth_projected(l, t) + 1)
                    after(dve, "qkv_mm", 3 * nth_projected(l, t) + 3)
                    dve.tensor_tensor(kn[:].rearrange("p (h d) -> p h d", d=DH), ps_qkv[1][:].rearrange("p (h d) -> p h d", d=DH),
                                      rk[:].unsqueeze(2).broadcast_to([P, LH, DH]), ALU.mult).then_inc(s["kn_done"], 1)

                def qk_lo(l, t, par, i):
                    after(dve, "qkT_hi", 2 * nth_rotated(l, t) + i + 1)
                    if i == 0:
                        hi, lo, src = qT[:, par, 0], qT[:, par, 1], ps_misc
                    else:
                        hi, lo, src = kT[:, 0, :, par * P:(par + 1) * P], kT[:, 1, :, par * P:(par + 1) * P], ps_qkv[2]
                    dve.tensor_tensor(lo, src[:].rearrange("p (j q) -> p j q", j=LP), f32(hi), ALU.subtract).then_inc(s["qkT_lo"], 1)

                def maxima(l, t, g, j, par):
                    hold(dve, s["tick"], (s["sc_mm"], at(nth_scores(l, t, j) + 1)), (s["ex_done"], at(LP * g + j - 1)))
                    for h in range(2):
                        dve.tensor_tensor_reduce(sm[:, j % 2, h, :], ps_s[h][:, 0:2 * P], mask[:, par].rearrange("p a b -> p (a b)"),
                                                 1.0, -3.0e38, ALU.add, ALU.max, small[:, j % 2, 0, h:h + 1]).then_inc(s["mx_done"], 1)
                    after(dve, "mx_done", 2 * nth_scores(l, t, j) + 2)
                    after(dve, "pw_done", 2 * nth_projected(l, t) + 2)
                    dve.scalar_tensor_tensor(small[:, j % 2, 1, :], small[:, j % 2, 0, :], -1.0, rq[:, par, 2 * j:2 * j + 2],
                                             ALU.mult, ALU.mult).then_inc(s["nb_done"], 1)

                def normalise_out(g, par):
                    after(dve, "ex_done", LP * g + LP)
                    after(dve, "on_done", g)
                    dve.reciprocal(rsum[:], sums[:, par, :]).then_inc(s["rc_done"], 1)
                    after(dve, "rc_done", g + 1)
                    after(dve, "pv_mm", LP * g + LP)
                    after(dve, "oT_mm", g)
                    dve.tensor_tensor(on[:].rearrange("p (h d) -> p h d", d=DH), ps_pv[:].rearrange("p (h d) -> p h d", d=DH),
                                      rsum[:].unsqueeze(2).broadcast_to([P, LH, DH]), ALU.mult).then_inc(s["on_done"], 1)

                def out_lo(g):
                    after(dve, "o_hi", g + 1)
                    dve.tensor_tensor(oT[:, 1].rearrange("p j q -> p (j q)"), ps_pv[:], f32(oT[:, 0]).rearrange("p j q -> p (j q)"),
                                      ALU.subtract).then_inc(s["o_lo"], 1)

                def chunk_statistics(l, c, step_no, where):
                    n = nth_norm(l, c)
                    if step_no == 0:
                        after(dve, "ag", CT * n)
                        for t in range(CT):
                            dve.bn_stats(st[:, t, 0:6], x[:, where * CT + t, 0:P]).then_inc(s["bn"], 1)
                            dve.bn_stats(st[:, t, 6:12], shifted[:, where * CT + t, :]).then_inc(s["bn"], 1)
                    else:
                        after(dve, "bn", 2 * CT * (n + 1))
                        after(dve, "nr", n)
                        dve.sem_inc(s["tick"], 1)
                        for t in range(CT):
                            dve.bn_aggr(mv[:, t, :], st[:, t, :]).then_inc(s["ag"], 1)
                        after(dve, "ag", CT * (n + 1))
                        dve.tensor_scalar(nrm[:, 0, :], mv[:, :, 1], EPS, None, ALU.add).then_inc(s["vr"], 1)

                def chunk_normalise(l, c, where):
                    n = nth_norm(l, c)
                    after(dve, "pw2", n + 1)
                    dve.scalar_tensor_tensor(nrm[:, 2, :], mv[:, :, 0], -1.0, nrm[:, 1, :], ALU.mult, ALU.mult).then_inc(s["nr"], 1)
                    after(dve, "nr", n + 1)
                    after(dve, "fT_mm", n)
                    for t in range(CT):
                        for k, src in enumerate((x[:, where * CT + t, 0:P], shifted[:, where * CT + t, :])):
                            step = dve.tensor_scalar(xn[:, t, k * P:(k + 1) * P], src, nrm[:, 1, t:t + 1], nrm[:, 2, t:t + 1],
                                                     ALU.mult, ALU.add)
                    step.then_inc(s["xnd"], 1)

                def chunk_lo(l, c):
                    after(dve, "f_hi", nth_norm(l, c) + 1)
                    dve.tensor_tensor(fT[:, 1], ffull[:], f32(fT[:, 0]), ALU.subtract).then_inc(s["f_lo"], 1)

                def hidden_full(n, i):
                    after(dve, "gl_done", n + i + 1)
                    after(dve, "u_lo", n + i - 1)
                    dve.scalar_tensor_tensor(uf[:, i % 2, :], bank[i % 2][:], b1[:, i:i + 1], gl[:, i % 2, :],
                                             ALU.add, ALU.mult).then_inc(s["uf_done"], 1)

                def hidden_lo(n, i):
                    after(dve, "u_hi", n + i + 1)
                    dve.tensor_tensor(uT[:, 1, i, :], uf[:, i % 2, :], f32(uT[:, 0, i, :]), ALU.subtract).then_inc(s["u_lo"], 1)

                with dve.Fori(0, L) as l:
                    after(dve, "f_lo", nth_norm(l, 0))
                    split_weights(4 * l, A_COLS)
                    for i in range(4):
                        dve.tensor_tensor(rope[:, i], raw[:, A_COLS + i * TB * DH:A_COLS + (i + 1) * TB * DH].rearrange("p (t d) -> p t d", d=DH),
                                          rows[:, i, :].unsqueeze(1).broadcast_to([P, TB, DH]), ALU.mult).then_inc(s["rope_q"], 1)
                    hold(dve, s["tick"], (s["rope_q"], at(4 * l + 4)))
                    stream_lo(l, 0, 0)
                    squared_norms(l, 0, 0)
                    squared_norms(l, 0, 1)
                    rotate_q(l, 0, 0)
                    normalise_keys(l, 0)
                    rotate_k(l, 0, 0)
                    qk_lo(l, 0, 0, 0)
                    qk_lo(l, 0, 0, 1)
                    stream_lo(l, 1, 1)
                    squared_norms(l, 1, 0)
                    squared_norms(l, 1, 1)
                    stream_lo(l, 2, 0)
                    after(dve, "msk", (NT // 2 + 1) * l)
                    dve.tensor_copy(mask[:, 0, 1, :], prev_mask[:, 0, :]).then_inc(s["msk"], 1)
                    after(dve, "msk", (NT // 2 + 1) * l + 1)
                    maxima(l, 0, nth(l, 0), 0, 0)
                    dve.sem_inc(s["tick"], 1)
                    with dve.Fori(0, B) as b, dve.Fori(0, TB // 2) as jj:
                        for par in range(2):
                            t = b * TB + jj * 2 + par
                            g = nth(l, t)
                            w = (jj * 2 + par + 1) % TB
                            maxima(l, t, g, 1, par)
                            rotate_q(l, t + 1, w)
                            maxima(l, t, g, 2, par)
                            normalise_keys(l, t + 1)
                            rotate_k(l, t + 1, w)
                            maxima(l, t, g, 3, par)
                            qk_lo(l, t + 1, 1 - par, 0)
                            qk_lo(l, t + 1, 1 - par, 1)
                            normalise_out(g, par)
                            squared_norms(l, t + 2, 0)
                            if par == 1:
                                m = (NT // 2 + 1) * l + b * (TB // 2) + jj + 1
                                after(dve, "msk", m)
                                dve.tensor_copy(mask[:, 0, 1, :], prev_mask[:, (jj + 1) % (TB // 2), :]).then_inc(s["msk"], 1)
                                after(dve, "msk", m + 1)
                            stream_lo(l, t + 3, 1 - par)
                            out_lo(g)
                            maxima(l, t + 1, g + 1, 0, 1 - par)
                            squared_norms(l, t + 2, 1)
                            after(dve, "wo_mm", g + 1)
                            dve.tensor_tensor(x[:, t, :], x[:, t, :], ps_misc[:, 0:D], ALU.add).then_inc(s["xa_done"], 1)
                    split_weights(4 * l + 2, F_COLS)
                    hold(dve, s["tick"], (s["shift_in"], 128 * l + 128))
                    chunk_statistics(l, 0, 0, 0)
                    chunk_statistics(l, 0, 1, 0)
                    chunk_normalise(l, 0, 0)
                    chunk_lo(l, 0)
                    dve.sem_inc(s["tick"], 1)
                    with dve.Fori(0, NCH) as c:
                        ci = l * NCH + c
                        nxt = (c + 1) % NCH
                        hidden_full(ci * HT, 0)
                        after(dve, "ya_done", ci)
                        chunk_statistics(l, c + 1, 0, nxt)
                        hidden_full(ci * HT, 1)
                        hidden_lo(ci * HT, 0)
                        chunk_statistics(l, c + 1, 1, nxt)
                        hidden_full(ci * HT, 2)
                        hidden_lo(ci * HT, 1)
                        chunk_normalise(l, c + 1, nxt)
                        for i in range(3, HT):
                            hidden_full(ci * HT, i)
                            hidden_lo(ci * HT, i - 1)
                        hidden_lo(ci * HT, HT - 1)
                        chunk_lo(l, c + 1)
                        after(dve, "y_mm", HT * (ci + 1))
                        after(dve, "b2_done", ci + 1)
                        for i in range(2):
                            step = dve.tensor_tensor(x[:, ds(c * CT + 2 * i, 2), :], x[:, ds(c * CT + 2 * i, 2), :],
                                                     bank[6 + i][:].rearrange("p (t d) -> p t d", d=D), ALU.add)
                        step.then_inc(s["ya_done"], 1)

            @block.tensor
            def _(pe):
                start(pe, PE_SEMS)
                pe.wait_ge(s["zeroed"], 4)

                def stream_T(l, t, par):
                    after(pe, "xs_done", nth_staged(l, t) + 1)
                    after(pe, "h_lo", nth_transposed(l, t))
                    for k in range(KT):
                        step = pe.transpose(ps_misc[:, k * P:(k + 1) * P], xs[:, par, k * P:(k + 1) * P], ident[:])
                    step.then_inc(s["xT_mm"], 1)

                def project(l, t, par, i):
                    n = nth_rotated(l, t)
                    if i == 2:
                        after(pe, "h_lo", nth_transposed(l, t) + 1)
                        after(pe, "ca_in", nth_transposed(l, t) + 1)
                        after(pe, "v_done", nth_projected(l, t))
                    if i == 0:
                        after(pe, "ra_done", 6 * n - 3)
                        after(pe, "sq_done", 2 * nth_projected(l, t))
                    if i == 1:
                        after(pe, "kn_done", n)
                    cols = slice(i * INNER, (i + 1) * INNER)
                    for k in range(KT):
                        step = three_products(pe, ps_qkv[i][:], hT[:, par, 0, k, 0:P], hT[:, par, 1, k, 0:P],
                                              wqkv[0][:, k, cols], wqkv[1][:, k, cols], k == 0, k == KT - 1)
                    step.then_inc(s["qkv_mm"], 1)

                def qk_T(l, t, i):
                    after(pe, "add_done", 2 * nth_rotated(l, t) + i + 1)
                    for j in range(LP):
                        dst = (ps_misc, ps_qkv[2])[i]
                        step = pe.transpose(dst[:, j * P:(j + 1) * P], ra[:, i, j * P:(j + 1) * P], ident[:])
                    step.then_inc(s["qkT_mm"], 1)

                def scores(l, t, j, par):
                    after(pe, "mx_done", 2 * nth_scores(l, t, j))
                    for n, (qx, kx) in enumerate(((0, 0), (0, 1), (1, 0))):
                        for h in range(2):
                            rws = slice(h * DH, (h + 1) * DH)
                            step = pe.matmul(ps_s[h][:, 0:2 * P], qT[rws, par, qx, j, :], kT[rws, kx, j, :], start=(n == 0),
                                             stop=(n == 2), skip_group_check=True)
                    step.then_inc(s["sc_mm"], 1)

                def probs_T(g, j):
                    after(pe, "ex_done", LP * g + j + 1)
                    after(pe, "pt_done", LP * g + j)
                    for slot in range(2):
                        for h in range(2):
                            step = pe.transpose(ps_pt[:, (2 * slot + h) * P:(2 * slot + h + 1) * P],
                                                pr[:, j % 2, h, slot * P:(slot + 1) * P], ident[:])
                    step.then_inc(s["pt_mm"], 1)

                def values(g, j, v_slots):
                    after(pe, "pt_done", LP * g + j + 1)
                    for h in range(2):
                        cols = slice((2 * j + h) * DH, (2 * j + h + 1) * DH)
                        for slot in range(2):
                            step = pe.matmul(ps_pv[:, cols], pT[:, (2 * slot + h) * P:(2 * slot + h + 1) * P], vv[:, v_slots[slot], cols],
                                             start=(j == 0 and h == 0 and slot == 0), stop=(slot == 1), skip_group_check=True)
                    step.then_inc(s["pv_mm"], 1)

                def out_T(g):
                    after(pe, "on_done", g + 1)
                    for j in range(LP):
                        step = pe.transpose(ps_pv[:, j * P:(j + 1) * P], on[:, j * P:(j + 1) * P], ident[:])
                    step.then_inc(s["oT_mm"], 1)

                def project_out(g):
                    after(pe, "o_lo", g + 1)
                    for k in range(LP):
                        step = three_products(pe, ps_misc[:, 0:D], oT[:, 0, k, :], oT[:, 1, k, :], wo[0][:, k, :], wo[1][:, k, :],
                                              k == 0, k == LP - 1)
                    step.then_inc(s["wo_mm"], 1)

                def chunk_T(l, c):
                    n = nth_norm(l, c)
                    after(pe, "xnd", n + 1)
                    after(pe, "f_hi", n)
                    for t in range(CT):
                        for k in range(KT):
                            step = pe.transpose(bank[4 + k][:, t * P:(t + 1) * P], xn[:, t, k * P:(k + 1) * P], ident[:])
                    step.then_inc(s["fT_mm"], 1)

                def hidden(n, i):
                    after(pe, "uf_done", n + i - 1)
                    for gate in range(2):
                        cols = slice((gate * HT + i) * P, (gate * HT + i + 1) * P)
                        for k in range(KT):
                            step = three_products(pe, bank[2 * gate + i % 2][:], w1[0][:, k, cols], w1[1][:, k, cols],
                                                  fT[:, 0, k, :], fT[:, 1, k, :], k == 0, k == KT - 1)
                        step.then_inc(s["gu_mm"], 1)

                def hidden_out(n, i):
                    after(pe, "u_lo", n + i + 1)
                    for t in range(CT):
                        step = three_products(pe, bank[6 + t // 2][:, (t % 2) * D:(t % 2 + 1) * D],
                                              uT[:, 0, i, t * P:(t + 1) * P], uT[:, 1, i, t * P:(t + 1) * P],
                                              w2[0][:, i, :], w2[1][:, i, :], i == 0 and t % 2 == 0, i == HT - 1)
                    step.then_inc(s["y_mm"], 1)

                with pe.Fori(0, L) as l:
                    after(pe, "w_lo_done", 4 * l + 2)
                    after(pe, "ya_done", NCH * l)
                    stream_T(l, 0, 0)
                    for i in (2, 0, 1):
                        project(l, 0, 0, i)
                    qk_T(l, 0, 0)
                    after(pe, "v_done", nth_projected(l, 0) + 1)
                    qk_T(l, 0, 1)
                    after(pe, "qkT_lo", 2 * nth_rotated(l, 0) + 2)
                    stream_T(l, 1, 1)
                    for i in (2, 0, 1):
                        project(l, 1, 1, i)
                    stream_T(l, 2, 0)
                    scores(l, 0, 0, 0)
                    with pe.Fori(0, B) as b, pe.Fori(0, TB // 2) as jj:
                        for par in range(2):
                            t = b * TB + jj * 2 + par
                            g = nth(l, t)
                            this, before = (jj * 2 + par) % V_RING, (jj * 2 + par + V_RING - 1) % V_RING
                            v_slots = (this, before) if par == 0 else (before, this)
                            scores(l, t, 1, par)
                            project(l, t + 2, par, 2)
                            probs_T(g, 0)
                            scores(l, t, 2, par)
                            values(g, 0, v_slots)
                            probs_T(g, 1)
                            project(l, t + 2, par, 0)
                            scores(l, t, 3, par)
                            probs_T(g, 2)
                            values(g, 1, v_slots)
                            after(pe, "xa_done", g)
                            qk_T(l, t + 1, 0)
                            after(pe, "v_done", nth_projected(l, t + 2) + 1)
                            qk_T(l, t + 1, 1)
                            values(g, 2, v_slots)
                            probs_T(g, 3)
                            values(g, 3, v_slots)
                            after(pe, "qkT_lo", 2 * nth_rotated(l, t + 1) + 1)
                            stream_T(l, t + 3, 1 - par)
                            project(l, t + 2, par, 1)
                            out_T(g)
                            after(pe, "qkT_lo", 2 * nth_rotated(l, t + 1) + 2)
                            scores(l, t + 1, 0, 1 - par)
                            after(pe, "h_lo", nth_transposed(l, t + 3) + 1)
                            project_out(g)
                    hold(pe, s["tick"], (s["w_lo_done"], at(4 * l + 4)), (s["sq_done"], at(2 * (NT + 2) * (l + 1))),
                         (s["nb_done"], at((LP * NT + 1) * (l + 1))), (s["xa_done"], at(NT * (l + 1))))
                    chunk_T(l, 0)
                    with pe.Fori(0, NCH) as c:
                        ci = l * NCH + c
                        after(pe, "f_lo", nth_norm(l, c) + 1)
                        hidden(ci * HT, 0)
                        hidden(ci * HT, 1)
                        hidden(ci * HT, 2)
                        after(pe, "ya_done", ci)
                        hidden_out(ci * HT, 0)
                        hidden(ci * HT, 3)
                        hidden_out(ci * HT, 1)
                        hidden(ci * HT, 4)
                        hidden_out(ci * HT, 2)
                        chunk_T(l, c + 1)
                        hidden(ci * HT, 5)
                        for i in range(3, HT):
                            hidden_out(ci * HT, i)

def constants():
    k, q = np.arange(P)[:, None], np.arange(P)[None, :]
    return {
        "ident": np.eye(P, dtype=np.float32),
        "ident16": np.eye(P, dtype=np.float16),
        "causal16": np.where(q >= k, 0.0, -60000.0).astype(np.float16),
        "rope": rope_tables(),
        **local_masks(),
    }


def rope_tables():
    half = np.arange(0, DH, 2, dtype=np.float32)
    inv_freq = np.float32(1.0) / np.float32(10000.0) ** (half / np.float32(DH))
    t = np.arange(S, dtype=np.float32)
    freqs = np.concatenate([t[:, None] * inv_freq[None, :]] * 2, axis=-1)
    base = (half + np.float32(0.4 * DH)) / np.float32(1.4 * DH)
    power = (t - np.float32(S // 2)) / np.float32(P // 2)
    scale = base[None, :] ** power[:, None]
    scale = np.concatenate([scale, scale], axis=-1)
    sign = np.where(np.arange(DH) < DH // 2, -1.0, 1.0).astype(np.float32)
    cos, sin = np.cos(freqs), np.sin(freqs) * sign
    tables = np.stack([cos * scale, sin * scale, cos / scale, sin / scale]).astype(np.float32)
    return np.ascontiguousarray(tables.reshape(4, TB, P, DH).transpose(2, 0, 1, 3).reshape(P, -1))


def local_masks():
    q, k = np.arange(P)[:, None], np.arange(P)[None, :]
    own = np.where(k <= q, 0.0, MASKED).astype(np.float32)
    before = np.where(k >= q, 0.0, MASKED).astype(np.float32)
    none = np.full((P, P), MASKED, np.float32)
    mask = np.stack([np.stack([own, before], axis=1), np.stack([before, own], axis=1)], axis=1)
    return {"mask": mask, "prev_mask": np.stack([none] + [before] * (TB // 2 - 1), axis=1)}


def build(nc, io):
    scr = {
        "hT_hi": nc.dram_tensor("hT_hi", [B, P, KT, S], F32, kind="Internal").ap(),
        "hT_lo": nc.dram_tensor("hT_lo", [B, P, KT, S], F32, kind="Internal").ap(),
        "x1": nc.dram_tensor("x1", [B, S, D], F32, kind="Internal").ap(),
    }
    with ExitStack() as ctx:
        a = Allocator(nc, ctx)
        keep = {
            "ident": a.sb("ident", [P, P]),
            "modT": a.sb("modT", [P, 6, B]),
            "modB": a.sb("modB", [P, B, 3 * D]),
        }
        phase_modulation_and_norm1(nc, io, scr, keep)
        phase_attention(nc, io, scr, keep)
        keep["stream"] = a.sb("stream", [P, NT, D])
        phase_norm2(nc, io, scr, keep)
        phase_layers(nc, io, scr, keep)
        phase_output(nc, io, scr, keep)


def kernel(**inputs):
    import concourse.bacc as _bacc
    from concourse.bass_utils import run_bass_kernel_spmd as _run

    nc = _bacc.Bacc("TRN2", target_bir_lowering=False, num_devices=1)
    arrays = {n.removeprefix("L0_attn_").removeprefix("L0_"): np.ascontiguousarray(v) for n, v in inputs.items()}
    arrays["cT"] = np.ascontiguousarray(arrays.pop("c").T)
    arrays["b_vqk"] = np.stack([arrays.pop(n).reshape(HP, P).T for n in ("bv", "bq", "bk")], axis=1)
    arrays["bo_col"] = np.ascontiguousarray(arrays.pop("bo").reshape(KT, P).T)
    qs, ks = arrays.pop("ffn_q_scale"), arrays.pop("ffn_k_scale")
    arrays["qk_rows"] = np.stack([qs, np.roll(qs, DH // 2, axis=1), ks, np.roll(ks, DH // 2, axis=1)], axis=1)
    arrays["ln_col"] = np.ascontiguousarray(
        np.stack([arrays.pop("ffn_ln_g"), arrays.pop("ffn_ln_b")], axis=1).reshape(L, 2, KT, P).transpose(0, 3, 1, 2))
    w1, w2, b1 = arrays.pop("ffn_w1"), arrays.pop("ffn_w2"), arrays.pop("ffn_b1")
    arrays["w1"] = np.zeros((L, D, 2, HT * P), w1.dtype)
    arrays["w1"][:, :, :, :HID] = w1.reshape(L, D, 2, HID)
    arrays["w2"] = np.zeros((L, HT * P, D), w2.dtype)
    arrays["w2"][:, :HID] = w2
    b1_pad = np.zeros((L, 2, HT * P), b1.dtype)
    b1_pad[:, :, :HID] = b1.reshape(L, 2, HID)
    arrays["b1_col"] = np.ascontiguousarray(b1_pad.reshape(L, 2 * HT, P).transpose(0, 2, 1))
    arrays.update(constants())
    io = {n: nc.dram_tensor("in_" + n, v.shape, mybir.dt.from_np(v.dtype), kind="ExternalInput").ap()
          for n, v in arrays.items()}
    io["out"] = nc.dram_tensor("out", (B, S, D), F32, kind="ExternalOutput").ap()
    build(nc, io)
    r = _run(nc, [{"in_" + n: v for n, v in arrays.items()}], core_ids=[0])
    return r.results[0]["out"]
```

```python
import numpy as np
import concourse.bass as bass
from concourse import mybir
from contextlib import ExitStack

F32 = mybir.dt.float32
F32R = mybir.dt.float32r
F16 = mybir.dt.float16
ALU = mybir.AluOpType
ACT = mybir.ActivationFunctionType
AX = mybir.AxisListType
ds = bass.ds

P = 128
B, S, D = 4, 1024, 256
KT = D // P
NT = B * S // P
TB = S // P
H, DH = 16, 64
HP = H // 2
CH = 512
NC = S // CH
CT = CH // P
EPS = 1e-5
SCORE_SCALE = DH ** -0.5
SCORE_SHIFT = 3.0
VW = 2 * DH + 2
MASKED = -1.0e30
CREDIT = 4


def at(n):
    return n + CREDIT


def hold(eng, tick, *waits):
    for sem, value in waits:
        eng.wait_ge(sem, value)
    eng.sem_inc(tick, 1)


def f32(ap):
    return ap.bitcast(F32)


class Allocator:
    def __init__(self, nc, ctx):
        self.nc, self.ctx = nc, ctx

    def sb(self, name, shape, dt=F32):
        return self.ctx.enter_context(self.nc.sbuf_tensor(name, shape, dt))

    def ps(self, name, shape, dt=F32):
        return self.ctx.enter_context(self.nc.psum_tensor(name, shape, dt))

    def sems(self, prefix, names):
        return [self.ctx.enter_context(self.nc.semaphore(prefix + n)) for n in names.split()]


def three_products(pe, out, w_hi, w_lo, x_hi, x_lo, first, last):
    pe.matmul(out, w_hi, x_hi, start=first, stop=False, skip_group_check=True)
    pe.matmul(out, w_hi, x_lo, start=False, stop=False, skip_group_check=True)
    return pe.matmul(out, w_lo, x_hi, start=False, stop=last, skip_group_check=True)


def variance_steps(dve, chain, n, st, mean2, tmp, var, var_ready):
    dve.tensor_tensor(tmp[:, 0, :], st[:, :, 1], st[:, :, 4], ALU.subtract).then_inc(chain, 1)
    dve.tensor_tensor(tmp[:, 1, :], st[:, :, 2], st[:, :, 5], ALU.add).then_inc(chain, 1)
    dve.tensor_tensor(mean2, st[:, :, 1], st[:, :, 4], ALU.add).then_inc(chain, 1)
    dve.wait_ge(chain, n + 2)
    dve.tensor_tensor(tmp[:, 2, :], tmp[:, 0, :], tmp[:, 0, :], ALU.mult).then_inc(chain, 1)
    dve.tensor_scalar(tmp[:, 3, :], tmp[:, 1, :], 1.0 / D, EPS, ALU.mult, ALU.add).then_inc(chain, 1)
    dve.wait_ge(chain, n + 5)
    dve.scalar_tensor_tensor(var, tmp[:, 2, :], 0.25, tmp[:, 3, :], ALU.mult, ALU.add).then_inc(var_ready, 1)
    return n + 5


def phase_modulation_and_norm1(nc, io, scr, keep):
    with ExitStack() as ctx:
        a = Allocator(nc, ctx)
        x = a.sb("n1_x", [P, NT, D])
        ident, modT, modB = keep["ident"], keep["modT"], keep["modB"]
        cT = a.sb("n1_cT", [P, KT, B])
        silu = a.sb("n1_silu", [P, 4, KT, B])
        silu_rows = a.sb("n1_silu_rows", [P, KT, B, P])
        wmod = a.sb("n1_wmod", [P, KT, 6 * D])
        gate = a.sb("n1_gate", [P, 3, D])
        st = a.sb("n1_stats", [P, NT, 6])
        tmp = a.sb("n1_tmp", [P, 4, NT])
        col = a.sb("n1_columns", [P, 5, NT])
        xn = a.sb("n1_xn", [P, NC, CT, D])
        full = a.sb("n1_full", [P, NC, KT, CH])
        hi = a.sb("n1_hi", [P, NC, KT, CH], F32R)
        lo = a.sb("n1_lo", [P, NC, KT, CH], F32R)
        ps_mod = a.ps("n1_ps_mod", [P, 12, B])
        ps_row = a.ps("n1_ps_row", [P, 2, CH])
        ps_t = [a.ps(f"n1_ps_t{i}", [P, KT, CH]) for i in range(NC)]
        (ld_c, ld_w, ld_i, exp_done, silu_done, silu_bc, mod_mm, mod_ev, row_mm, row_ev, bn, chain, var_ready,
         std_ready, norm_ready, xn_ready, t_done, full_done, hi_done, lo_done, tick) = a.sems(
            "n1_", "ld_c ld_w ld_i exp_done silu_done silu_bc mod_mm mod_ev row_mm row_ev bn chain var_ready "
            "std_ready norm_ready xn_ready t_done full_done hi_done lo_done tick")
        ld_x = [a.sems("n1_", f"ld_x{b}")[0] for b in range(B)]
        out_hi = a.sems("n1_", "out_hi0 out_hi1")
        out_lo = a.sems("n1_", "out_lo0 out_lo1")
        with nc.Block() as block:

            @block.sync
            def _(sp):
                for s in out_hi + out_lo:
                    sp.sem_inc(s, 16)
                sp.dma_start(cT[:], io["cT"].rearrange("(k p) b -> p k b", p=P)).then_inc(ld_c, 16)
                sp.dma_start(wmod[:], io["wmod"].rearrange("(k p) n -> p k n", p=P)).then_inc(ld_w, 16)
                for b in range(B):
                    sp.dma_start(x[:, b * TB:(b + 1) * TB, :],
                                 io["states"][b].rearrange("(t p) d -> p t d", p=P)).then_inc(ld_x[b], 16)
                sp.dma_start(ident[:], io["ident"]).then_inc(ld_i, 16)
                with sp.Fori(0, B) as b:
                    for c in range(NC):
                        cols = slice(c * CH, (c + 1) * CH)
                        sp.wait_ge(hi_done, at(b * NC + c + 1))
                        sp.dma_start(scr["hT_hi"][b, :, :, cols], f32(hi[:, c])).then_inc(out_hi[c], 16)
                        sp.wait_ge(lo_done, at(b * NC + c + 1))
                        sp.dma_start(scr["hT_lo"][b, :, :, cols], f32(lo[:, c])).then_inc(out_lo[c], 16)
                for s in out_hi + out_lo:
                    sp.wait_ge(s, 16 * (B + 1))

            @block.scalar
            def _(act):
                act.sem_inc(full_done, CREDIT)
                act.sem_inc(hi_done, CREDIT)
                act.wait_ge(ld_c, 16)
                act.activation(silu[:, 0], cT[:], ACT.Exp, scale=-1.0).then_inc(exp_done, 1)
                act.wait_ge(var_ready, 1)
                act.activation(col[:, 2, :], col[:, 1, :], ACT.Sqrt).then_inc(std_ready, 1)
                act.wait_ge(mod_ev, 2)
                with act.Fori(0, B) as b:
                    for c in range(NC):
                        hold(act, tick, (t_done, b * NC + c + 1), (lo_done, at(b * NC + c - 1)))
                        for k in range(KT):
                            step = act.activation(full[:, c, k, :], ps_t[c][:, k, :], ACT.Identity,
                                                  scale=modT[:, KT + k, ds(b, 1)], bias=modT[:, k, ds(b, 1)])
                        step.then_inc(full_done, 1)
                        hold(act, tick, (out_hi[c], 16 * b + 16))
                        for k in range(KT):
                            step = act.activation(hi[:, c, k, :], ps_t[c][:, k, :], ACT.Identity,
                                                  scale=modT[:, KT + k, ds(b, 1)], bias=modT[:, k, ds(b, 1)])
                        step.then_inc(hi_done, 1)

            @block.vector
            def _(dve):
                dve.sem_inc(lo_done, CREDIT)

                def modulation_rows(b):
                    dve.wait_ge(row_mm, b + 1)
                    dve.tensor_copy(modB[:, b, 0:D], ps_row[:, 0, 0:D]).then_inc(row_ev, 1)
                    dve.tensor_scalar(modB[:, b, D:2 * D], ps_row[:, 0, D:2 * D], 1.0, None, ALU.add).then_inc(row_ev, 1)
                    if b:
                        dve.wait_ge(row_ev, 6 * b)
                    dve.tensor_scalar(gate[:, 0, 0:D], ps_row[:, 1, 0:D], 0.0, 2.0, ALU.is_ge, ALU.mult).then_inc(row_ev, 1)
                    dve.tensor_scalar(gate[:, 2, 0:D], ps_row[:, 1, 0:D], -1.0, 0.25, ALU.mult, ALU.max).then_inc(row_ev, 1)
                    dve.wait_ge(row_ev, 6 * b + 4)
                    dve.tensor_tensor(gate[:, 1, 0:D], ps_row[:, 1, 0:D], gate[:, 2, 0:D], ALU.max).then_inc(row_ev, 1)
                    dve.wait_ge(row_ev, 6 * b + 5)
                    dve.scalar_tensor_tensor(modB[:, b, 2 * D:3 * D], gate[:, 0, 0:D], -1.0, gate[:, 1, 0:D],
                                             ALU.add, ALU.mult).then_inc(row_ev, 1)

                dve.wait_ge(exp_done, 1)
                dve.tensor_scalar(silu[:, 1], silu[:, 0], 1.0, None, ALU.add).then_inc(silu_done, 1)
                dve.wait_ge(silu_done, 1)
                dve.reciprocal(silu[:, 2], silu[:, 1]).then_inc(silu_done, 1)
                dve.wait_ge(silu_done, 2)
                dve.tensor_tensor(silu[:, 3], silu[:, 2], cT[:], ALU.mult).then_inc(silu_done, 1)
                dve.wait_ge(silu_done, 3)
                for k in range(KT):
                    dve.tensor_copy(silu_rows[:, k], silu[:, 3, k].unsqueeze(2).broadcast_to([P, B, P])).then_inc(silu_bc, 1)
                for b in range(B):
                    for t in range(TB):
                        if t == 0:
                            dve.wait_ge(ld_x[b], 16)
                        dve.bn_stats(st[:, b * TB + t, :], x[:, b * TB + t, :]).then_inc(bn, 1)
                    modulation_rows(b)
                dve.wait_ge(bn, NT)
                variance_steps(dve, chain, 0, st, col[:, 0, :], tmp, col[:, 1, :], var_ready)
                dve.wait_ge(mod_mm, 1)
                dve.wait_ge(row_ev, 6 * B)
                dve.tensor_copy(modT[:, 0:2, :], ps_mod[:, 0:2, :]).then_inc(mod_ev, 1)
                dve.tensor_scalar(modT[:, 2:4, :], ps_mod[:, 2:4, :], 1.0, None, ALU.add).then_inc(mod_ev, 1)
                dve.tensor_scalar(gate[:, 0, 0:8], ps_mod[:, 4:6, :].rearrange("p a b -> p (a b)"), 0.0, 2.0,
                                  ALU.is_ge, ALU.mult).then_inc(mod_ev, 1)
                dve.tensor_scalar(gate[:, 2, 0:8], ps_mod[:, 4:6, :].rearrange("p a b -> p (a b)"), -1.0, 0.25,
                                  ALU.mult, ALU.max).then_inc(mod_ev, 1)
                dve.wait_ge(mod_ev, 4)
                dve.tensor_tensor(gate[:, 1, 0:8], ps_mod[:, 4:6, :].rearrange("p a b -> p (a b)"), gate[:, 2, 0:8],
                                  ALU.max).then_inc(mod_ev, 1)
                dve.wait_ge(mod_ev, 5)
                dve.scalar_tensor_tensor(modT[:, 4:6, :].rearrange("p a b -> p (a b)"), gate[:, 0, 0:8], -1.0,
                                         gate[:, 1, 0:8], ALU.add, ALU.mult).then_inc(mod_ev, 1)
                dve.wait_ge(std_ready, 1)
                dve.reciprocal(col[:, 3, :], col[:, 2, :]).then_inc(norm_ready, 1)
                dve.wait_ge(norm_ready, 1)
                dve.scalar_tensor_tensor(col[:, 4, :], col[:, 0, :], -0.5, col[:, 3, :], ALU.mult,
                                         ALU.mult).then_inc(norm_ready, 1)
                dve.wait_ge(norm_ready, 2)

                def normalise_chunk(b, c):
                    for t in range(CT):
                        n = b * TB + c * CT + t
                        step = dve.tensor_scalar(xn[:, c, t, :], x[:, n, :], col[:, 3, ds(n, 1)], col[:, 4, ds(n, 1)],
                                                 ALU.mult, ALU.add)
                    step.then_inc(xn_ready, 1)

                for c in range(NC):
                    normalise_chunk(0, c)
                dve.sem_inc(tick, 1)
                with dve.Fori(0, B) as b:
                    for c in range(NC):
                        dve.wait_ge(hi_done, at(b * NC + c + 1))
                        dve.wait_ge(out_lo[c], 16 * b + 16)
                        dve.tensor_tensor(lo[:, c], full[:, c], f32(hi[:, c]), ALU.subtract).then_inc(lo_done, 1)
                        normalise_chunk((b + 1) % B, c)

            @block.tensor
            def _(pe):
                pe.wait_ge(silu_bc, KT)
                pe.wait_ge(ld_w, 16)
                for m in range(12):
                    for k in range(KT):
                        step = pe.matmul(ps_mod[:, m, :], wmod[:, k, m * P:(m + 1) * P], silu[:, 3, k, :],
                                         start=(k == 0), stop=(k == KT - 1))
                step.then_inc(mod_mm, 1)
                for b in range(B):
                    if b:
                        pe.wait_ge(row_ev, 6 * b)
                    for half in range(2):
                        lo_c = 3 * D + half * CH
                        hi_c = min(lo_c + CH, 6 * D)
                        for k in range(KT):
                            step = pe.matmul(ps_row[:, half, 0:hi_c - lo_c], silu_rows[:, k, b, :], wmod[:, k, lo_c:hi_c],
                                             start=(k == 0), stop=(k == KT - 1))
                    step.then_inc(row_mm, 1)
                pe.wait_ge(ld_i, 16)
                with pe.Fori(0, B) as b:
                    for c in range(NC):
                        pe.wait_ge(xn_ready, b * NC + c + 1)
                        pe.wait_ge(hi_done, at(b * NC + c - 1))
                        for t in range(CT):
                            for k in range(KT):
                                step = pe.transpose(ps_t[c][:, k, t * P:(t + 1) * P], xn[:, c, t, k * P:(k + 1) * P], ident[:])
                        step.then_inc(t_done, 1)


UNITS = [(qc, kt) for qc in range(NC) for kt in range((qc + 1) * CT)]
NU = len(UNITS)
LAG = 2
V_, Q_, K_ = range(3)
PROJ = [(V_, 0), (V_, 1), (Q_, 0), (K_, 0), (Q_, 1), (K_, 1)]
NPJ = len(PROJ)
FIRST_PROJ = 4
PROJ_AT = {1: 0, 2: 1, 6: 2, 7: 3, 9: 4, 10: 5}
VALUES_AT = {3: 0, 4: 1}
CTX_AT = 11


def phase_attention(nc, io, scr, keep):
    with ExitStack() as ctx:
        a = Allocator(nc, ctx)
        ident, modT = keep["ident"], keep["modT"]
        ident16 = a.sb("at_ident16", [P, P], F16)
        causal = a.sb("at_causal", [P, P], F16)
        bias = a.sb("at_bias", [P, 3, HP])
        bo = a.sb("at_bo", [P, KT])
        shift = a.sb("at_shift", [P, 1])
        hT = a.sb("at_hT", [P, 2, 2, KT, S], F32R)
        w_raw = a.sb("at_w_raw", [P, 3, KT, P])
        w_hi = a.sb("at_w_hi", [P, 3, KT, P], F32R)
        w_lo = a.sb("at_w_lo", [P, 3, KT, P], F32R)
        stage = a.sb("at_stage", [P, 2, CH])
        qk = [[[a.sb(f"at_{n}{i}{part}", [P, S], F16) for part in ("hi", "lo")] for n in "qk"] for i in range(2)]
        vT = [a.sb(f"at_vT_{part}", [P, S], F16) for part in ("hi", "lo")]
        v = [a.sb(f"at_v{i}", [P, TB, 2, VW], F16) for i in range(2)]
        probs = [a.sb(f"at_p{i}", [P, 2, CH]) for i in range(2)]
        p_hi = [a.sb(f"at_p_hi{i}", [P, 2, CH], F16) for i in range(2)]
        p_lo = [a.sb(f"at_p_lo{i}", [P, 2, CH], F16) for i in range(2)]
        rsum = a.sb("at_rsum", [P, 2, CT])
        ctx_tok = a.sb("at_ctx_tok", [P, CT, 2, DH])
        cT_hi = a.sb("at_cT_hi", [P, HP, S], F32R)
        cT_lo = a.sb("at_cT_lo", [P, HP, S], F32R)
        xio = a.sb("at_xio", [P, TB, D])
        wo_hi = a.sb("at_wo_hi", [P, HP, D], F32R)
        wo_lo = a.sb("at_wo_lo", [P, HP, D], F32R)
        y = a.sb("at_y", [P, KT, CH])
        ps_s = [a.ps(f"at_ps_s{i}", [P, 2, CH]) for i in range(2)]
        ps_o = a.ps("at_ps_o", [P, 2, CH])
        ps_m = [a.ps(f"at_ps_m{i}", [P, CH]) for i in range(2)]
        ps_m16 = [m[:].bitcast(F16).rearrange("p (t h d) -> p t h d", t=TB, h=2) for m in ps_m]
        (ld_const, ld_wo, ld_hT, ld_w, ld_x, st_x, const_done, wo_done, sc_done, pv_done, pj_mm, vt_mm, ct_mm, op_mm, yt_mm,
         exp_done, pj_full, vt_hi, ct_hi, y_done, p_hi_done, pj_hi, wh_done, p_lo_done, pj_lo, wl_done, r_done, cx_done,
         vt_lo, ct_lo, yg_done, x1_done, tick) = a.sems(
            "at_", "ld_const ld_wo ld_hT ld_w ld_x st_x const_done wo_done sc_done pv_done pj_mm vt_mm ct_mm op_mm yt_mm "
            "exp_done pj_full vt_hi ct_hi y_done p_hi_done pj_hi wh_done p_lo_done pj_lo wl_done r_done cx_done "
            "vt_lo ct_lo yg_done x1_done tick")
        w_dram = [io[n].rearrange("(k p) n -> p k n", p=P) for n in ("Wv", "Wq", "Wk")]

        def o_view():
            return ps_o[:, :, 0:CT * (DH + 1)].rearrange("p h (t c) -> p h t c", c=DH + 1)

        with nc.Block() as block:

            @block.sync
            def _(sp):
                def load_hT(b):
                    for part, name in enumerate(("hT_hi", "hT_lo")):
                        sp.dma_start(f32(hT[:, b % 2, part]), scr[name][b % B]).then_inc(ld_hT, 16)

                def load_w(n):
                    for i in range(3):
                        sp.dma_start(w_raw[:, i], w_dram[i][:, :, ds((n % HP) * P, P)]).then_inc(ld_w, 16)

                load_w(0)
                load_hT(0)
                sp.dma_start(ident16[:], io["ident16"]).then_inc(ld_const, 16)
                sp.dma_start(causal[:], io["causal16"]).then_inc(ld_const, 16)
                sp.dma_start(bias[:], io["b_vqk"]).then_inc(ld_const, 16)
                sp.dma_start(bo[:], io["bo_col"]).then_inc(ld_const, 16)
                sp.wait_ge(wh_done, at(1))
                sp.wait_ge(wl_done, at(1))
                load_w(1)
                sp.dma_start(xio[:], io["Wo"].rearrange("(h p) n -> p h n", p=P)).then_inc(ld_wo, 16)
                sp.wait_ge(wo_done, 2)
                with sp.Fori(0, B) as b:
                    hold(sp, tick, (pj_mm, at(NPJ * HP * b)))
                    load_hT(b + 1)
                    sp.dma_start(xio[:], io["states"][b].rearrange("(t p) d -> p t d", p=P)).then_inc(ld_x, 16)
                    with sp.Fori(0, HP) as j:
                        hold(sp, tick, (wh_done, at(b * HP + j + 2)), (wl_done, at(b * HP + j + 2)))
                        load_w(b * HP + j + 2)
                    hold(sp, tick, (x1_done, at(NC * (b + 1))))
                    sp.dma_start(scr["x1"][b].rearrange("(t p) d -> p t d", p=P), xio[:]).then_inc(st_x, 16)
                    hold(sp, tick, (st_x, 16 * b + 16))

            @block.gpsimd
            def _(pool):
                pool.sem_inc(pj_lo, CREDIT)
                pool.memset(shift[:], SCORE_SHIFT).then_inc(const_done, 1)
                for i in range(2):
                    pool.memset(v[i][:, :, :, DH:DH + 2], 1.0).then_inc(const_done, 1)

                def split_projection(base, i, dst):
                    w, c = PROJ[i]
                    cols = slice(c * CH, (c + 1) * CH)
                    hi, lo = vT if w == V_ else qk[dst][w - 1]
                    hold(pool, tick, (pj_hi, at(base + i + 1)))
                    pool.tensor_tensor(lo[:, cols], stage[:, i % 2, :], hi[:, cols], ALU.subtract).then_inc(pj_lo, 1)

                for i in range(NPJ):
                    split_projection(0, i, 0)
                with pool.Fori(0, B) as b, pool.Fori(0, HP // 2) as j:
                    for par in range(2):
                        it = b * HP + j * 2 + par
                        for i in range(NPJ):
                            split_projection(NPJ * (it + 1), i, 1 - par)

            @block.vector
            def _(dve):
                for s in (p_hi_done, p_lo_done, wl_done, r_done, cx_done, vt_lo, ct_lo, yg_done, x1_done):
                    dve.sem_inc(s, CREDIT)

                def split_weights(n):
                    dve.wait_ge(wh_done, at(n + 1))
                    dve.tensor_tensor(w_lo[:], w_raw[:], f32(w_hi[:]), ALU.subtract).then_inc(wl_done, 1)

                def low_values(n, dst):
                    dve.wait_ge(vt_mm, 2 * n + 2)
                    dve.tensor_copy(v[dst][:, :, :, DH + 2:VW], ps_m16[0]).then_inc(vt_lo, 1)

                def normalise(n, count):
                    dve.wait_ge(pv_done, at(count))
                    dve.reciprocal(rsum[:], o_view()[:, :, :, DH]).then_inc(r_done, 1)
                    dve.wait_ge(r_done, at(n + 1))
                    dve.tensor_tensor(ctx_tok[:].rearrange("p t h d -> p h t d"), o_view()[:, :, :, 0:DH],
                                      rsum[:].unsqueeze(3).broadcast_to([P, 2, CT, DH]), ALU.mult).then_inc(cx_done, 1)

                def low_context(n, hp, c):
                    dve.wait_ge(ct_hi, at(n + 1))
                    cols = slice(c * CH, (c + 1) * CH)
                    dve.tensor_tensor(cT_lo[:, hp, cols], ps_m[c][:], f32(cT_hi[:, hp, cols]), ALU.subtract).then_inc(ct_lo, 1)

                split_weights(0)
                dve.wait_ge(pj_mm, at(NPJ))
                split_weights(1)
                dve.wait_ge(const_done, 3)
                low_values(0, 0)
                dve.wait_ge(wo_done, 1)
                dve.tensor_tensor(wo_lo[:], xio[:], f32(wo_hi[:]), ALU.subtract).then_inc(wo_done, 1)
                with dve.Fori(0, B) as b:
                    with dve.Fori(0, HP // 2) as j:
                        for par in range(2):
                            hp = j * 2 + par
                            it = b * HP + hp
                            for u, (qc, kt) in enumerate(UNITS):
                                off = max(0, kt * P - qc * CH)
                                dve.wait_ge(exp_done, at(it * NU + u + 1))
                                dve.wait_ge(pv_done, at(it * NU + u - 1))
                                dve.tensor_copy(p_hi[u % 2][:, :, off:], probs[u % 2][:, :, off:]).then_inc(p_hi_done, 1)
                                if u == CT - 1 + LAG:
                                    normalise(it * NC, it * NU + CT)
                                dve.wait_ge(p_hi_done, at(it * NU + u + 1))
                                dve.tensor_tensor(p_lo[u % 2][:, :, off:], probs[u % 2][:, :, off:],
                                                  p_hi[u % 2][:, :, off:], ALU.subtract).then_inc(p_lo_done, 1)
                                if VALUES_AT.get(u) == 1:
                                    low_values(it + 1, 1 - par)
                                if u == CTX_AT:
                                    low_context(it * NC, hp, 0)
                            normalise(it * NC + 1, it * NU + NU)
                            split_weights(it + 2)
                            low_context(it * NC + 1, hp, 1)
                    for c in range(NC):
                        for m in range(KT):
                            dve.wait_ge(y_done, at(b * NC * KT + c * KT + m + 1))
                            dve.tensor_scalar(y[:, m, :], y[:, m, :], modT[:, 2 * KT + m, ds(b, 1)], None,
                                              ALU.mult).then_inc(yg_done, 1)
                        if c == 0:
                            dve.wait_ge(ld_x, 16 * b + 16)
                        dve.wait_ge(yt_mm, at(b * NC + c + 1))
                        tiles = slice(c * CT, (c + 1) * CT)
                        dve.tensor_tensor(xio[:, tiles, :], xio[:, tiles, :],
                                          (ps_s[1], ps_o)[c][:].rearrange("p h (t d) -> p (h t) d", d=D), ALU.add).then_inc(x1_done, 1)

            @block.scalar
            def _(act):
                for s in (exp_done, pj_full, pj_hi, vt_hi, ct_hi, y_done, wh_done):
                    act.sem_inc(s, CREDIT)

                def split_weights(n):
                    hold(act, tick, (ld_w, 48 * n + 48), (pj_mm, at(NPJ * n)))
                    act.activation(w_hi[:], w_raw[:], ACT.Copy).then_inc(wh_done, 1)

                def project(base, i, hp, dst):
                    w, c = PROJ[i]
                    hold(act, tick, (pj_mm, at(base + i + 1)), (pj_lo, at(base + i - 1)))
                    act.activation(stage[:, i % 2, :], ps_m[i % 2][:], ACT.Tanh, bias=bias[:, w, ds(hp, 1)]).then_inc(pj_full, 1)
                    hi = vT[0] if w == V_ else qk[dst][w - 1][0]
                    act.activation(hi[:, c * CH:(c + 1) * CH], ps_m[i % 2][:], ACT.Tanh,
                                   bias=bias[:, w, ds(hp, 1)]).then_inc(pj_hi, 1)

                def high_values(n, dst):
                    act.wait_ge(vt_mm, 2 * n + 1)
                    act.activation(v[dst][:, :, :, 0:DH], ps_m16[1], ACT.Copy).then_inc(vt_hi, 1)

                def high_context(n, hp, c):
                    hold(act, tick, (ct_mm, n + 1))
                    act.activation(cT_hi[:, hp, c * CH:(c + 1) * CH], ps_m[c][:], ACT.Copy).then_inc(ct_hi, 1)

                split_weights(0)
                act.wait_ge(ld_const, 16 * 4)
                for i in range(NPJ):
                    project(0, i, 0, 0)
                split_weights(1)
                act.wait_ge(const_done, 3)
                high_values(0, 0)
                act.wait_ge(ld_wo, 16)
                act.activation(wo_hi[:], xio[:], ACT.Copy).then_inc(wo_done, 1)
                with act.Fori(0, B) as b:
                    with act.Fori(0, HP // 2) as j:
                        for par in range(2):
                            hp = j * 2 + par
                            it = b * HP + hp
                            for u, (qc, kt) in enumerate(UNITS):
                                off = max(0, kt * P - qc * CH)
                                act.wait_ge(sc_done, it * NU + u + 1)
                                act.wait_ge(p_lo_done, at(it * NU + u - 1))
                                act.activation(probs[u % 2][:, :, off:], ps_s[u % 2][:, :, off:], ACT.Exp,
                                               bias=shift[:], scale=SCORE_SCALE).then_inc(exp_done, 1)
                                if u in PROJ_AT:
                                    project(NPJ * (it + 1), PROJ_AT[u], (hp + 1) % HP, 1 - par)
                                if VALUES_AT.get(u) == 0:
                                    high_values(it + 1, 1 - par)
                                if u == CTX_AT:
                                    split_weights(it + 2)
                                    high_context(it * NC, hp, 0)
                            high_context(it * NC + 1, hp, 1)
                    for c in range(NC):
                        for m in range(KT):
                            act.wait_ge(op_mm, b * NC * KT + c * KT + m + 1)
                            if m == 0:
                                act.wait_ge(yt_mm, at(b * NC + c))
                            act.activation(y[:, m, :], (ps_s[1], ps_o)[c][:, m, :], ACT.Tanh, bias=bo[:, m:m + 1]).then_inc(y_done, 1)

            @block.tensor
            def _(pe):
                for s in (pv_done, pj_mm, yt_mm):
                    pe.sem_inc(s, CREDIT)

                def project(i, buf):
                    w, c = PROJ[i]
                    cols = slice(c * CH, (c + 1) * CH)
                    for k in range(KT):
                        step = three_products(pe, ps_m[i % 2][:], w_hi[:, w, k, :], w_lo[:, w, k, :],
                                              hT[:, buf, 0, k, cols], hT[:, buf, 1, k, cols], k == 0, k == KT - 1)
                    step.then_inc(pj_mm, 1)

                def values(part, base):
                    pe.wait_ge(pj_lo if part else pj_hi, at(base + NC))
                    for t in range(TB):
                        step = pe.transpose(ps_m16[1 - part][:, t, :, :].rearrange("p h d -> p (h d)"),
                                            vT[part][:, t * P:(t + 1) * P], ident16[:])
                    step.then_inc(vt_mm, 1)

                def scores(par, u):
                    qc, kt = UNITS[u]
                    off = max(0, kt * P - qc * CH)
                    cols = slice(qc * CH + off, (qc + 1) * CH)
                    diagonal = kt * P >= qc * CH
                    (q_hi, q_lo), (k_hi, k_lo) = qk[par]
                    keys = slice(kt * P, (kt + 1) * P)
                    pairs = [(k_hi, q_hi), (k_hi, q_lo), (k_lo, q_hi)]
                    for n, (kx, qx) in enumerate(pairs):
                        for h in range(2):
                            rows = slice(h * DH, (h + 1) * DH)
                            step = pe.matmul(ps_s[u % 2][:, h, off:], kx[rows, keys], qx[rows, cols], start=(n == 0),
                                             stop=(n == 2 and not diagonal), skip_group_check=True)
                    if diagonal:
                        for h in range(2):
                            step = pe.matmul(ps_s[u % 2][:, h, off:off + P], ident16[:], causal[:], start=False, stop=True,
                                             skip_group_check=True)
                    step.then_inc(sc_done, 1)

                def value_products(par, u):
                    qc, kt = UNITS[u]
                    first = max(0, kt - qc * CT)
                    for h in range(2):
                        ones_hi, lo = v[par][:, kt, h, 0:DH + 1], v[par][:, kt, h, DH + 2:VW]
                        for t in range(first, CT):
                            ph, pl = (p[u % 2][:, h, t * P:(t + 1) * P] for p in (p_hi, p_lo))
                            out = ps_o[:, h, t * (DH + 1):(t + 1) * (DH + 1)]
                            pe.matmul(out, ph, ones_hi, start=(kt == 0 and t == 0), stop=False, skip_group_check=True)
                            pe.matmul(out[:, 0:DH], ph, lo, start=False, stop=False, skip_group_check=True)
                            step = pe.matmul(out, pl, ones_hi, start=False, stop=(kt == qc * CT + t), skip_group_check=True)
                    step.then_inc(pv_done, 1)

                def context(n, c):
                    pe.wait_ge(cx_done, at(n + 1))
                    for t in range(CT):
                        step = pe.transpose(ps_m[c][:, t * P:(t + 1) * P], ctx_tok[:, t].rearrange("p h d -> p (h d)"),
                                            ident[:])
                    step.then_inc(ct_mm, 1)

                def output_T(b, c):
                    pe.wait_ge(yg_done, at(b * NC * KT + (c + 1) * KT))
                    for t in range(CT):
                        for m in range(KT):
                            step = pe.transpose((ps_s[1], ps_o)[c][:, t // 2, (t % 2) * D + m * P:(t % 2) * D + (m + 1) * P],
                                                y[:, m, t * P:(t + 1) * P], ident[:])
                    step.then_inc(yt_mm, 1)

                pe.wait_ge(ld_hT, 32)
                pe.wait_ge(wl_done, at(1))
                for i in range(NPJ):
                    if i >= 2:
                        pe.wait_ge(pj_hi, at(i - 1))
                    project(i, 0)
                pe.wait_ge(ld_const, 16 * 4)
                pe.wait_ge(pj_hi, at(NPJ))
                values(0, 0)
                values(1, 0)
                pe.wait_ge(pj_lo, at(FIRST_PROJ))
                scores(0, 0)
                with pe.Fori(0, B) as b:
                    with pe.Fori(0, HP // 2) as j:
                        for par in range(2):
                            it = b * HP + j * 2 + par
                            nxt = it + 1
                            buf = (nxt // HP) % 2
                            base = NPJ * nxt
                            for s in range(1, NU + LAG):
                                if s < NU:
                                    if s == 1:
                                        pe.wait_ge(x1_done, at(b * NC - 1))
                                    if s == CT:
                                        pe.wait_ge(pj_lo, at(base))
                                    pe.wait_ge(exp_done, at(it * NU + s - 1))
                                    scores(par, s)
                                if s in PROJ_AT:
                                    i = PROJ_AT[s]
                                    if i == 0:
                                        pe.wait_ge(ld_hT, 32 * (nxt // HP) + 32)
                                        pe.wait_ge(wl_done, at(nxt + 1))
                                        pe.wait_ge(vt_lo, at(it + 1))
                                        pe.wait_ge(ct_lo, at(NC * it - 1))
                                    elif i == 1:
                                        pe.wait_ge(vt_hi, at(it + 1))
                                        pe.wait_ge(ct_lo, at(NC * it))
                                    elif i == 2:
                                        pe.wait_ge(vt_lo, at(it + 2))
                                    elif i == 3:
                                        pe.wait_ge(vt_hi, at(it + 2))
                                    else:
                                        pe.wait_ge(pj_hi, at(base + i - 1))
                                    project(i, buf)
                                if s in VALUES_AT:
                                    values(VALUES_AT[s], base)
                                if s == CTX_AT:
                                    pe.wait_ge(pj_hi, at(base + 5))
                                    context(it * NC, 0)
                                if s >= LAG:
                                    u = s - LAG
                                    if u == 0:
                                        pe.wait_ge(vt_hi, at(it + 1))
                                        pe.wait_ge(vt_lo, at(it + 1))
                                        pe.wait_ge(cx_done, at(it * NC))
                                        pe.wait_ge(x1_done, at(b * NC))
                                    if u == CT:
                                        pe.wait_ge(cx_done, at(it * NC + 1))
                                    pe.wait_ge(p_lo_done, at(it * NU + u + 1))
                                    value_products(par, u)
                            pe.wait_ge(pj_lo, at(base + FIRST_PROJ))
                            pe.wait_ge(exp_done, at(it * NU + NU - 1))
                            scores(1 - par, 0)
                            pe.wait_ge(pj_hi, at(base + NPJ))
                            context(it * NC + 1, 1)
                    pe.wait_ge(exp_done, at((b + 1) * HP * NU))
                    pe.wait_ge(wo_done, 2)
                    for c in range(NC):
                        pe.wait_ge(ct_lo, at((b + 1) * HP * NC - 1 + c))
                        for m in range(KT):
                            outs = slice(m * P, (m + 1) * P)
                            for hp in range(HP):
                                step = three_products(pe, (ps_s[1], ps_o)[c][:, m, :], wo_hi[:, hp, outs], wo_lo[:, hp, outs],
                                                      cT_hi[:, hp, c * CH:(c + 1) * CH], cT_lo[:, hp, c * CH:(c + 1) * CH],
                                                      hp == 0, hp == HP - 1)
                            step.then_inc(op_mm, 1)
                            if (c, m) in ((1, 0), (1, 1)):
                                output_T(b, m)

POOL_BATCHES = (1,)


def phase_output(nc, io, scr, keep):
    with ExitStack() as ctx:
        a = Allocator(nc, ctx)
        h, modB = keep["stream"], keep["modB"]
        x1 = a.sb("out_x1", [P, NT, D])
        gated, added, added_pool, stored = a.sems("out_", "gated added added_pool stored")
        ld = [a.sems("out_", f"ld{b}")[0] for b in range(B)]
        with nc.Block() as block:

            @block.sync
            def _(sp):
                for b in range(B):
                    sp.dma_start(x1[:, b * TB:(b + 1) * TB, :],
                                 scr["x1"][b].rearrange("(t p) d -> p t d", p=P)).then_inc(ld[b], 16)
                for b in range(B):
                    sp.wait_ge(added_pool if b in POOL_BATCHES else added, sum(1 for i in range(b + 1) if (i in POOL_BATCHES) == (b in POOL_BATCHES)))
                    sp.dma_start(io["out"][b].rearrange("(t p) d -> p t d", p=P),
                                 h[:, b * TB:(b + 1) * TB, :]).then_inc(stored, 16)
                sp.wait_ge(stored, 16 * B)

            @block.vector
            def _(dve):
                for b in range(B):
                    part = h[:, b * TB:(b + 1) * TB, :]
                    gb = modB[:, b, 2 * D:3 * D].unsqueeze(1).broadcast_to([P, TB, D])
                    dve.tensor_tensor(part, part, gb, ALU.mult).then_inc(gated, 1)
                for b in range(B):
                    if b not in POOL_BATCHES:
                        part = h[:, b * TB:(b + 1) * TB, :]
                        dve.wait_ge(gated, b + 1)
                        dve.wait_ge(ld[b], 16)
                        dve.tensor_tensor(part, part, x1[:, b * TB:(b + 1) * TB, :], ALU.add).then_inc(added, 1)

            @block.gpsimd
            def _(pool):
                for b in POOL_BATCHES:
                    part = h[:, b * TB:(b + 1) * TB, :]
                    pool.wait_ge(gated, b + 1)
                    pool.wait_ge(ld[b], 16)
                    pool.tensor_tensor(part, part, x1[:, b * TB:(b + 1) * TB, :], ALU.add).then_inc(added_pool, 1)


L = 2
LH = 8
LP = LH // 2
INNER = LH * DH
HID = D * 4 * 2 // 3
HT = -(-HID // P)
QK_SCALE = 8.0
NORM_FLOOR = 1e-12
NCH = NT // CT
V_RING = 4


def phase_layers(nc, io, scr, keep):
    with ExitStack() as ctx:
        a = Allocator(nc, ctx)
        x, ident, modB = keep["stream"], keep["ident"], keep["modB"]
        raw = a.sb("ly_raw", [P, 6144])
        w_hi = a.sb("ly_w_hi", [P, 4608], F32R)
        w_lo = a.sb("ly_w_lo", [P, 4608], F32R)
        opnd = a.sb("ly_operands", [P, 9232], F32R)
        rope = a.sb("ly_rope", [P, 4, TB, DH])
        rows = a.sb("ly_rows", [P, 4, DH])
        lncol = a.sb("ly_ln", [P, 2, KT])
        b1 = a.sb("ly_b1", [P, 2 * HT])
        b2 = a.sb("ly_b2", [P, D])
        prev_mask = a.sb("ly_prev_mask", [P, TB // 2, P])
        mask = a.sb("ly_mask", [P, 2, 2, P])
        carry = a.sb("ly_carry", [P, 2, TB + 1], F32R)
        shifted = a.sb("ly_shifted", [P, NT, P])
        expo = a.sb("ly_expo", [P, LH])
        sq = a.sb("ly_sq", [P, 2, INNER])
        norm2 = a.sb("ly_norm2", [P, 2, 2, LH])
        rq = a.sb("ly_rq", [P, 2, LH])
        rk = a.sb("ly_rk", [P, LH])
        kn = a.sb("ly_kn", [P, INNER])
        xs = a.sb("ly_xs", [P, 2, D])
        ra = a.sb("ly_rope_a", [P, 2, INNER])
        rt = a.sb("ly_rope_t", [P, 2, INNER])
        sm = a.sb("ly_masked", [P, 2, 2, 2 * P])
        pr = a.sb("ly_probs", [P, 2, 2, 2 * P])
        small = a.sb("ly_small", [P, 2, 2, 2])
        sums = a.sb("ly_sums", [P, 2, LH])
        rsum = a.sb("ly_rsum", [P, LH])
        vv = a.sb("ly_values", [P, V_RING, INNER])
        pT = a.sb("ly_probs_T", [P, 4 * P])
        on = a.sb("ly_on", [P, INNER])
        def cut(start, *shape):
            n = int(np.prod(shape))
            names = "abcd"[:len(shape)]
            v = opnd[:, start:start + n]
            if len(shape) > 1:
                v = v.rearrange(f"p ({' '.join(names)}) -> p {' '.join(names)}", **dict(zip(names, shape)))
            return v, start + n
        hT, o = cut(0, 2, 2, KT, P + 1)
        qT, o = cut(o + o % 2, 2, 2, LP, P)
        kT, o = cut(o, 2, LP, 2 * P)
        oT, o = cut(o, 2, LP, P)
        assert o <= 9232
        fT_hi, o = cut(0, 2, KT, CH)
        fT_lo, o = cut(o, KT, CH)
        uT, o = cut(o, 2, HT, CH)
        assert o <= 9232
        warm = a.sb("ly_warm", [P, 1])
        st = a.sb("ly_st", [P, CT, 12])
        mv = a.sb("ly_mv", [P, CT, 2])
        nrm = a.sb("ly_nrm", [P, 3, CT])
        xn = sq[:].rearrange("p a (b d) -> p (a b) d", d=D)
        ffull = ra
        gl = pr[:].rearrange("p a b c -> p a (b c)")
        uf = rt
        bank = [a.ps(f"ly_ps{i}", [P, CH]) for i in range(8)]
        ps_qkv, ps_s, ps_pt, ps_misc, ps_pv = bank[0:3], bank[3:5], bank[5], bank[6], bank[7]
        wqkv = [w[:, 0:KT * 3 * INNER].rearrange("p (k n) -> p k n", k=KT) for w in (w_hi, w_lo)]
        wo = [w[:, KT * 3 * INNER:KT * 3 * INNER + LP * D].rearrange("p (k n) -> p k n", k=LP) for w in (w_hi, w_lo)]
        w1 = [w[:, 0:KT * 2 * HT * P].rearrange("p (k n) -> p k n", k=KT) for w in (w_hi, w_lo)]
        w2 = [w[:, KT * 2 * HT * P:KT * 2 * HT * P + HT * D].rearrange("p (k n) -> p k n", k=HT) for w in (w_hi, w_lo)]
        A_COLS, F_COLS = KT * 3 * INNER + LP * D, KT * 2 * HT * P + HT * D
        T_COLS = 4 * TB * DH
        qkv_cols = slice(0, KT * 3 * INNER)
        flat = sm[:].rearrange("p a b c -> p (a b c)")
        st0 = flat[:, 0:6 * NT].rearrange("p (n c) -> p n c", c=6)
        tmp0 = flat[:, 6 * NT:10 * NT].rearrange("p (c n) -> p c n", c=4)
        col0 = flat[:, 10 * NT:15 * NT].rearrange("p (c n) -> p c n", c=5)
        ld_x1 = [a.sems("ly_", f"ld_x1_{b}")[0] for b in range(B)]
        n0_bn, n0_chain, n0_var, n0_std, n0_norm, n0_xn, n0_scaled, n0_first, n0_added = a.sems(
            "ly_n0_", "bn chain var std norm xn scaled first added")
        names = ("ld_const ld_attn ld_ffn shift_in const_done zeroed "
                 "w_hi_done w_lo_done rope_q "
                 "xT_mm qkv_mm sc_mm pt_mm pv_mm qkT_mm oT_mm wo_mm "
                 "h_hi ex_done sq_done pt_done o_hi qkT_hi v_done "
                 "mx_done nb_done h_lo rc_done on_done red_done fl_done ra_done kn_done o_lo qkT_lo xa_done msk "
                 "ca_in ca_out pw_done add_done xs_done "
                 "warmed bn ag vr nr xnd fT_mm ff_done f_hi f_lo gu_mm gl_done uf_done u_hi u_lo y_mm ya_done pw2 b2_done tick")
        s = dict(zip(names.split(), a.sems("ly_", names)))
        PE_SEMS = "xT_mm qkv_mm sc_mm pt_mm pv_mm qkT_mm oT_mm wo_mm fT_mm gu_mm y_mm"
        ACT_SEMS = "h_hi ex_done sq_done pt_done o_hi qkT_hi v_done w_hi_done warmed ff_done f_hi gl_done"
        DVE_SEMS = ("mx_done nb_done h_lo rc_done on_done red_done fl_done ra_done kn_done o_lo qkT_lo xa_done msk "
                    "w_lo_done rope_q bn ag vr nr xnd f_lo uf_done u_lo ya_done")
        POOL_SEMS = "xs_done ca_in ca_out pw_done add_done u_hi pw2 b2_done"

        def start(eng, which):
            for n in which.split():
                eng.sem_inc(s[n], CREDIT)

        def after(eng, name, n):
            eng.wait_ge(s[name], at(n))

        def nth(l, t):
            return l * NT + t

        def nth_rotated(l, t):
            return l * (NT + 1) + t

        def nth_projected(l, t):
            return l * (NT + 2) + t

        def nth_transposed(l, t):
            return l * (NT + 3) + t

        def nth_staged(l, t):
            return l * (NT + 4) + t

        def nth_scores(l, t, j):
            return l * (LP * NT + 2) + LP * t + j

        def nth_norm(l, c):
            return l * (NCH + 1) + c

        with nc.Block() as block:

            @block.sync
            def _(sp):
                for b in range(B):
                    sp.dma_start(x[:, b * TB:(b + 1) * TB, :],
                                 scr["x1"][b].rearrange("(t p) d -> p t d", p=P)).then_inc(ld_x1[b], 16)
                sp.dma_start(prev_mask[:], io["prev_mask"]).then_inc(s["ld_const"], 16)
                sp.dma_start(mask[:], io["mask"]).then_inc(s["ld_const"], 16)
                with sp.Fori(0, L) as l:
                    hold(sp, s["tick"], (s["w_lo_done"], at(4 * l)))
                    hold(sp, s["tick"], (s["rope_q"], at(4 * l)))
                    sp.dma_start(raw[:, qkv_cols].rearrange("p (k n) -> p k n", k=KT),
                                 io["ffn_wqkv"][l].rearrange("(k p) n -> p k n", p=P)).then_inc(s["ld_attn"], 16)
                    sp.dma_start(raw[:, KT * 3 * INNER:A_COLS].rearrange("p (k n) -> p k n", k=LP),
                                 io["ffn_wo"][l].rearrange("(k p) n -> p k n", p=P)).then_inc(s["ld_attn"], 16)
                    sp.dma_start(raw[:, A_COLS:A_COLS + T_COLS], io["rope"]).then_inc(s["ld_attn"], 16)
                    sp.dma_start(rows[:], io["qk_rows"][l].partition_broadcast(P)).then_inc(s["ld_attn"], 16)
                    hold(sp, s["tick"], (s["ya_done"], at(NCH * l)))
                    hold(sp, s["tick"], (s["w_lo_done"], at(4 * l + 2)))
                    hold(sp, s["tick"], (s["rope_q"], at(4 * l + 4)))
                    sp.dma_start(raw[:, 0:KT * 2 * HT * P].rearrange("p (k n) -> p k n", k=KT),
                                 io["w1"][l].rearrange("(k p) a n -> p k (a n)", p=P)).then_inc(s["ld_ffn"], 16)
                    sp.dma_start(raw[:, KT * 2 * HT * P:F_COLS].rearrange("p (k n) -> p k n", k=HT),
                                 io["w2"][l].rearrange("(k p) n -> p k n", p=P)).then_inc(s["ld_ffn"], 16)
                    sp.dma_start(lncol[:], io["ln_col"][l]).then_inc(s["ld_ffn"], 16)
                    sp.dma_start(b1[:], io["b1_col"][l]).then_inc(s["ld_ffn"], 16)
                    sp.dma_start(b2[:], io["ffn_b2"][l].partition_broadcast(P)).then_inc(s["ld_ffn"], 16)
                    with sp.Fori(0, B) as b:
                        hold(sp, s["tick"], (s["xa_done"], at(l * NT + b * TB + TB)))
                        sp.dma_start(shifted[1:P, ds(b * TB, TB), :], x[0:P - 1, ds(b * TB, TB), P:D]).then_inc(s["shift_in"], 16)
                        sp.dma_start(shifted[0:1, ds(b * TB + 1, TB - 1), :],
                                     x[P - 1:P, ds(b * TB, TB - 1), P:D]).then_inc(s["shift_in"], 16)

            @block.gpsimd
            def _(pool):
                start(pool, POOL_SEMS)
                pool.memset(expo[:], -0.5).then_inc(s["const_done"], 1)
                for b in range(B):
                    pool.memset(shifted[0:1, b * TB, :], 0.0).then_inc(s["zeroed"], 1)
                for part in range(2):
                    pool.memset(f32(kT[:, part, :, P:2 * P]), 0.0).then_inc(s["zeroed"], 1)
                pool.memset(f32(carry[:]), 0.0).then_inc(s["zeroed"], 1)
                pool.memset(vv[:, V_RING - 1, :], 0.0).then_inc(s["zeroed"], 1)
                pool.wait_ge(s["const_done"], 1)
                pool.wait_ge(s["zeroed"], B + 4)
                for b in range(1, B):
                    pool.wait_ge(n0_scaled, b + 1)
                    pool.tensor_tensor(x[:, b * TB:(b + 1) * TB, :], x[:, b * TB:(b + 1) * TB, :],
                                       modB[:, b, 0:D].unsqueeze(1).broadcast_to([P, TB, D]), ALU.add).then_inc(n0_added, 1)
                pool.wait_ge(n0_first, 1)
                pool.wait_ge(n0_added, B - 1)

                def carry_over(l, t, par, w):
                    n = nth_transposed(l, t)
                    hold(pool, s["tick"], (s["qkv_mm"], at(3 * nth_projected(l, t) - 3)), (s["ca_out"], at(n)))
                    pool.tensor_copy(hT[:, par, :, 1, 0], f32(carry[:, :, ds(w, 1)]).rearrange("p a b -> p (a b)")).then_inc(s["ca_in"], 1)
                    hold(pool, s["tick"], (s["h_lo"], at(n + 1)))
                    pool.tensor_copy(carry[:, :, ds(w + 1, 1)].rearrange("p a b -> p (a b)"), f32(hT[:, par, :, 1, P])).then_inc(s["ca_out"], 1)

                def stage_tile(par, tile):
                    pool.tensor_copy(xs[:, par, :], x[:, tile, :]).then_inc(s["xs_done"], 1)

                def inverse_norms(l, t, par, extra=0):
                    n = nth_rotated(l, t)
                    hold(pool, s["tick"], (s["fl_done"], at(2 * nth_projected(l, t) + 2)), (s["kn_done"], at(n)),
                         (s["ex_done"], at(LP * (nth(l, t) - 1) + extra)))
                    pool.tensor_tensor(rk[:], norm2[:, 1, 1, :], expo[:], ALU.pow).then_inc(s["pw_done"], 1)
                    pool.tensor_tensor(rq[:, par, :], norm2[:, 0, 1, :], expo[:], ALU.pow).then_inc(s["pw_done"], 1)

                def add_rotated(l, t, i):
                    hold(pool, s["tick"], (s["ra_done"], at(6 * nth_rotated(l, t) + 3 * i + 3)))
                    pool.tensor_tensor(ra[:, i, :], ra[:, i, :], rt[:, i, :], ALU.add).then_inc(s["add_done"], 1)

                def inverse_deviation(l, c):
                    n = nth_norm(l, c)
                    hold(pool, s["tick"], (s["vr"], at(n + 1)), (s["nr"], at(n)))
                    pool.tensor_tensor(nrm[:, 1, :], nrm[:, 0, :], expo[:, 0:CT], ALU.pow).then_inc(s["pw2"], 1)

                with pool.Fori(0, L) as l:
                    hold(pool, s["tick"], (s["ya_done"], at(NCH * l)))
                    stage_tile(0, 0)
                    stage_tile(1, 1)
                    carry_over(l, 0, 0, 0)
                    stage_tile(0, 2)
                    inverse_norms(l, 0, 0, LP)
                    add_rotated(l, 0, 0)
                    add_rotated(l, 0, 1)
                    carry_over(l, 1, 1, 1)
                    stage_tile(1, 3)
                    inverse_norms(l, 1, 1)
                    carry_over(l, 2, 0, 2)
                    with pool.Fori(0, B) as b, pool.Fori(0, TB // 2) as jj:
                        for par in range(2):
                            t = b * TB + jj * 2 + par
                            add_rotated(l, t + 1, 0)
                            add_rotated(l, t + 1, 1)
                            hold(pool, s["tick"], (s["xT_mm"], at(nth_transposed(l, t + 3))))
                            stage_tile(par, (t + 4) % NT)
                            carry_over(l, t + 3, 1 - par, (jj * 2 + par + 3) % TB)
                            inverse_norms(l, t + 2, par)
                    inverse_deviation(l, 0)
                    with pool.Fori(0, NCH) as c:
                        hold(pool, s["tick"], (s["xnd"], at(nth_norm(l, c) + 1)))
                        pool.tensor_tensor(x[:, ds(c * CT, CT), :], x[:, ds(c * CT, CT), :],
                                           b2[:].unsqueeze(1).broadcast_to([P, CT, D]), ALU.add).then_inc(s["b2_done"], 1)
                        inverse_deviation(l, c + 1)

            @block.scalar
            def _(act):
                start(act, ACT_SEMS)
                for b in range(B):
                    tiles = slice(b * TB, (b + 1) * TB)
                    act.wait_ge(n0_var, b + 1)
                    act.activation(col0[:, 2, tiles], col0[:, 1, tiles], ACT.Sqrt).then_inc(n0_std, 1)
                    act.wait_ge(n0_norm, 2 * b + 2)
                    for t in range(b * TB, (b + 1) * TB):
                        act.activation(x[:, t, :], x[:, t, :], ACT.Identity, scale=col0[:, 3, t:t + 1],
                                       bias=col0[:, 4, t:t + 1]).then_inc(n0_xn, 1)
                act.wait_ge(s["ld_const"], 32)
                act.wait_ge(s["zeroed"], B + 4)

                def split_weights(n, ld, ld_n, cols):
                    hold(act, s["tick"], (s[ld], ld_n))
                    for i in range(2):
                        part = slice(i * cols // 2, (i + 1) * cols // 2)
                        act.activation(w_hi[:, part], raw[:, part], ACT.Copy).then_inc(s["w_hi_done"], 1)

                def stream_hi(l, t, par):
                    n = nth_transposed(l, t)
                    hold(act, s["tick"], (s["xT_mm"], at(n + 1)), (s["qkv_mm"], at(3 * nth_projected(l, t) - 3)), (s["ca_out"], at(n - 1)))
                    act.activation(hT[:, par, 0, 0, 0:P], ps_misc[:, 0:P], ACT.Copy)
                    act.activation(hT[:, par, 0, 1, 1:P + 1], ps_misc[:, P:2 * P], ACT.Copy).then_inc(s["h_hi"], 1)

                def squares(l, t, i):
                    n = nth_projected(l, t)
                    hold(act, s["tick"], (s["qkv_mm"], at(3 * n + 2 + i)), (s["red_done"], at(2 * n + i - 1)))
                    act.activation(sq[:, i, :], ps_qkv[i][:], ACT.Square, scale=(1 / QK_SCALE, 1.0)[i]).then_inc(s["sq_done"], 1)

                def qk_hi(l, t, par, i):
                    hold(act, s["tick"], (s["qkT_mm"], at(2 * nth_rotated(l, t) + i + 1)))
                    if i == 0:
                        act.activation(qT[:, par, 0], ps_misc[:].rearrange("p (j q) -> p j q", j=LP), ACT.Copy).then_inc(s["qkT_hi"], 1)
                    else:
                        act.activation(kT[:, 0, :, par * P:(par + 1) * P], ps_qkv[2][:].rearrange("p (j q) -> p j q", j=LP),
                                       ACT.Copy).then_inc(s["qkT_hi"], 1)

                def copy_values(l, t, slot):
                    hold(act, s["tick"], (s["qkv_mm"], at(3 * nth_projected(l, t) + 1)))
                    act.activation(vv[:, slot, :], ps_qkv[2][:], ACT.Copy).then_inc(s["v_done"], 1)

                def exps(l, t, g, j, par):
                    hold(act, s["tick"], (s["nb_done"], at(nth_scores(l, t, j) + 1)))
                    for h in range(2):
                        step = act.activation(pr[:, j % 2, h, :], sm[:, j % 2, h, :], ACT.Exp,
                                              bias=small[:, j % 2, 1, h:h + 1], scale=rq[:, par, 2 * j + h:2 * j + h + 1],
                                              accum_out=sums[:, par, 2 * j + h:2 * j + h + 1])
                    step.then_inc(s["ex_done"], 1)

                def copy_probs(g, j):
                    if j == 2:
                        after(act, "pv_mm", LP * g + j)
                    after(act, "pt_mm", LP * g + j + 1)
                    act.activation(pT[:], ps_pt[:], ACT.Copy).then_inc(s["pt_done"], 1)

                def out_hi(g):
                    hold(act, s["tick"], (s["oT_mm"], at(g + 1)), (s["wo_mm"], at(g)))
                    act.activation(oT[:, 0].rearrange("p j q -> p (j q)"), ps_pv[:], ACT.Copy).then_inc(s["o_hi"], 1)

                def chunk_full(l, c):
                    n = nth_norm(l, c)
                    hold(act, s["tick"], (s["fT_mm"], at(n + 1)), (s["f_lo"], at(n)))
                    for k in range(KT):
                        step = act.activation(ffull[:, k, :], bank[4 + k][:], ACT.Identity,
                                              scale=lncol[:, 0, k:k + 1], bias=lncol[:, 1, k:k + 1])
                    step.then_inc(s["ff_done"], 1)

                def chunk_hi(l, c, par):
                    for k in range(KT):
                        step = act.activation(fT_hi[:, par, k, :], bank[4 + k][:], ACT.Identity,
                                              scale=lncol[:, 0, k:k + 1], bias=lncol[:, 1, k:k + 1])
                    step.then_inc(s["f_hi"], 1)

                def gelu(n, i):
                    hold(act, s["tick"], (s["gu_mm"], at(2 * (n + i) + 2)), (s["uf_done"], at(n + i - 1)))
                    act.activation(gl[:, i % 2, :], bank[2 + i % 2][:], ACT.Gelu, bias=b1[:, HT + i:HT + i + 1]).then_inc(s["gl_done"], 1)

                def u_high(n, i):
                    hold(act, s["tick"], (s["uf_done"], at(n + i + 1)), (s["y_mm"], at(n)))
                    act.activation(uT[:, 0, i, :], uf[:, i % 2, :], ACT.Copy).then_inc(s["u_hi"], 1)

                with act.Fori(0, L) as l:
                    after(act, "y_mm", HT * NCH * l)
                    after(act, "f_lo", nth_norm(l, 0))
                    split_weights(0, "ld_attn", 64 * l + 64, A_COLS)
                    stream_hi(l, 0, 0)
                    squares(l, 0, 0)
                    squares(l, 0, 1)
                    copy_values(l, 0, 0)
                    qk_hi(l, 0, 0, 0)
                    qk_hi(l, 0, 0, 1)
                    stream_hi(l, 1, 1)
                    squares(l, 1, 0)
                    squares(l, 1, 1)
                    copy_values(l, 1, 1)
                    stream_hi(l, 2, 0)
                    with act.Fori(0, B) as b, act.Fori(0, TB // 2) as jj:
                        for par in range(2):
                            t = b * TB + jj * 2 + par
                            g = nth(l, t)
                            exps(l, t, g, 0, par)
                            exps(l, t, g, 1, par)
                            copy_probs(g, 0)
                            copy_values(l, t + 2, (jj * 2 + par + 2) % V_RING)
                            exps(l, t, g, 2, par)
                            copy_probs(g, 1)
                            copy_probs(g, 2)
                            exps(l, t, g, 3, par)
                            qk_hi(l, t + 1, 1 - par, 0)
                            copy_probs(g, 3)
                            qk_hi(l, t + 1, 1 - par, 1)
                            squares(l, t + 2, 0)
                            squares(l, t + 2, 1)
                            stream_hi(l, t + 3, 1 - par)
                            out_hi(g)
                    after(act, "wo_mm", NT * (l + 1))
                    after(act, "sc_mm", (LP * NT + 2) * (l + 1))
                    after(act, "ca_out", (NT + 3) * (l + 1))
                    split_weights(1, "ld_ffn", 80 * l + 80, F_COLS)
                    act.activation(warm[:], b1[:, 0:1], ACT.Gelu).then_inc(s["warmed"], 1)
                    chunk_full(l, 0)
                    chunk_hi(l, 0, 0)
                    after(act, "warmed", l + 1)
                    with act.Fori(0, NCH // 2) as cc:
                        for par in range(2):
                            c = cc * 2 + par
                            n = (l * NCH + c) * HT
                            for i in range(HT):
                                gelu(n, i)
                                if 0 < i < HT - 1:
                                    u_high(n, i - 1)
                                if i == HT - 2:
                                    chunk_full(l, c + 1)
                                    u_high(n, i)
                                    chunk_hi(l, c + 1, 1 - par)
                            u_high(n, HT - 1)

            @block.vector
            def _(dve):
                start(dve, DVE_SEMS)

                def scale_batch(b):
                    part = x[:, b * TB:(b + 1) * TB, :]
                    sb, cb = (modB[:, b, i * D:(i + 1) * D].unsqueeze(1).broadcast_to([P, TB, D]) for i in range(2))
                    dve.wait_ge(n0_xn, TB * (b + 1))
                    dve.tensor_tensor(part, part, cb, ALU.mult).then_inc(n0_scaled, 1)
                    if b == 0:
                        dve.wait_ge(n0_scaled, 1)
                        dve.tensor_tensor(part, part, sb, ALU.add).then_inc(n0_first, 1)

                for b in range(B):
                    tiles = slice(b * TB, (b + 1) * TB)
                    dve.wait_ge(ld_x1[b], 16)
                    for t in range(b * TB, (b + 1) * TB):
                        dve.bn_stats(st0[:, t, :], x[:, t, :]).then_inc(n0_bn, 1)
                    dve.wait_ge(n0_bn, TB * (b + 1))
                    variance_steps(dve, n0_chain, 5 * b, st0[:, tiles], col0[:, 0, tiles], tmp0[:, :, tiles], col0[:, 1, tiles], n0_var)
                    dve.wait_ge(n0_std, b + 1)
                    dve.reciprocal(col0[:, 3, tiles], col0[:, 2, tiles]).then_inc(n0_norm, 1)
                    dve.wait_ge(n0_norm, 2 * b + 1)
                    dve.scalar_tensor_tensor(col0[:, 4, tiles], col0[:, 0, tiles], -0.5, col0[:, 3, tiles], ALU.mult,
                                             ALU.mult).then_inc(n0_norm, 1)
                    if b:
                        scale_batch(b - 1)
                scale_batch(B - 1)
                dve.wait_ge(s["ld_const"], 32)
                dve.wait_ge(s["zeroed"], B + 4)

                def split_weights(n, cols, i):
                    part = slice(i * cols // 2, (i + 1) * cols // 2)
                    after(dve, "w_hi_done", n + i + 1)
                    dve.tensor_tensor(w_lo[:, part], raw[:, part], f32(w_hi[:, part]), ALU.subtract).then_inc(s["w_lo_done"], 1)

                def stream_lo(l, t, par):
                    after(dve, "h_hi", nth_transposed(l, t) + 1)
                    dve.tensor_tensor(hT[:, par, 1, 0, 0:P], ps_misc[:, 0:P], f32(hT[:, par, 0, 0, 0:P]), ALU.subtract)
                    dve.tensor_tensor(hT[:, par, 1, 1, 1:P + 1], ps_misc[:, P:2 * P], f32(hT[:, par, 0, 1, 1:P + 1]),
                                      ALU.subtract).then_inc(s["h_lo"], 1)

                def squared_norms(l, t, i):
                    n = 2 * nth_projected(l, t) + i
                    after(dve, "sq_done", n + 1)
                    after(dve, "pw_done", 2 * nth_projected(l, t))
                    dve.tensor_reduce(norm2[:, i, 0, :], sq[:, i, :].rearrange("p (h d) -> p h d", d=DH), AX.X, ALU.add).then_inc(s["red_done"], 1)
                    after(dve, "red_done", n + 1)
                    dve.tensor_scalar(norm2[:, i, 1, :], norm2[:, i, 0, :], (NORM_FLOOR / (QK_SCALE, 1.0)[i]) ** 2, None,
                                      ALU.max).then_inc(s["fl_done"], 1)

                def rotate(l, t, i, z, w):
                    cos, sin = rope[:, 2 * i, w, :], rope[:, 2 * i + 1, w, :]
                    zh = z.rearrange("p (h d) -> p h d", d=DH)
                    th = rt[:, i, :].rearrange("p (h d) -> p h d", d=DH)
                    half = DH // 2
                    dve.tensor_tensor(ra[:, i, :].rearrange("p (h d) -> p h d", d=DH), zh,
                                      cos.unsqueeze(1).broadcast_to([P, LH, DH]), ALU.mult).then_inc(s["ra_done"], 1)
                    for a0, b0 in ((0, half), (half, 0)):
                        dve.tensor_tensor(th[:, :, a0:a0 + half], zh[:, :, b0:b0 + half],
                                          sin[:, a0:a0 + half].unsqueeze(1).broadcast_to([P, LH, half]), ALU.mult).then_inc(s["ra_done"], 1)

                def rotate_q(l, t, w):
                    rotate(l, t, 0, ps_qkv[0][:], w)

                def rotate_k(l, t, w):
                    after(dve, "kn_done", nth_rotated(l, t) + 1)
                    rotate(l, t, 1, kn[:], w)

                def normalise_keys(l, t):
                    after(dve, "pw_done", 2 * nth_projected(l, t) + 1)
                    dve.tensor_tensor(kn[:].rearrange("p (h d) -> p h d", d=DH), ps_qkv[1][:].rearrange("p (h d) -> p h d", d=DH),
                                      rk[:].unsqueeze(2).broadcast_to([P, LH, DH]), ALU.mult).then_inc(s["kn_done"], 1)

                def qk_lo(l, t, par, i):
                    after(dve, "qkT_hi", 2 * nth_rotated(l, t) + i + 1)
                    if i == 0:
                        hi, lo, src = qT[:, par, 0], qT[:, par, 1], ps_misc
                    else:
                        hi, lo, src = kT[:, 0, :, par * P:(par + 1) * P], kT[:, 1, :, par * P:(par + 1) * P], ps_qkv[2]
                    dve.tensor_tensor(lo, src[:].rearrange("p (j q) -> p j q", j=LP), f32(hi), ALU.subtract).then_inc(s["qkT_lo"], 1)

                def maxima(l, t, g, j, par):
                    if j >= 2:
                        after(dve, "ex_done", LP * g + j - 1)
                    hold(dve, s["tick"], (s["sc_mm"], at(nth_scores(l, t, j) + 1)))
                    for h in range(2):
                        dve.tensor_tensor_reduce(sm[:, j % 2, h, :], ps_s[h][:, 0:2 * P], mask[:, par].rearrange("p a b -> p (a b)"),
                                                 1.0, -3.0e38, ALU.add, ALU.max, small[:, j % 2, 0, h:h + 1]).then_inc(s["mx_done"], 1)
                    after(dve, "mx_done", 2 * nth_scores(l, t, j) + 2)
                    dve.scalar_tensor_tensor(small[:, j % 2, 1, :], small[:, j % 2, 0, :], -1.0, rq[:, par, 2 * j:2 * j + 2],
                                             ALU.mult, ALU.mult).then_inc(s["nb_done"], 1)

                def normalise_out(g, par):
                    after(dve, "ex_done", LP * g + LP)
                    after(dve, "on_done", g)
                    dve.reciprocal(rsum[:], sums[:, par, :]).then_inc(s["rc_done"], 1)
                    after(dve, "rc_done", g + 1)
                    after(dve, "pv_mm", LP * g + LP)
                    after(dve, "oT_mm", g)
                    dve.tensor_tensor(on[:].rearrange("p (h d) -> p h d", d=DH), ps_pv[:].rearrange("p (h d) -> p h d", d=DH),
                                      rsum[:].unsqueeze(2).broadcast_to([P, LH, DH]), ALU.mult).then_inc(s["on_done"], 1)

                def out_lo(g):
                    after(dve, "o_hi", g + 1)
                    dve.tensor_tensor(oT[:, 1].rearrange("p j q -> p (j q)"), ps_pv[:], f32(oT[:, 0]).rearrange("p j q -> p (j q)"),
                                      ALU.subtract).then_inc(s["o_lo"], 1)

                def chunk_statistics(l, c, step_no, where):
                    n = nth_norm(l, c)
                    if step_no == 0:
                        after(dve, "ag", CT * n)
                        for t in range(CT):
                            dve.bn_stats(st[:, t, 0:6], x[:, where * CT + t, 0:P]).then_inc(s["bn"], 1)
                            dve.bn_stats(st[:, t, 6:12], shifted[:, where * CT + t, :]).then_inc(s["bn"], 1)
                    else:
                        after(dve, "bn", 2 * CT * (n + 1))
                        after(dve, "nr", n)
                        dve.sem_inc(s["tick"], 1)
                        for t in range(CT):
                            dve.bn_aggr(mv[:, t, :], st[:, t, :]).then_inc(s["ag"], 1)
                        after(dve, "ag", CT * (n + 1))
                        dve.tensor_scalar(nrm[:, 0, :], mv[:, :, 1], EPS, None, ALU.add).then_inc(s["vr"], 1)

                def chunk_normalise(l, c, where):
                    n = nth_norm(l, c)
                    after(dve, "pw2", n + 1)
                    dve.scalar_tensor_tensor(nrm[:, 2, :], mv[:, :, 0], -1.0, nrm[:, 1, :], ALU.mult, ALU.mult).then_inc(s["nr"], 1)
                    after(dve, "nr", n + 1)
                    after(dve, "fT_mm", n)
                    for t in range(CT):
                        for k, src in enumerate((x[:, where * CT + t, 0:P], shifted[:, where * CT + t, :])):
                            step = dve.tensor_scalar(xn[:, t, k * P:(k + 1) * P], src, nrm[:, 1, t:t + 1], nrm[:, 2, t:t + 1],
                                                     ALU.mult, ALU.add)
                    step.then_inc(s["xnd"], 1)

                def chunk_lo(l, c, par):
                    after(dve, "f_hi", nth_norm(l, c) + 1)
                    after(dve, "gu_mm", 2 * HT * (l * NCH + c))
                    dve.tensor_tensor(fT_lo[:], ffull[:], f32(fT_hi[:, par]), ALU.subtract).then_inc(s["f_lo"], 1)

                def hidden_full(n, i):
                    after(dve, "gl_done", n + i + 1)
                    after(dve, "u_lo", n + i - 1)
                    dve.scalar_tensor_tensor(uf[:, i % 2, :], bank[i % 2][:], b1[:, i:i + 1], gl[:, i % 2, :],
                                             ALU.add, ALU.mult).then_inc(s["uf_done"], 1)

                def hidden_lo(n, i):
                    after(dve, "u_hi", n + i + 1)
                    dve.tensor_tensor(uT[:, 1, i, :], uf[:, i % 2, :], f32(uT[:, 0, i, :]), ALU.subtract).then_inc(s["u_lo"], 1)

                with dve.Fori(0, L) as l:
                    after(dve, "f_lo", nth_norm(l, 0))
                    split_weights(4 * l, A_COLS, 0)
                    split_weights(4 * l, A_COLS, 1)
                    stream_lo(l, 0, 0)
                    for i in range(4):
                        dve.tensor_tensor(rope[:, i], raw[:, A_COLS + i * TB * DH:A_COLS + (i + 1) * TB * DH].rearrange("p (t d) -> p t d", d=DH),
                                          rows[:, i, :].unsqueeze(1).broadcast_to([P, TB, DH]), ALU.mult).then_inc(s["rope_q"], 1)
                    after(dve, "rope_q", 4 * l + 4)
                    squared_norms(l, 0, 0)
                    squared_norms(l, 0, 1)
                    rotate_q(l, 0, 0)
                    normalise_keys(l, 0)
                    rotate_k(l, 0, 0)
                    qk_lo(l, 0, 0, 0)
                    qk_lo(l, 0, 0, 1)
                    stream_lo(l, 1, 1)
                    squared_norms(l, 1, 0)
                    squared_norms(l, 1, 1)
                    stream_lo(l, 2, 0)
                    after(dve, "msk", (NT // 2 + 1) * l)
                    dve.tensor_copy(mask[:, 0, 1, :], prev_mask[:, 0, :]).then_inc(s["msk"], 1)
                    after(dve, "msk", (NT // 2 + 1) * l + 1)
                    maxima(l, 0, nth(l, 0), 0, 0)
                    maxima(l, 0, nth(l, 0), 1, 0)
                    dve.sem_inc(s["tick"], 1)
                    with dve.Fori(0, B) as b, dve.Fori(0, TB // 2) as jj:
                        for par in range(2):
                            t = b * TB + jj * 2 + par
                            g = nth(l, t)
                            w = (jj * 2 + par + 1) % TB
                            rotate_q(l, t + 1, w)
                            maxima(l, t, g, 2, par)
                            normalise_keys(l, t + 1)
                            rotate_k(l, t + 1, w)
                            if par == 1:
                                m = (NT // 2 + 1) * l + b * (TB // 2) + jj + 1
                                after(dve, "msk", m)
                                dve.tensor_copy(mask[:, 0, 1, :], prev_mask[:, (jj + 1) % (TB // 2), :]).then_inc(s["msk"], 1)
                                after(dve, "msk", m + 1)
                            maxima(l, t, g, 3, par)
                            qk_lo(l, t + 1, 1 - par, 0)
                            qk_lo(l, t + 1, 1 - par, 1)
                            normalise_out(g, par)
                            stream_lo(l, t + 3, 1 - par)
                            maxima(l, t + 1, g + 1, 0, 1 - par)
                            out_lo(g)
                            squared_norms(l, t + 2, 0)
                            maxima(l, t + 1, g + 1, 1, 1 - par)
                            squared_norms(l, t + 2, 1)
                            after(dve, "wo_mm", g + 1)
                            dve.tensor_tensor(x[:, t, :], x[:, t, :], ps_misc[:, 0:D], ALU.add).then_inc(s["xa_done"], 1)
                    split_weights(4 * l + 2, F_COLS, 0)
                    hold(dve, s["tick"], (s["shift_in"], 128 * l + 128))
                    chunk_statistics(l, 0, 0, 0)
                    chunk_statistics(l, 0, 1, 0)
                    chunk_normalise(l, 0, 0)
                    split_weights(4 * l + 2, F_COLS, 1)
                    chunk_lo(l, 0, 0)
                    dve.sem_inc(s["tick"], 1)
                    with dve.Fori(0, NCH // 2) as cc:
                        for par in range(2):
                            c = cc * 2 + par
                            ci = l * NCH + c
                            nxt = (c + 1) % NCH
                            hidden_full(ci * HT, 0)
                            after(dve, "ya_done", ci)
                            chunk_statistics(l, c + 1, 0, nxt)
                            hidden_full(ci * HT, 1)
                            hidden_lo(ci * HT, 0)
                            chunk_statistics(l, c + 1, 1, nxt)
                            hidden_full(ci * HT, 2)
                            hidden_lo(ci * HT, 1)
                            chunk_normalise(l, c + 1, nxt)
                            for i in range(3, HT - 1):
                                hidden_full(ci * HT, i)
                                hidden_lo(ci * HT, i - 1)
                            hidden_lo(ci * HT, HT - 2)
                            hidden_full(ci * HT, HT - 1)
                            hidden_lo(ci * HT, HT - 1)
                            chunk_lo(l, c + 1, 1 - par)
                            after(dve, "y_mm", HT * (ci + 1))
                            after(dve, "b2_done", ci + 1)
                            for i in range(2):
                                step = dve.tensor_tensor(x[:, ds(c * CT + 2 * i, 2), :], x[:, ds(c * CT + 2 * i, 2), :],
                                                         bank[6 + i][:].rearrange("p (t d) -> p t d", d=D), ALU.add)
                            step.then_inc(s["ya_done"], 1)

            @block.tensor
            def _(pe):
                start(pe, PE_SEMS)
                pe.wait_ge(s["zeroed"], B + 4)

                def stream_T(l, t, par):
                    after(pe, "xs_done", nth_staged(l, t) + 1)
                    after(pe, "h_lo", nth_transposed(l, t))
                    for k in range(KT):
                        step = pe.transpose(ps_misc[:, k * P:(k + 1) * P], xs[:, par, k * P:(k + 1) * P], ident[:])
                    step.then_inc(s["xT_mm"], 1)

                def project(l, t, par, i):
                    n = nth_rotated(l, t)
                    if i == 2:
                        after(pe, "ca_in", nth_transposed(l, t) + 1)
                    if i == 0:
                        after(pe, "ra_done", 6 * n - 3)
                    if i == 1:
                        after(pe, "kn_done", n)
                    cols = slice(i * INNER, (i + 1) * INNER)
                    for k in range(KT):
                        step = three_products(pe, ps_qkv[i][:], hT[:, par, 0, k, 0:P], hT[:, par, 1, k, 0:P],
                                              wqkv[0][:, k, cols], wqkv[1][:, k, cols], k == 0, k == KT - 1)
                    step.then_inc(s["qkv_mm"], 1)

                def qk_T(l, t, i):
                    after(pe, "add_done", 2 * nth_rotated(l, t) + i + 1)
                    for j in range(LP):
                        dst = (ps_misc, ps_qkv[2])[i]
                        step = pe.transpose(dst[:, j * P:(j + 1) * P], ra[:, i, j * P:(j + 1) * P], ident[:])
                    step.then_inc(s["qkT_mm"], 1)

                def scores(l, t, j, par):
                    after(pe, "mx_done", 2 * nth_scores(l, t, j))
                    for n, (qx, kx) in enumerate(((0, 0), (0, 1), (1, 0))):
                        for h in range(2):
                            rws = slice(h * DH, (h + 1) * DH)
                            step = pe.matmul(ps_s[h][:, 0:2 * P], qT[rws, par, qx, j, :], kT[rws, kx, j, :], start=(n == 0),
                                             stop=(n == 2), skip_group_check=True)
                    step.then_inc(s["sc_mm"], 1)

                def probs_T(g, j):
                    after(pe, "ex_done", LP * g + j + 1)
                    if j == 2:
                        after(pe, "pt_done", LP * g + j)
                    for slot in range(2):
                        for h in range(2):
                            step = pe.transpose(ps_pt[:, (2 * slot + h) * P:(2 * slot + h + 1) * P],
                                                pr[:, j % 2, h, slot * P:(slot + 1) * P], ident[:])
                    step.then_inc(s["pt_mm"], 1)

                def values(g, j, v_slots):
                    after(pe, "pt_done", LP * g + j + 1)
                    for h in range(2):
                        cols = slice((2 * j + h) * DH, (2 * j + h + 1) * DH)
                        for slot in range(2):
                            step = pe.matmul(ps_pv[:, cols], pT[:, (2 * slot + h) * P:(2 * slot + h + 1) * P], vv[:, v_slots[slot], cols],
                                             start=(j == 0 and h == 0 and slot == 0), stop=(slot == 1), skip_group_check=True)
                    step.then_inc(s["pv_mm"], 1)

                def out_T(g):
                    after(pe, "on_done", g + 1)
                    for j in range(LP):
                        step = pe.transpose(ps_pv[:, j * P:(j + 1) * P], on[:, j * P:(j + 1) * P], ident[:])
                    step.then_inc(s["oT_mm"], 1)

                def project_out(g):
                    after(pe, "o_lo", g + 1)
                    for k in range(LP):
                        step = three_products(pe, ps_misc[:, 0:D], oT[:, 0, k, :], oT[:, 1, k, :], wo[0][:, k, :], wo[1][:, k, :],
                                              k == 0, k == LP - 1)
                    step.then_inc(s["wo_mm"], 1)

                def chunk_T(l, c):
                    n = nth_norm(l, c)
                    after(pe, "xnd", n + 1)
                    after(pe, "f_hi", n)
                    for t in range(CT):
                        for k in range(KT):
                            step = pe.transpose(bank[4 + k][:, t * P:(t + 1) * P], xn[:, t, k * P:(k + 1) * P], ident[:])
                    step.then_inc(s["fT_mm"], 1)

                def hidden(n, i, par):
                    after(pe, "uf_done", n + i - 1)
                    for gate in range(2):
                        cols = slice((gate * HT + i) * P, (gate * HT + i + 1) * P)
                        for k in range(KT):
                            step = three_products(pe, bank[2 * gate + i % 2][:], w1[0][:, k, cols], w1[1][:, k, cols],
                                                  fT_hi[:, par, k, :], fT_lo[:, k, :], k == 0, k == KT - 1)
                        step.then_inc(s["gu_mm"], 1)

                def hidden_out(n, i):
                    after(pe, "u_lo", n + i + 1)
                    for t in range(CT):
                        step = three_products(pe, bank[6 + t // 2][:, (t % 2) * D:(t % 2 + 1) * D],
                                              uT[:, 0, i, t * P:(t + 1) * P], uT[:, 1, i, t * P:(t + 1) * P],
                                              w2[0][:, i, :], w2[1][:, i, :], i == 0 and t % 2 == 0, i == HT - 1)
                    step.then_inc(s["y_mm"], 1)

                with pe.Fori(0, L) as l:
                    after(pe, "ya_done", NCH * l)
                    stream_T(l, 0, 0)
                    after(pe, "w_lo_done", 4 * l + 2)
                    after(pe, "h_lo", nth_transposed(l, 0) + 1)
                    for i in (2, 0, 1):
                        project(l, 0, 0, i)
                    qk_T(l, 0, 0)
                    after(pe, "v_done", nth_projected(l, 0) + 1)
                    qk_T(l, 0, 1)
                    after(pe, "qkT_lo", 2 * nth_rotated(l, 0) + 2)
                    stream_T(l, 1, 1)
                    after(pe, "h_lo", nth_transposed(l, 1) + 1)
                    for i in (2, 0, 1):
                        project(l, 1, 1, i)
                    stream_T(l, 2, 0)
                    scores(l, 0, 0, 0)
                    scores(l, 0, 1, 0)
                    with pe.Fori(0, B) as b, pe.Fori(0, TB // 2) as jj:
                        for par in range(2):
                            t = b * TB + jj * 2 + par
                            g = nth(l, t)
                            this, before = (jj * 2 + par) % V_RING, (jj * 2 + par + V_RING - 1) % V_RING
                            v_slots = (this, before) if par == 0 else (before, this)
                            probs_T(g, 0)
                            scores(l, t, 2, par)
                            project(l, t + 2, par, 2)
                            values(g, 0, v_slots)
                            probs_T(g, 1)
                            project(l, t + 2, par, 0)
                            scores(l, t, 3, par)
                            probs_T(g, 2)
                            values(g, 1, v_slots)
                            after(pe, "xa_done", g)
                            qk_T(l, t + 1, 0)
                            after(pe, "v_done", nth_projected(l, t + 2) + 1)
                            qk_T(l, t + 1, 1)
                            values(g, 2, v_slots)
                            probs_T(g, 3)
                            project(l, t + 2, par, 1)
                            values(g, 3, v_slots)
                            after(pe, "qkT_lo", 2 * nth_rotated(l, t + 1) + 2)
                            stream_T(l, t + 3, 1 - par)
                            scores(l, t + 1, 0, 1 - par)
                            out_T(g)
                            scores(l, t + 1, 1, 1 - par)
                            after(pe, "h_lo", nth_transposed(l, t + 3) + 1)
                            project_out(g)
                    hold(pe, s["tick"], (s["sq_done"], at(2 * (NT + 2) * (l + 1))),
                         (s["nb_done"], at((LP * NT + 2) * (l + 1))), (s["xa_done"], at(NT * (l + 1))))
                    chunk_T(l, 0)
                    hold(pe, s["tick"], (s["w_lo_done"], at(4 * l + 4)))
                    with pe.Fori(0, NCH // 2) as cc:
                        for par in range(2):
                            c = cc * 2 + par
                            ci = l * NCH + c
                            after(pe, "f_lo", nth_norm(l, c) + 1)
                            for i in range(3):
                                hidden(ci * HT, i, par)
                            after(pe, "ya_done", ci)
                            hidden_out(ci * HT, 0)
                            hidden(ci * HT, 3, par)
                            hidden_out(ci * HT, 1)
                            chunk_T(l, c + 1)
                            hidden(ci * HT, 4, par)
                            hidden_out(ci * HT, 2)
                            hidden(ci * HT, 5, par)
                            for i in range(3, HT):
                                hidden_out(ci * HT, i)

def constants():
    k, q = np.arange(P)[:, None], np.arange(P)[None, :]
    return {
        "ident": np.eye(P, dtype=np.float32),
        "ident16": np.eye(P, dtype=np.float16),
        "causal16": np.where(q >= k, 0.0, -60000.0).astype(np.float16),
        "rope": rope_tables(),
        **local_masks(),
    }


def rope_tables():
    half = np.arange(0, DH, 2, dtype=np.float32)
    inv_freq = np.float32(1.0) / np.float32(10000.0) ** (half / np.float32(DH))
    t = np.arange(S, dtype=np.float32)
    freqs = np.concatenate([t[:, None] * inv_freq[None, :]] * 2, axis=-1)
    base = (half + np.float32(0.4 * DH)) / np.float32(1.4 * DH)
    power = (t - np.float32(S // 2)) / np.float32(P // 2)
    scale = base[None, :] ** power[:, None]
    scale = np.concatenate([scale, scale], axis=-1)
    sign = np.where(np.arange(DH) < DH // 2, -1.0, 1.0).astype(np.float32)
    cos, sin = np.cos(freqs), np.sin(freqs) * sign
    tables = np.stack([cos * scale, sin * scale, cos / scale, sin / scale]).astype(np.float32)
    return np.ascontiguousarray(tables.reshape(4, TB, P, DH).transpose(2, 0, 1, 3).reshape(P, -1))


def local_masks():
    q, k = np.arange(P)[:, None], np.arange(P)[None, :]
    own = np.where(k <= q, 0.0, MASKED).astype(np.float32)
    before = np.where(k >= q, 0.0, MASKED).astype(np.float32)
    none = np.full((P, P), MASKED, np.float32)
    mask = np.stack([np.stack([own, before], axis=1), np.stack([before, own], axis=1)], axis=1)
    return {"mask": mask, "prev_mask": np.stack([none] + [before] * (TB // 2 - 1), axis=1)}


def build(nc, io):
    scr = {
        "hT_hi": nc.dram_tensor("hT_hi", [B, P, KT, S], F32, kind="Internal").ap(),
        "hT_lo": nc.dram_tensor("hT_lo", [B, P, KT, S], F32, kind="Internal").ap(),
        "x1": nc.dram_tensor("x1", [B, S, D], F32, kind="Internal").ap(),
    }
    with ExitStack() as ctx:
        a = Allocator(nc, ctx)
        keep = {
            "ident": a.sb("ident", [P, P]),
            "modT": a.sb("modT", [P, 6, B]),
            "modB": a.sb("modB", [P, B, 3 * D]),
        }
        phase_modulation_and_norm1(nc, io, scr, keep)
        phase_attention(nc, io, scr, keep)
        keep["stream"] = a.sb("stream", [P, NT, D])
        phase_layers(nc, io, scr, keep)
        phase_output(nc, io, scr, keep)


def kernel(**inputs):
    import concourse.bacc as _bacc
    from concourse.bass_utils import run_bass_kernel_spmd as _run

    nc = _bacc.Bacc("TRN2", target_bir_lowering=False, num_devices=1)
    arrays = {n.removeprefix("L0_attn_").removeprefix("L0_"): np.ascontiguousarray(v) for n, v in inputs.items()}
    arrays["cT"] = np.ascontiguousarray(arrays.pop("c").T)
    arrays["b_vqk"] = np.stack([arrays.pop(n).reshape(HP, P).T for n in ("bv", "bq", "bk")], axis=1)
    arrays["bo_col"] = np.ascontiguousarray(arrays.pop("bo").reshape(KT, P).T)
    qs, ks = arrays.pop("ffn_q_scale"), arrays.pop("ffn_k_scale")
    arrays["qk_rows"] = np.stack([qs, np.roll(qs, DH // 2, axis=1), ks, np.roll(ks, DH // 2, axis=1)], axis=1)
    arrays["ln_col"] = np.ascontiguousarray(
        np.stack([arrays.pop("ffn_ln_g"), arrays.pop("ffn_ln_b")], axis=1).reshape(L, 2, KT, P).transpose(0, 3, 1, 2))
    w1, w2, b1 = arrays.pop("ffn_w1"), arrays.pop("ffn_w2"), arrays.pop("ffn_b1")
    arrays["w1"] = np.zeros((L, D, 2, HT * P), w1.dtype)
    arrays["w1"][:, :, :, :HID] = w1.reshape(L, D, 2, HID)
    arrays["w2"] = np.zeros((L, HT * P, D), w2.dtype)
    arrays["w2"][:, :HID] = w2
    b1_pad = np.zeros((L, 2, HT * P), b1.dtype)
    b1_pad[:, :, :HID] = b1.reshape(L, 2, HID)
    arrays["b1_col"] = np.ascontiguousarray(b1_pad.reshape(L, 2 * HT, P).transpose(0, 2, 1))
    arrays.update(constants())
    io = {n: nc.dram_tensor("in_" + n, v.shape, mybir.dt.from_np(v.dtype), kind="ExternalInput").ap()
          for n, v in arrays.items()}
    io["out"] = nc.dram_tensor("out", (B, S, D), F32, kind="ExternalOutput").ap()
    build(nc, io)
    r = _run(nc, [{"in_" + n: v for n, v in arrays.items()}], core_ids=[0])
    return r.results[0]["out"]
```
